# Optimizing a Trainium2 kernel written in Bass

```python
import numpy as np
import jax
import jax.numpy as jnp

def _softmax(x, axis=-1):
    return jax.nn.softmax(x, axis=axis)

def _gelu(x):
    return jax.nn.gelu(x, approximate=True)

def _silu(x):
    return jax.nn.silu(x)

def _sigmoid(x):
    return jax.nn.sigmoid(x)

def _layernorm(x, axis=-1, eps=1e-05):
    m = jnp.mean(x, axis=axis, keepdims=True)
    v = jnp.var(x, axis=axis, keepdims=True)
    return (x - m) / jnp.sqrt(v + eps)

def _scatter_add(tgt, idx, src, axis=0):
    return tgt.at[idx].add(src)

def _segment_sum(src, seg, n):
    return jax.ops.segment_sum(src, seg, n)
kernel_name = 'mk_gnn_ffn_d2_gnn_r8_ff85ed'

def setup_inputs(seed: int=0):
    np.random.seed(seed)
    _w = jnp.asarray

    def _rec_inputs():
        import jax
        import jax.numpy as jnp
        _gk = jax.random.key(seed)
        x = -0.0003713 + 1 * jax.random.normal(jax.random.fold_in(_gk, 1), (6250, 256), jnp.float32)
        src = jax.random.randint(jax.random.fold_in(_gk, 2), (100000,), 0, 6250, jnp.int32)
        dst = jax.random.randint(jax.random.fold_in(_gk, 3), (100000,), 0, 6250, jnp.int32)
        _o = jnp.argsort(dst, stable=True)
        src = src[_o]
        dst = dst[_o]
        edge_weight = jax.random.uniform(jax.random.fold_in(_gk, 13), (100000,), jnp.float32, 0.0, 0.03125)
        return (x, src, dst, edge_weight)
    x, src, dst, edge_weight = _rec_inputs()

    def _L0_gnn_setup():
        import jax, jax.numpy as jnp
        import numpy as np
        N = 6250
        E = 200000
        D = 256
        H = 256
        EPS = 1e-05

        def _gnn_layer(x, row, col, W, b, g, beta):
            n = x.shape[0]
            neigh = x[col]
            agg = jax.ops.segment_sum(neigh, row, num_segments=n)
            deg = jax.ops.segment_sum(jnp.ones((row.shape[0],), x.dtype), row, num_segments=n)
            deg = jnp.maximum(deg, 1.0)[:, None]
            h = (x + agg / deg) @ W.T + b
            mu = jnp.mean(h, axis=-1, keepdims=True)
            var = jnp.mean(jnp.square(h - mu), axis=-1, keepdims=True)
            hn = (h - mu) * jax.lax.rsqrt(var + EPS) * g + beta
            return jax.nn.silu(hn)
        key = jax.random.key(seed)
        ks = jax.random.split(key, 12)
        x = jax.random.normal(ks[0], (N, D), dtype=jnp.float32)
        edge_index = jax.random.randint(ks[1], (2, E), 0, N, dtype=jnp.int32)
        s0 = 1.0 / np.sqrt(D)
        s1 = 1.0 / np.sqrt(H)
        W0 = jax.random.uniform(ks[2], (H, D), jnp.float32, -s0, s0)
        b0 = jax.random.uniform(ks[3], (H,), jnp.float32, -s0, s0)
        g0 = jnp.ones((H,), jnp.float32)
        beta0 = jnp.zeros((H,), jnp.float32)
        W1 = jax.random.uniform(ks[4], (H, H), jnp.float32, -s1, s1)
        b1 = jax.random.uniform(ks[5], (H,), jnp.float32, -s1, s1)
        g1 = jnp.ones((H,), jnp.float32)
        beta1 = jnp.zeros((H,), jnp.float32)
        return {'x': x, 'edge_index': edge_index, 'W0': W0, 'b0': b0, 'g0': g0, 'beta0': beta0, 'W1': W1, 'b1': b1, 'g1': g1, 'beta1': beta1}
    _L0_gnn_all = _L0_gnn_setup()
    _L0_gnn_in = {k: v for k, v in _L0_gnn_all.items() if k in ('W0', 'b0', 'g0', 'beta0', 'W1', 'b1', 'g1', 'beta1')}
    del _L0_gnn_all

    def _L0_ffn_setup():
        import jax, jax.numpy as jnp
        import numpy as np
        TOP_K = 2
        LN_EPS = 1e-05
        key = jax.random.key(seed)
        ks = jax.random.split(key, 8)
        B, S, D, E, H = (16, 1024, 256, 8, 1024)
        x = jax.random.normal(ks[0], (B, S, D), dtype=jnp.float32)
        Wr = jax.random.normal(ks[1], (D, E), dtype=jnp.float32) * 0.1
        br = jnp.zeros((E,), dtype=jnp.float32)
        ln_g = jnp.ones((E, D), dtype=jnp.float32)
        ln_b = jnp.zeros((E, D), dtype=jnp.float32)
        W1 = jax.random.normal(ks[2], (E, D, H), dtype=jnp.float32) * (1.0 / np.sqrt(D))
        b1 = jnp.zeros((E, H), dtype=jnp.float32)
        W2 = jax.random.normal(ks[3], (E, H, D), dtype=jnp.float32) * (1.0 / np.sqrt(H))
        b2 = jnp.zeros((E, D), dtype=jnp.float32)
        return {'x': x, 'Wr': Wr, 'br': br, 'ln_g': ln_g, 'ln_b': ln_b, 'W1': W1, 'b1': b1, 'W2': W2, 'b2': b2}
    _L0_ffn_all = _L0_ffn_setup()
    _L0_ffn_in = {k: v for k, v in _L0_ffn_all.items() if k in ('Wr', 'br', 'ln_g', 'ln_b', 'W1', 'b1', 'W2', 'b2')}
    del _L0_ffn_all

    def _L1_gnn_setup():
        import jax, jax.numpy as jnp
        import numpy as np
        N_NODES = 12500
        N_EDGES = 400000
        HIDDEN = 256
        key = jax.random.key(seed)
        ks = jax.random.split(key, 6)
        node_states = jax.random.normal(ks[0], (N_NODES, HIDDEN), dtype=jnp.float32)
        edge_src = jax.random.randint(ks[1], (N_EDGES,), 0, N_NODES, dtype=jnp.int32)
        edge_dst = jax.random.randint(ks[2], (N_EDGES,), 0, N_NODES, dtype=jnp.int32)
        edge_weight = jax.random.uniform(ks[3], (N_EDGES,), dtype=jnp.float32) / 32.0
        scale = 1.0 / np.sqrt(HIDDEN)
        W_self = jax.random.normal(ks[4], (HIDDEN, HIDDEN), dtype=jnp.float32) * scale
        W_msg = jax.random.normal(ks[5], (HIDDEN, HIDDEN), dtype=jnp.float32) * scale
        b_self = jnp.zeros((HIDDEN,), dtype=jnp.float32)
        b_msg = jnp.zeros((HIDDEN,), dtype=jnp.float32)
        ln_gamma = jnp.ones((HIDDEN,), dtype=jnp.float32)
        ln_beta = jnp.zeros((HIDDEN,), dtype=jnp.float32)
        return {'node_states': node_states, 'edge_src': edge_src, 'edge_dst': edge_dst, 'edge_weight': edge_weight, 'W_self': W_self, 'b_self': b_self, 'W_msg': W_msg, 'b_msg': b_msg, 'ln_gamma': ln_gamma, 'ln_beta': ln_beta}
    _L1_gnn_all = _L1_gnn_setup()
    _L1_gnn_in = {k: v for k, v in _L1_gnn_all.items() if k in ('W_self', 'b_self', 'W_msg', 'b_msg', 'ln_gamma', 'ln_beta')}
    del _L1_gnn_all

    def _L1_ffn_setup():
        import jax, jax.numpy as jnp
        import numpy as np
        B, S, D = (8, 512, 256)
        H = 4 * D
        CAPACITY = 0.5
        key = jax.random.key(seed)
        ks = jax.random.split(key, 6)
        x = jax.random.normal(ks[0], (B, S, D), dtype=jnp.float32)
        attention_mask = jnp.zeros((B, 1, 1, S), dtype=jnp.float32)
        wr = jax.random.normal(ks[1], (D, 1), dtype=jnp.float32) * 0.02
        br = jnp.zeros((1,), dtype=jnp.float32)
        w1 = jax.random.normal(ks[2], (D, H), dtype=jnp.float32) * 0.02
        b1 = jnp.zeros((H,), dtype=jnp.float32)
        w2 = jax.random.normal(ks[3], (H, D), dtype=jnp.float32) * 0.02
        b2 = jnp.zeros((D,), dtype=jnp.float32)
        return {'x': x, 'attention_mask': attention_mask, 'wr': wr, 'br': br, 'w1': w1, 'b1': b1, 'w2': w2, 'b2': b2}
    _L1_ffn_all = _L1_ffn_setup()
    _L1_ffn_in = {k: v for k, v in _L1_ffn_all.items() if k in ('attention_mask', 'wr', 'br', 'w1', 'b1', 'w2', 'b2')}
    del _L1_ffn_all
    return {'x': x, 'src': src, 'dst': dst, 'edge_weight': edge_weight, 'L0_gnn_W0': _L0_gnn_in['W0'], 'L0_gnn_b0': _L0_gnn_in['b0'], 'L0_gnn_g0': _L0_gnn_in['g0'], 'L0_gnn_beta0': _L0_gnn_in['beta0'], 'L0_gnn_W1': _L0_gnn_in['W1'], 'L0_gnn_b1': _L0_gnn_in['b1'], 'L0_gnn_g1': _L0_gnn_in['g1'], 'L0_gnn_beta1': _L0_gnn_in['beta1'], 'L0_ffn_Wr': _L0_ffn_in['Wr'], 'L0_ffn_br': _L0_ffn_in['br'], 'L0_ffn_ln_g': _L0_ffn_in['ln_g'], 'L0_ffn_ln_b': _L0_ffn_in['ln_b'], 'L0_ffn_W1': _L0_ffn_in['W1'], 'L0_ffn_b1': _L0_ffn_in['b1'], 'L0_ffn_W2': _L0_ffn_in['W2'], 'L0_ffn_b2': _L0_ffn_in['b2'], 'L1_gnn_W_self': _L1_gnn_in['W_self'], 'L1_gnn_b_self': _L1_gnn_in['b_self'], 'L1_gnn_W_msg': _L1_gnn_in['W_msg'], 'L1_gnn_b_msg': _L1_gnn_in['b_msg'], 'L1_gnn_ln_gamma': _L1_gnn_in['ln_gamma'], 'L1_gnn_ln_beta': _L1_gnn_in['ln_beta'], 'L1_ffn_attention_mask': _L1_ffn_in['attention_mask'], 'L1_ffn_wr': _L1_ffn_in['wr'], 'L1_ffn_br': _L1_ffn_in['br'], 'L1_ffn_w1': _L1_ffn_in['w1'], 'L1_ffn_b1': _L1_ffn_in['b1'], 'L1_ffn_w2': _L1_ffn_in['w2'], 'L1_ffn_b2': _L1_ffn_in['b2']}

def reference(x, src, dst, edge_weight, L0_gnn_W0, L0_gnn_b0, L0_gnn_g0, L0_gnn_beta0, L0_gnn_W1, L0_gnn_b1, L0_gnn_g1, L0_gnn_beta1, L0_ffn_Wr, L0_ffn_br, L0_ffn_ln_g, L0_ffn_ln_b, L0_ffn_W1, L0_ffn_b1, L0_ffn_W2, L0_ffn_b2, L1_gnn_W_self, L1_gnn_b_self, L1_gnn_W_msg, L1_gnn_b_msg, L1_gnn_ln_gamma, L1_gnn_ln_beta, L1_ffn_attention_mask, L1_ffn_wr, L1_ffn_br, L1_ffn_w1, L1_ffn_b1, L1_ffn_w2, L1_ffn_b2):
    import jax
    import jax.numpy as jnp

    def _L0_gnn_ref(x, edge_index, W0, b0, g0, beta0, W1, b1, g1, beta1):
        import jax, jax.numpy as jnp
        import numpy as np
        N = 6250
        E = 200000
        D = 256
        H = 256
        EPS = 1e-05

        def _gnn_layer(x, row, col, W, b, g, beta):
            n = x.shape[0]
            neigh = x[col]
            agg = jax.ops.segment_sum(neigh, row, num_segments=n)
            deg = jax.ops.segment_sum(jnp.ones((row.shape[0],), x.dtype), row, num_segments=n)
            deg = jnp.maximum(deg, 1.0)[:, None]
            h = (x + agg / deg) @ W.T + b
            mu = jnp.mean(h, axis=-1, keepdims=True)
            var = jnp.mean(jnp.square(h - mu), axis=-1, keepdims=True)
            hn = (h - mu) * jax.lax.rsqrt(var + EPS) * g + beta
            return jax.nn.silu(hn)
        row, col = (edge_index[0], edge_index[1])
        x = _gnn_layer(x, row, col, W0, b0, g0, beta0)
        x = _gnn_layer(x, row, col, W1, b1, g1, beta1)
        return x

    def _L0_ffn_ref(x, Wr, br, ln_g, ln_b, W1, b1, W2, b2):
        import jax, jax.numpy as jnp
        import numpy as np
        TOP_K = 2
        LN_EPS = 1e-05
        B, S, D = x.shape
        N = B * S
        xt = x.reshape(N, D)
        logits = xt @ Wr + br
        probs = jax.nn.softmax(logits, axis=-1)
        top_p, top_idx = jax.lax.top_k(probs, TOP_K)
        weights = top_p / top_p.sum(axis=-1, keepdims=True)
        mu = xt.mean(axis=-1, keepdims=True)
        var = ((xt - mu) ** 2).mean(axis=-1, keepdims=True)
        xn = (xt - mu) * jax.lax.rsqrt(var + LN_EPS)
        xe = xn[None, :, :] * ln_g[:, None, :] + ln_b[:, None, :]
        h = jax.nn.gelu(jnp.einsum('end,edh->enh', xe, W1) + b1[:, None, :], approximate=False)
        y = jnp.einsum('enh,ehd->end', h, W2) + b2[:, None, :]
        y_tok = jnp.transpose(y, (1, 0, 2))
        sel = jnp.take_along_axis(y_tok, top_idx[:, :, None], axis=1)
        out = (weights[:, :, None] * sel).sum(axis=1)
        return out.reshape(B, S, D)

    def _L1_gnn_ref(node_states, edge_src, edge_dst, edge_weight, W_self, b_self, W_msg, b_msg, ln_gamma, ln_beta):
        import jax, jax.numpy as jnp
        import numpy as np
        N_NODES = 12500
        N_EDGES = 400000
        HIDDEN = 256
        n = node_states.shape[0]
        gathered = edge_weight[:, None] * node_states[edge_src]
        aggregate = jax.ops.segment_sum(gathered, edge_dst, num_segments=n)
        updated = node_states @ W_self.T + b_self + aggregate @ W_msg.T + b_msg
        mean = jnp.mean(updated, axis=-1, keepdims=True)
        var = jnp.var(updated, axis=-1, keepdims=True)
        normed = (updated - mean) * jax.lax.rsqrt(var + 1e-05) * ln_gamma + ln_beta
        return jax.nn.gelu(normed, approximate=False)

    def _L1_ffn_ref(x, attention_mask, wr, br, w1, b1, w2, b2):
        import jax, jax.numpy as jnp
        import numpy as np
        B, S, D = (8, 512, 256)
        H = 4 * D
        CAPACITY = 0.5
        b, s, d = x.shape
        weights = (jnp.einsum('bsd,do->bso', x, wr) + br)[..., 0]
        k = max(1, int(CAPACITY * s))
        kk = k - 1 if k > 1 else 1
        _, idx = jax.lax.top_k(weights, k)
        sel_idx = idx[:, :kk]
        sel = jnp.take_along_axis(x, sel_idx[:, :, None], axis=1)
        h = jax.nn.gelu(jnp.einsum('bkd,dh->bkh', sel, w1) + b1)
        y = jnp.einsum('bkh,hd->bkd', h, w2) + b2
        w_sel = jnp.take_along_axis(weights, sel_idx, axis=1)
        y = y * w_sel[..., None]
        batch_idx = jnp.arange(b)[:, None]
        processed = jnp.zeros_like(x).at[batch_idx, sel_idx].set(y)
        return processed + x
    edge_index = jnp.stack([src, dst])
    x = x + _L0_gnn_ref(_layernorm(x, axis=-1), edge_index, L0_gnn_W0, L0_gnn_b0, L0_gnn_g0, L0_gnn_beta0, L0_gnn_W1, L0_gnn_b1, L0_gnn_g1, L0_gnn_beta1)
    x = x + _L0_ffn_ref(_layernorm(x, axis=-1)[None], L0_ffn_Wr, L0_ffn_br, L0_ffn_ln_g, L0_ffn_ln_b, L0_ffn_W1, L0_ffn_b1, L0_ffn_W2, L0_ffn_b2)[0]
    x = x + _L1_gnn_ref(_layernorm(x, axis=-1), src, dst, edge_weight, L1_gnn_W_self, L1_gnn_b_self, L1_gnn_W_msg, L1_gnn_b_msg, L1_gnn_ln_gamma, L1_gnn_ln_beta)
    x = x + _L1_ffn_ref(_layernorm(x, axis=-1)[None], L1_ffn_attention_mask, L1_ffn_wr, L1_ffn_br, L1_ffn_w1, L1_ffn_b1, L1_ffn_w2, L1_ffn_b2)[0]
    return x

_drawn_inputs = setup_inputs


def setup_inputs(seed=0):
    import zlib

    import numpy as np

    out = dict(_drawn_inputs(seed))
    spreads = {'L0_gnn_g0': (1.0, 0.2),
     'L0_gnn_beta0': (0.0, 0.1),
     'L0_gnn_g1': (1.0, 0.2),
     'L0_gnn_beta1': (0.0, 0.1),
     'L0_ffn_br': (0.0, 0.1),
     'L0_ffn_ln_g': (1.0, 0.2),
     'L0_ffn_ln_b': (0.0, 0.1),
     'L0_ffn_b1': (0.0, 0.1),
     'L0_ffn_b2': (0.0, 0.1),
     'L1_gnn_b_self': (0.0, 0.1),
     'L1_gnn_b_msg': (0.0, 0.1),
     'L1_gnn_ln_gamma': (1.0, 0.2),
     'L1_gnn_ln_beta': (0.0, 0.1),
     'L1_ffn_b1': (0.0, 0.8),
     'L1_ffn_b2': (0.0, 0.8)}
    factors = {'edge_weight': 3.339, 'L1_ffn_wr': 5.769, 'L1_ffn_w1': 7.031, 'L1_ffn_w2': 6.492}
    for name, (base, spread) in spreads.items():
        noise = np.random.default_rng([zlib.crc32(name.encode()), seed]).standard_normal(out[name].shape)
        drawn = base * np.exp(spread * noise) if base else spread * noise
        out[name] = jnp.asarray(drawn.astype(out[name].dtype))
    for name, factor in factors.items():
        out[name] = (out[name] * factor).astype(out[name].dtype)
    return out
```

```python
from contextlib import ExitStack

import numpy as np
import concourse.bass as bass
from concourse import mybir

ALU = mybir.AluOpType
ACT = mybir.ActivationFunctionType
AX = mybir.AxisListType.X
F32 = mybir.dt.float32
BF16 = mybir.dt.bfloat16
U16 = mybir.dt.uint16
I32 = mybir.dt.int32

P = 128
N = 6250
D = 256
KB = D // P
H = 1024
HB = H // P
NT = -(-N // P)
LAST = N - (NT - 1) * P
E = 100000
EC = 784
EROWS = E // EC
ETAIL = E - EROWS * EC
EU = 8
NCH = -(-((E + NT * (P - 1)) // P) // (2 * EU)) * 2 * EU
QW = NCH + 2 * EU
KEYBITS = 13
NONE = P
EX = 8
TOP = 2
FT = 256
MOE_TILES = (TOP * N + EX * (FT - 1)) // FT
KEEP = N // 2 - 1
MOD_TILES = -(-KEEP // FT)
EPS = 1e-5
U = 7
STEPS = NT // U
assert STEPS * U == NT and EC % (2 * EU) == 0 and MOE_TILES % 2 == 0


class Chain:

    def __init__(self, eng, sem):
        self.eng, self.sem, self.n, self.base = eng, sem, 0, 0

    def done(self, ins):
        ins.then_inc(self.sem, 1)
        self.n += 1

    def settle(self):
        self.eng.wait_ge(self.sem, self.base + self.n)

    def link(self, ins):
        self.done(ins)
        self.settle()

    def enter(self, i, per):
        self.start, self.per, self.base = self.n, per, i * per

    def leave(self, iterations):
        assert self.n - self.start == self.per, (self.n - self.start, self.per)
        self.n, self.base = self.start + iterations * self.per, 0


class PoolWait:

    def __init__(self, p, pool, sem):
        self.p, self.pool, self.sem = p, pool, sem
        p.nc.gpsimd.memset(p.idle[:], 0.0).then_inc(sem, 1)
        pool.wait_ge(sem, 1)

    def __call__(self, sem, value, before):
        self.pool.wait_ge(self.sem, before + 1)
        self.pool.wait_ge(sem, value)
        self.p.nc.gpsimd.tensor_tensor(self.p.idle[:, 0:1], self.p.idle[:, 1:2], self.p.idle[:, 1:2],
                                       ALU.add).then_inc(self.sem, 1)


def rows(dram, t, n=P):
    return dram[t * P:t * P + n, :]


def tiles(dram, a, b):
    return dram[a * P:b * P, :].rearrange("(t p) d -> p t d", p=P)


class Program:
    def __init__(self, nc, ctx):
        self.nc, self.ctx, self.names, self.stage = nc, ctx, 0, ""

    def sb(self, name, shape, dt=F32, ctx=None):
        return (ctx or self.ctx).enter_context(self.nc.sbuf_tensor(self.stage + name, shape, dt))

    def ps(self, name, shape, ctx):
        return ctx.enter_context(self.nc.psum_tensor(self.stage + name, shape, F32))

    def sem(self, name, ctx):
        return self.nc.alloc_semaphore(self.stage + name)



def sort_edges_and_normalize(p, io, dram):
    nc = p.nc
    with ExitStack() as ctx:
        key = [p.sb(f"key{k}", [P, EC], I32, ctx) for k in range(2)]
        weight = p.weight1
        win_i = p.sb("win_i", [P, EC], I32, ctx)
        win = p.sb("win", [P, EC], BF16, ctx)
        mask = p.sb("mask", [P, EC], BF16, ctx)
        ones_row = p.sb("ones_row", [P, EC], BF16, ctx)
        rank = p.sb("rank", [P, EC], F32, ctx)
        pos = p.sb("pos", [P, EC], F32, ctx)
        pos_i = p.sb("pos_i", [P, EC], I32, ctx)
        lane = p.sb("lane", [P, EC], I32, ctx)
        local = p.sb("local_sh", [P, EC], I32, ctx)
        addr = [p.sb("addr0", [P, EC], I32, ctx), p.addr1]
        rec = [p.sb("rec0", [P, EC], I32, ctx), p.rec1]
        count = p.sb("count", [P, NT], F32, ctx)
        room = p.acc[:].rearrange("p t d -> p (t d)")
        fill = room[:, 0:2 * QW].bitcast(I32)
        zero = room[:, 2 * QW:2 * QW + 4 * D]
        wload = room[:, 2 * QW + 4 * D:2 * QW + 4 * D + 4 * KB * D].rearrange("p (k b d) -> p k b d", k=4, b=KB)
        slot_addr = p.sb("slot_addr", [P, 2 * EU], I32, ctx)
        slot_rec = p.sb("slot_rec", [P, 2 * EU], I32, ctx)
        xb = p.xb
        norm = RowNorm(p, ctx)
        spent = p.sb("spent", [P, 1], F32, ctx)
        b = Binning(p, ctx, NT, NCH)
        psw = [p.ps(f"psw{i}", [P, 512], ctx) for i in range(2)]

        s = lambda name: p.sem(name, ctx)
        s_const, s_keys0, s_keys1, s_keyfill = s("s_const"), s("s_keys0"), s("s_keys1"), s("s_keyfill")
        s_dve, s_pe, s_addr, s_fill, s_prefill = s("s_dve"), s("s_pe"), s("s_addr"), s("s_fill"), s("s_prefill")
        s_zero, s_xpad, s_x, s_xn, s_xnout = (
            s("s_zero"), s("s_xpad"), s("s_x"), s("s_xn"), s("s_xnout"))
        s_slot = [s(f"s_slot{h}") for h in range(2)]
        s_scat = [s(f"s_scat{h}") for h in range(2)]
        s_wload, s_wT, s_wcopied = s("s_wload"), s("s_wT"), s("s_wcopied")
        s_pool, s_idle, s_small = s("s_pool"), s("s_idle"), s("s_small")
        block = ctx.enter_context(nc.Block())
        weights = [io["L0_gnn_W0"], io["L0_gnn_W1"], io["L1_gnn_W_self"], io["L1_gnn_W_msg"]]

        @block.gpsimd
        def _(pool):
            c = Chain(pool, s_pool)
            c.done(nc.gpsimd.memset(p.ident[:], 0.0))
            c.done(nc.gpsimd.memset(p.before[:], 1.0))
            c.done(nc.gpsimd.memset(p.upto[:], 1.0))
            c.done(nc.gpsimd.iota(p.iota[:], [[1, P]], base=0, channel_multiplier=0,
                                  allow_small_or_imprecise_dtypes=True))
            c.done(nc.gpsimd.iota(p.chunk_no[:], [[1, NCH]], base=0, channel_multiplier=0,
                                  allow_small_or_imprecise_dtypes=True))
            c.done(nc.gpsimd.iota(p.part_no[:], [[0, 1]], base=0, channel_multiplier=1,
                                  allow_small_or_imprecise_dtypes=True))
            c.done(nc.gpsimd.iota(p.node_no[:], [[P, NT]], base=0, channel_multiplier=1,
                                  allow_small_or_imprecise_dtypes=True))
            c.settle()
            nc.gpsimd.affine_select(out=p.ident[:], in_=p.ident[:], compare_op=ALU.not_equal, fill=1.0, base=0,
                                    pattern=[[-1, P]], channel_multiplier=1).then_inc(s_const, 1)
            nc.gpsimd.affine_select(out=p.before[:], in_=p.before[:], compare_op=ALU.is_gt, fill=0.0, base=0,
                                    pattern=[[1, P]], channel_multiplier=-1).then_inc(s_const, 1)
            nc.gpsimd.affine_select(out=p.upto[:], in_=p.upto[:], compare_op=ALU.is_ge, fill=0.0, base=0,
                                    pattern=[[1, P]], channel_multiplier=-1).then_inc(s_const, 1)
            pool.wait_ge(s_prefill, 32)
            ready = PoolWait(p, pool, s_idle)
            with pool.Fori(0, EC // (2 * EU)) as i:
                for h in range(2):
                    ready(s_slot[h], 2 * i + 2, 2 * i + h)
                    for u in range(h * EU, (h + 1) * EU):
                        pool.indirect_dma_start(
                            dram["table0"], bass.IndirectOffsetOnAxis(ap=slot_addr[:, u:u + 1], axis=0),
                            slot_rec[:, u:u + 1], None, bounds_check=P * QW - 1,
                            oob_is_err=False).then_inc(s_scat[h], 16)
            for h in range(2):
                pool.wait_ge(s_scat[h], 16 * EU * (EC // (2 * EU)))

        @block.scalar
        def _(act):
            for k in range(4):
                act.dma_start(wload[:, k, :, :], weights[k].rearrange("(b p) d -> p b d", p=P)).then_inc(s_wload, 16)
            for k in range(4):
                for kb in range(KB):
                    n = k * KB + kb
                    act.wait_ge(s_wT, n + 1)
                    nc.scalar.activation(p.wT[:, k, kb, :], psw[n % 2][:, 0:D], ACT.Copy).then_inc(s_wcopied, 1)

            def fill_slots(h, c0):
                nc.scalar.activation(slot_addr[:, h * EU:(h + 1) * EU], addr[0][:, bass.ds(c0, EU)],
                                     ACT.Copy).then_inc(s_slot[h], 1)
                nc.scalar.activation(slot_rec[:, h * EU:(h + 1) * EU], rec[0][:, bass.ds(c0, EU)],
                                     ACT.Copy).then_inc(s_slot[h], 1)

            act.wait_ge(s_addr, 1)
            for h in range(2):
                fill_slots(h, h * EU)
            with act.Fori(0, EC // (2 * EU) - 1) as i:
                for h in range(2):
                    act.wait_ge(s_scat[h], 16 * EU * i + 16 * EU)
                    fill_slots(h, 2 * EU * i + 2 * EU + h * EU)
            norm.root(act)

        @block.sync
        def _(sp):
            sp.wait_ge(s_keyfill, 2)
            for k, (name, sem) in enumerate((("src", s_keys0), ("dst", s_keys1))):
                sp.dma_start(key[k][0:EROWS, :], io[name][0:EROWS * EC].rearrange("(p c) -> p c", c=EC)).then_inc(sem, 16)
                sp.dma_start(key[k][EROWS:EROWS + 1, 0:ETAIL],
                             io[name][EROWS * EC:E].rearrange("(a c) -> a c", a=1)).then_inc(sem, 16)
            sp.wait_ge(s_keyfill, 3)
            sp.dma_start(weight[0:EROWS, :], io["edge_weight"][0:EROWS * EC].rearrange("(p c) -> p c", c=EC)).then_inc(s_keys1, 16)
            sp.dma_start(weight[EROWS:EROWS + 1, 0:ETAIL],
                         io["edge_weight"][EROWS * EC:E].rearrange("(a c) -> a c", a=1)).then_inc(s_keys1, 16)
            sp.wait_ge(s_fill, 1)
            sp.dma_start(dram["table0"].rearrange("(p q) a -> p (q a)", p=P), fill[:, 0:QW]).then_inc(s_prefill, 16)
            sp.dma_start(dram["table1"].rearrange("(p q) a -> p (q a)", p=P), fill[:, :]).then_inc(s_prefill, 16)
            sp.wait_ge(s_xpad, 1)
            sp.dma_start(xb[:, 0:NT - 1, :], tiles(io["x"], 0, NT - 1)).then_inc(s_x, 16)
            sp.dma_start(xb[0:LAST, NT - 1, :], rows(io["x"], NT - 1, LAST)).then_inc(s_x, 16)
            sp.wait_ge(s_zero, 1)
            zeros = 0
            for name in ("moe_in", "moe_out", "mod_in", "mod_out"):
                flat = dram[name].rearrange("(g r) d -> g (r d)", r=4)
                total = flat.shape[0]
                first = 0 if name.endswith("in") else total - P // 4
                for g in range(first, total, P):
                    n = min(P, total - g)
                    sp.dma_start(flat[g:g + n, :], zero[0:n, :]).then_inc(s_zero, 16)
                    zeros += 1
            sp.wait_ge(s_xn, 1)
            sp.dma_start(tiles(dram["xn"], 0, NT), xb[:, :, :]).then_inc(s_xnout, 16)
            sp.wait_ge(s_xnout, 16)
            small = 0
            with nc.allow_non_contiguous_dma("small parameters"):
                for dst, source in p.small:
                    sp.dma_start(dst, source).then_inc(s_small, 16)
                    small += 1
            sp.wait_ge(s_small, 16 * small)
            sp.wait_ge(s_zero, 1 + 16 * zeros)

        @block.tensor
        def _(pe):
            pe.wait_ge(s_const, 3)
            pe.wait_ge(s_wload, 64)
            for k in range(4):
                for kb in range(KB):
                    n = k * KB + kb
                    if n >= 2:
                        pe.wait_ge(s_wcopied, n - 1)
                    for jb in range(KB):
                        last = nc.tensor.transpose(psw[n % 2][:, jb * P:(jb + 1) * P],
                                                   wload[:, k, jb, kb * P:(kb + 1) * P], p.ident[:])
                    last.then_inc(s_wT, 1)
            for k in range(2):
                b.products(pe, k, count, b.s_count)

        @block.vector
        def _(dve):
            c = Chain(dve, s_dve)
            for k in range(2):
                nc.vector.memset(key[k][:], (NT + 14) * P).then_inc(s_keyfill, 1)
            nc.vector.memset(weight[:], 0.0).then_inc(s_keyfill, 1)
            nc.vector.memset(fill, NONE << KEYBITS).then_inc(s_fill, 1)
            nc.vector.memset(xb[:, NT - 1, :], 0.0).then_inc(s_xpad, 1)
            nc.vector.memset(zero, 0.0).then_inc(s_zero, 1)
            c.done(nc.vector.memset(p.ones[:], 1.0))
            c.done(nc.vector.memset(p.eps[:], EPS))
            c.done(nc.vector.memset(ones_row[:], 1.0))
            dve.wait_ge(s_keys0, 32)
            dve.wait_ge(s_keys1, 64)
            dve.wait_ge(s_const, 3)
            for k in range(2):
                mine, other = key[k], key[1 - k]
                c.done(nc.vector.tensor_single_scalar(win_i[:], mine[:], 7, ALU.arith_shift_right))
                c.done(nc.vector.tensor_scalar(local[:], mine[:], P - 1, KEYBITS, ALU.bitwise_and,
                                               ALU.logical_shift_left))
                c.done(nc.vector.memset(pos[:], 0.0))
                c.settle()
                c.done(nc.vector.tensor_copy(win[:], win_i[:]))
                c.link(nc.vector.tensor_tensor(rec[k][:], local[:], other[:], ALU.bitwise_or))
                with dve.Fori(0, NT) as w:
                    c.enter(w, 1)
                    c.link(nc.vector.tensor_scalar(mask[:], win[:], p.iota[:, bass.ds(w, 1)], None, ALU.is_equal,
                                                   ALU.add, accum_out=count[:, bass.ds(w, 1)]))
                c.leave(NT)
                nc.vector.tensor_copy(b.count[:], count[:]).then_inc(b.s_count, 1)
                b.starts(dve, c, k, 7, P)
                with dve.Fori(0, NT) as w:
                    c.enter(w, 4)
                    tile = p.iota[:, bass.ds(w, 1)]
                    c.link(nc.vector.tensor_scalar(mask[:], win[:], tile, None, ALU.is_equal))
                    c.link(nc.vector.tensor_tensor_scan(rank[:], ones_row[:], mask[:], b.start[:, bass.ds(w, 1)],
                                                        ALU.mult, ALU.add))
                    c.link(nc.vector.tensor_tensor(rank[:], rank[:], mask[:], ALU.mult))
                    c.link(nc.vector.tensor_tensor(pos[:], pos[:], rank[:], ALU.add))
                c.leave(NT)
                c.link(nc.vector.tensor_scalar(rank[:], win[:], float(NT), float(1 << 24), ALU.is_ge, ALU.mult))
                c.link(nc.vector.tensor_tensor(pos[:], pos[:], rank[:], ALU.add))
                c.link(nc.vector.tensor_copy(pos_i[:], pos[:]))
                c.done(nc.vector.tensor_single_scalar(lane[:], pos_i[:], P - 1, ALU.bitwise_and))
                c.link(nc.vector.tensor_single_scalar(win_i[:], pos_i[:], 7, ALU.arith_shift_right))
                c.done(nc.vector.scalar_tensor_tensor(out=addr[k][:], in0=lane[:], scalar=float(QW), in1=win_i[:],
                                                      op0=ALU.mult, op1=ALU.add))
                c.settle()
                b.table(dve, c, k, p.tile_of[k])
                nc.vector.memset(spent[:], 0.0).then_inc(s_addr, 1)
            dve.wait_ge(s_addr, 2)
            dve.wait_ge(s_x, 32)
            with dve.Fori(0, NT) as t:
                norm.take(flat(xb[:, bass.ds(t, 1), :]), t).then_inc(s_dve, 1)
            c.n += NT
            c.settle()
            norm.finish(dve, c)
            with dve.Fori(0, NT) as t:
                x_t = flat(xb[:, bass.ds(t, 1), :])
                nc.vector.tensor_scalar(x_t, x_t, norm.mean[:, bass.ds(t, 1)], norm.rstd[:, bass.ds(t, 1)],
                                        ALU.subtract, ALU.mult).then_inc(s_dve, 1)
            c.n += NT
            c.settle()
            nc.vector.memset(spent[:], 0.0).then_inc(s_xn, 1)


class RowNorm:

    def __init__(self, p, ctx):
        self.p = p
        tag = f"n{p.names}"
        p.names += 1
        self.stats = p.sb(tag + "stats", [P, NT, 6], F32, ctx)
        self.mean = p.sb(tag + "mean", [P, NT], F32, ctx)
        self.half = p.sb(tag + "half", [P, NT], F32, ctx)
        self.var = p.sb(tag + "var", [P, NT], F32, ctx)
        self.rstd = p.sb(tag + "rstd", [P, NT], F32, ctx)
        self.s_var = p.sem(tag + "s_var", ctx)
        self.s_std = p.sem(tag + "s_std", ctx)

    def take(self, row, t):
        return self.p.nc.vector.bn_stats(self.stats[:, bass.ds(t, 1), :].rearrange("p a s -> p (a s)"), row)

    def finish(self, dve, c):
        v, st = self.p.nc.vector, self.stats
        c.done(v.tensor_tensor(self.mean[:], st[:, :, 1], st[:, :, 4], ALU.add))
        c.done(v.tensor_tensor(self.half[:], st[:, :, 1], st[:, :, 4], ALU.subtract))
        c.done(v.tensor_tensor(self.var[:], st[:, :, 2], st[:, :, 5], ALU.add))
        c.settle()
        c.done(v.tensor_scalar(self.mean[:], self.mean[:], 0.5, None, ALU.mult))
        c.done(v.tensor_tensor(self.half[:], self.half[:], self.half[:], ALU.mult))
        c.done(v.tensor_scalar(self.var[:], self.var[:], 4.0 / D, None, ALU.mult))
        c.settle()
        c.link(v.tensor_tensor(self.var[:], self.var[:], self.half[:], ALU.add))
        v.tensor_scalar(self.var[:], self.var[:], 0.25, None, ALU.mult).then_inc(self.s_var, 1)
        dve.wait_ge(self.s_std, 1)
        c.link(v.reciprocal(self.rstd[:], self.rstd[:]))

    def root(self, act):
        act.wait_ge(self.s_var, 1)
        self.p.nc.scalar.activation(self.rstd[:], self.var[:], ACT.Sqrt, bias=self.p.eps[:, 0:1]).then_inc(self.s_std, 1)


def flat(ap):
    return ap.rearrange("p a d -> p (a d)")


class Binning:

    def __init__(self, p, ctx, bins, chunks):
        self.p, self.bins, self.chunks = p, bins, chunks
        tag = f"b{p.names}"
        p.names += 1
        self.count = p.sb(tag + "count", [P, bins], F32, ctx)
        self.start = p.sb(tag + "start", [P, bins], F32, ctx)
        self.total = p.sb(tag + "total", [P, 2 * bins + 2], F32, ctx)
        self.total_i = p.sb(tag + "total_i", [P, bins + 1], I32, ctx)
        self.full = p.sb(tag + "full", [P, bins + 1], F32, ctx)
        self.cum = p.sb(tag + "cum", [P, bins], F32, ctx)
        self.onesb = p.sb(tag + "onesb", [P, bins], F32, ctx)
        self.ended = p.sb(tag + "ended", [P, chunks], F32, ctx)
        self.ps = p.ps(tag + "ps", [P, 512], ctx)
        self.psrow = p.ps(tag + "psrow", [P, 1024], ctx)
        self.s_count = p.sem(tag + "s_count", ctx)
        self.s_sums = p.sem(tag + "s_sums", ctx)
        self.s_whole = p.sem(tag + "s_whole", ctx)
        self.s_cum = p.sem(tag + "s_cum", ctx)
        self.s_ended = p.sem(tag + "s_ended", ctx)
        self.s_row = p.sem(tag + "s_row", ctx)

    def products(self, pe, k, count, s_count):
        p, nc, B = self.p, self.p.nc, self.bins
        pe.wait_ge(s_count, k + 1)
        nc.tensor.matmul(self.ps[:, 0:B], p.before[:], self.count[:], start=True, stop=True)
        nc.tensor.matmul(self.ps[:, 64:64 + B], p.ones[:], self.count[:], start=True, stop=True)
        nc.tensor.matmul(self.ps[0:B, 128:129], self.count[:], p.ones[:, 0:1], start=True, stop=True).then_inc(self.s_sums, 1)
        pe.wait_ge(self.s_whole, k + 1)
        nc.tensor.matmul(self.ps[0:B, 192:193], p.upto[0:B, 0:B], self.full[0:B, B:B + 1],
                         start=True, stop=True).then_inc(self.s_cum, 1)
        pe.wait_ge(self.s_ended, k + 1)
        for a in range(0, self.chunks, 512):
            n = min(512, self.chunks - a)
            last = nc.tensor.matmul(self.psrow[0:1, a:a + n], p.ones[0:B, 0:1], self.ended[0:B, a:a + n],
                                    start=True, stop=True)
        last.then_inc(self.s_row, 1)

    def starts(self, dve, c, k, shift, chunk):
        p, nc, B = self.p, self.p.nc, self.bins
        c.done(nc.vector.memset(self.onesb[:], 1.0))
        c.done(nc.vector.memset(self.total[:], 0.0))
        c.settle()
        dve.wait_ge(self.s_sums, k + 1)
        c.done(nc.vector.tensor_copy(self.start[:], self.ps[:, 0:B]))
        c.done(nc.vector.tensor_scalar(self.total[:, 0:B], self.ps[:, 64:64 + B], float(chunk - 1), None, ALU.add))
        c.done(nc.vector.tensor_scalar(self.total[0:B, B:B + 1], self.ps[0:B, 128:129], float(chunk - 1), None, ALU.add))
        c.settle()
        c.link(nc.vector.tensor_copy(self.total_i[:], self.total[:, 0:B + 1]))
        c.link(nc.vector.tensor_single_scalar(self.total_i[:], self.total_i[:], shift, ALU.arith_shift_right))
        c.link(nc.vector.tensor_copy(self.full[:], self.total_i[:]))
        nc.vector.tensor_tensor_scan(self.cum[:], self.onesb[:], self.full[:, 0:B], 0.0,
                                     ALU.mult, ALU.add).then_inc(self.s_whole, 1)
        dve.wait_ge(self.s_whole, k + 1)
        c.link(nc.vector.tensor_tensor(self.cum[:], self.cum[:], self.full[:, 0:B], ALU.subtract))
        c.link(nc.vector.tensor_scalar(self.cum[:], self.cum[:], float(chunk), -1.0, ALU.mult, ALU.add))
        c.link(nc.vector.tensor_tensor(self.start[:], self.start[:], self.cum[:], ALU.add))

    def table(self, dve, c, k, row):
        p, nc, B, M = self.p, self.p.nc, self.bins, self.chunks
        dve.wait_ge(self.s_cum, k + 1)
        c.link(nc.vector.tensor_copy(self.total[0:B, B + 1:B + 2], self.ps[0:B, 192:193]))
        nc.vector.tensor_scalar(self.ended[0:B, :], p.chunk_no[0:B, 0:M], self.total[0:B, B + 1:B + 2], None,
                                ALU.is_ge).then_inc(self.s_ended, 1)
        dve.wait_ge(self.s_row, k + 1)
        c.link(nc.vector.tensor_scalar(row[0:1, 0:M], self.psrow[0:1, 0:M], float(B - 1), None, ALU.min))



def unpack_table(p, table, fields):
    nc = p.nc
    with ExitStack() as ctx:
        raw = p.sb(f"raw{fields}", [P, QW, fields], I32, ctx)
        loc_i = p.sb(f"loc_i{fields}", [P, QW], I32, ctx)
        s_raw, s_dve = p.sem("s_raw", ctx), p.sem("s_dve", ctx)
        block = ctx.enter_context(nc.Block())

        @block.sync
        def _(sp):
            sp.dma_start(raw[:], table.rearrange("(p q) a -> p q a", p=P)).then_inc(s_raw, 16)

        @block.vector
        def _(dve):
            c = Chain(dve, s_dve)
            dve.wait_ge(s_raw, 16)
            c.done(nc.vector.tensor_single_scalar(p.edge_row[:], raw[:, :, 0], (1 << KEYBITS) - 1, ALU.bitwise_and))
            c.done(nc.vector.tensor_single_scalar(loc_i[:], raw[:, :, 0], KEYBITS, ALU.arith_shift_right))
            if fields == 2:
                c.done(nc.vector.tensor_copy(p.edge_weight[:], raw[:, :, 1].bitcast(F32)))
            c.settle()
            c.link(nc.vector.tensor_copy(p.edge_local[:], loc_i[:]))


def sum_over_edges(p, source, order, weighted):
    nc = p.nc
    with ExitStack() as ctx:
        row_slot = p.sb("row_slot", [P, 2 * EU], I32, ctx)
        got = p.sb("got", [P, 2 * EU, D + 1], F32, ctx)
        onehot = p.sb("onehot", [P, 4, P], F32, ctx)
        sums = [p.ps(f"sums{i}", [P, 512], ctx) for i in range(4)]
        s = lambda name: p.sem(name, ctx)
        s_rows = [s(f"s_rows{h}") for h in range(2)]
        s_got = [s(f"s_got{h}") for h in range(2)]
        s_idle, s_ready, s_onehot, s_sum, s_added = s("s_idle"), s("s_ready"), s("s_onehot"), s("s_sum"), s("s_added")
        block = ctx.enter_context(nc.Block())
        STEPE = NCH // (2 * EU)

        @block.scalar
        def _(act):
            def fill(h, c0):
                nc.scalar.activation(row_slot[:, h * EU:(h + 1) * EU], p.edge_row[:, bass.ds(c0, EU)],
                                     ACT.Copy).then_inc(s_rows[h], 1)
            for h in range(2):
                fill(h, h * EU)
            with act.Fori(0, STEPE) as i:
                for h in range(2):
                    act.wait_ge(s_sum, 2 * EU * i + (h + 1) * EU)
                    fill(h, 2 * EU * i + 2 * EU + h * EU)

        @block.gpsimd
        def _(pool):
            pool.wait_ge(s_ready, 2)
            ready = PoolWait(p, pool, s_idle)
            with pool.Fori(0, STEPE) as i:
                for h in range(2):
                    ready(s_rows[h], i + 1, 2 * i + h)
                    for u in range(h * EU, (h + 1) * EU):
                        pool.indirect_dma_start(
                            got[:, u, 0:D], None, source,
                            bass.IndirectOffsetOnAxis(ap=row_slot[:, u:u + 1], axis=0)).then_inc(s_got[h], 16)

        @block.tensor
        def _(pe):
            pe.wait_ge(s_ready, 2)
            with pe.Fori(0, STEPE) as i:
                for h in range(2):
                    pe.wait_ge(s_got[h], 16 * EU * i + 16 * EU)
                    for u in range(EU):
                        n = h * EU + u
                        pe.wait_ge(s_onehot, 2 * EU * i + n + 1)
                        pe.wait_ge(s_added, 2 * EU * i + n + 1)
                        nc.tensor.matmul(sums[n % 4][:, 0:D + 1], onehot[:, n % 4, :], got[:, n, :],
                                         start=True, stop=True).then_inc(s_sum, 1)

        @block.vector
        def _(dve):
            nc.vector.memset(got[:], 1.0).then_inc(s_ready, 1)
            nc.vector.memset(p.acc[:], 0.0).then_inc(s_ready, 1)
            dve.wait_ge(s_ready, 2)
            for _i in range(4):
                nc.vector.memset(onehot[:, _i, 0:1], 0.0).then_inc(s_added, 1)
            dve.wait_ge(s_added, 4)

            def build(n, c):
                if weighted:
                    ins = nc.vector.tensor_scalar(onehot[:, n % 4, :], p.iota[:], p.edge_local[:, bass.ds(c, 1)],
                                                  p.edge_weight[:, bass.ds(c, 1)], ALU.is_equal, ALU.mult)
                else:
                    ins = nc.vector.tensor_scalar(onehot[:, n % 4, :], p.iota[:], p.edge_local[:, bass.ds(c, 1)],
                                                  None, ALU.is_equal)
                ins.then_inc(s_onehot, 1)

            build(0, 0)
            build(1, 1)
            with dve.Fori(0, STEPE) as i:
                tile_regs = [dve.value_load(p.tile_of[order][0:1, bass.ds(2 * EU * i + n, 1)], min_val=0,
                                            max_val=NT - 1) for n in range(2 * EU)]
                for n in range(2 * EU):
                    build(n + 2, 2 * EU * i + n + 2)
                    dve.wait_ge(s_sum, 2 * EU * i + n + 1)
                    dve.wait_ge(s_added, 2 * EU * i + n + 4)
                    a = p.acc[:, bass.ds(tile_regs[n], 1), :].rearrange("p a d -> p (a d)")
                    nc.vector.tensor_tensor(a, a, sums[n % 4][:, 0:D + 1], ALU.add).then_inc(s_added, 1)



BANK = [0, 1, 2, 0, 1, 2, 3]


class Project:

    def __init__(self, p, ctx, rhs, cols, put, take):
        self.p, self.rhs, self.cols, self.put, self.take = p, rhs, cols, put, take
        n = len(rhs)
        self.slots = p.sb("pr_rows", [P, U, n, D], F32, ctx)
        self.flip = p.sb("pr_flip", [P, U, n * D], F32, ctx)
        self.spare = p.sb("pr_spare", [P, 6], F32, ctx)
        self.ps_flip = [p.ps(f"pr_psflip{i}", [P, 512], ctx) for i in range(4)]
        self.ps_out = [p.ps(f"pr_psout{i}", [P, 512], ctx) for i in range(4)]
        self.s_put, self.s_flip, self.s_copied, self.s_out, self.s_taken = (
            p.sem(f"pr_{x}", ctx) for x in ("s_put", "s_flip", "s_copied", "s_out", "s_taken"))

    def steps(self, eng, tile):
        with eng.Fori(0, STEPS - 1) as i:
            self.i = i
            for u in range(U):
                tile(U * i + u, u, True)
        self.i = STEPS - 1
        for u in range(U):
            tile(U * (STEPS - 1) + u, u, u < U - 1)

    def dve(self, dve, c, per_take):
        p, n = self.p, len(self.rhs)

        def put(t, u):
            for ins in self.put(t, [self.slots[:, u, k, :] for k in range(n)]):
                ins.then_inc(self.s_put, 1)

        for k in range(3):
            p.nc.vector.memset(self.spare[:, k:k + 1], 0.0).then_inc(self.s_taken, 1)
        put(0, 0)

        def tile(t, u, more):
            if u == 0:
                if isinstance(self.i, int):
                    c.leave(STEPS - 1)
                else:
                    c.enter(self.i, U * per_take)
            if more:
                put(t + 1, (u + 1) % U)
            dve.wait_ge(self.s_out, t + 1)
            self.take(t, self.ps_out[BANK[u]], c).then_inc(self.s_taken, 1)

        self.steps(dve, tile)

    def pe(self, pe):
        nc, n = self.p.nc, len(self.rhs)

        def flip(t, u):
            pe.wait_ge(self.s_put, n * t + n)
            pe.wait_ge(self.s_copied, t + 1)
            for k in range(n):
                for kb in range(KB):
                    last = nc.tensor.transpose(self.ps_flip[BANK[u]][:, (k * KB + kb) * P:(k * KB + kb + 1) * P],
                                               self.slots[:, u, k, kb * P:(kb + 1) * P], self.p.ident[:])
            last.then_inc(self.s_flip, 1)

        flip(0, 0)

        def tile(t, u, more):
            if more:
                flip(t + 1, (u + 1) % U)
            pe.wait_ge(self.s_copied, t + 4)
            pe.wait_ge(self.s_taken, t + 1)
            for k in range(n):
                for kb in range(KB):
                    last = nc.tensor.matmul(self.ps_out[BANK[u]][:, 0:self.cols],
                                            self.flip[:, u, (k * KB + kb) * P:(k * KB + kb + 1) * P],
                                            self.rhs[k][kb], start=(k + kb == 0), stop=(k == n - 1 and kb == KB - 1))
            last.then_inc(self.s_out, 1)

        self.steps(pe, tile)

    def act(self, act):
        nc, n = self.p.nc, len(self.rhs)
        for k in range(3):
            nc.scalar.activation(self.spare[:, 3 + k:4 + k], self.p.eps[:], ACT.Copy).then_inc(self.s_copied, 1)

        def tile(t, u, more):
            act.wait_ge(self.s_flip, t + 1)
            nc.scalar.activation(self.flip[:, u, :], self.ps_flip[BANK[u]][:, 0:n * D], ACT.Copy).then_inc(self.s_copied, 1)

        self.steps(act, tile)


def gnn_dense(p, wk, biases, gamma, beta, func, residual):
    nc, v = p.nc, p.nc.vector
    mean_of_edges = len(wk) == 1
    with ExitStack() as ctx:
        bias = p.sb("g_bias", [P, D], F32, ctx)
        deg = p.sb("g_deg", [P, NT], F32, ctx)
        centered = p.sb("g_centered", [P, D], F32, ctx)
        active = p.sb("g_active", [P, U, D], F32, ctx)
        norm, norm2 = RowNorm(p, ctx), RowNorm(p, ctx)

        def put(t, slots):
            a, x = flat(p.acc[:, bass.ds(t, 1), 0:D]), flat(p.xb[:, bass.ds(t, 1), :])
            if mean_of_edges:
                return [v.scalar_tensor_tensor(out=slots[0], in0=a, scalar=deg[:, bass.ds(t, 1)], in1=x,
                                               op0=ALU.mult, op1=ALU.add)]
            return [v.tensor_copy(slots[0], x), v.tensor_copy(slots[1], a)]

        def take(t, psum, c):
            h = flat(p.acc[:, bass.ds(t, 1), 0:D])
            c.link(v.tensor_tensor(h, psum[:, 0:D], bias[:], ALU.add))
            return norm.take(h, t)

        pr = Project(p, ctx, [[p.wT[:, k, kb, :] for kb in range(KB)] for k in wk], D, put, take)
        old, scaled = pr.slots[:, :, 0, :], pr.flip[:, :, 0:D]
        s = lambda name: p.sem("g_" + name, ctx)
        s_dve, s_scaled, s_active = s("s_dve"), s("s_scaled"), s("s_active")
        s_summed = s("s_summed")
        s_old = [s(f"s_old{u}") for u in range(U)]
        block = ctx.enter_context(nc.Block())

        @block.vector
        def _(dve):
            c = Chain(dve, s_dve)
            if mean_of_edges:
                c.link(v.tensor_scalar(deg[:], p.acc[:, :, D], 1.0, None, ALU.max))
                c.link(v.reciprocal(deg[:], deg[:]))
            if len(biases) == 2:
                c.link(v.tensor_tensor(bias[:], biases[0][:], biases[1][:], ALU.add))
            else:
                c.link(v.tensor_copy(bias[:], biases[0][:]))
            pr.dve(dve, c, 1)
            dve.wait_ge(pr.s_taken, NT + 3)
            norm.finish(dve, c)

            def scale(t, u):
                h = flat(p.acc[:, bass.ds(t, 1), 0:D])
                if not (isinstance(t, int) and t == 0):
                    dve.wait_ge(s_scaled, t)
                c.link(v.scalar_tensor_tensor(out=centered[:], in0=h, scalar=norm.mean[:, bass.ds(t, 1)],
                                              in1=gamma[:], op0=ALU.subtract, op1=ALU.mult))
                v.scalar_tensor_tensor(out=scaled[:, u, :], in0=centered[:], scalar=norm.rstd[:, bass.ds(t, 1)],
                                       in1=beta[:], op0=ALU.mult, op1=ALU.add).then_inc(s_scaled, 1)

            def add_old(t, u, i):
                dve.wait_ge(s_active, t + 1)
                dve.wait_ge(s_old[u], 16 * i + 16)
                x = flat(p.acc[:, bass.ds(t, 1), 0:D])
                v.tensor_tensor(x, active[:, u, :], old[:, u, :], ALU.add).then_inc(s_summed, 1)
                dve.wait_ge(s_summed, t + 1)
                c.done(norm2.take(x, t))

            scale(0, 0)
            with dve.Fori(0, STEPS - 1) as i:
                c.enter(i, (2 if residual is not None else 1) * U)
                for u in range(U):
                    scale(U * i + u + 1, (u + 1) % U)
                    if residual is not None:
                        add_old(U * i + u, u, i)
                    else:
                        dve.wait_ge(s_active, U * i + u + 1)
            c.leave(STEPS - 1)
            for u in range(U):
                t = U * (STEPS - 1) + u
                if u < U - 1:
                    scale(t + 1, u + 1)
                if residual is not None:
                    add_old(t, u, STEPS - 1)
                else:
                    dve.wait_ge(s_active, t + 1)
            c.settle()
            if residual is not None:
                norm2.finish(dve, c)
                with dve.Fori(0, NT) as t:
                    v.tensor_scalar(flat(p.xb[:, bass.ds(t, 1), :]), flat(p.acc[:, bass.ds(t, 1), 0:D]),
                                    norm2.mean[:, bass.ds(t, 1)], norm2.rstd[:, bass.ds(t, 1)],
                                    ALU.subtract, ALU.mult).then_inc(s_dve, 1)
                c.n += NT
                c.settle()

        @block.tensor
        def _(pe):
            pr.pe(pe)

        @block.scalar
        def _(act):
            pr.act(act)
            norm.root(act)
            with act.Fori(0, STEPS) as i:
                for u in range(U):
                    act.wait_ge(s_scaled, U * i + u + 1)
                    out = flat(p.xb[:, bass.ds(U * i + u, 1), :]) if residual is None else active[:, u, :]
                    nc.scalar.activation(out, scaled[:, u, :], func).then_inc(s_active, 1)
            if residual is not None:
                norm2.root(act)

        if residual is not None:
            @block.sync
            def _(sp):
                sp.wait_ge(pr.s_taken, NT + 3)
                for u in range(U):
                    sp.dma_start(old[:, u, :], rows(residual, u)).then_inc(s_old[u], 16)
                with sp.Fori(0, STEPS - 2) as i:
                    for u in range(U):
                        sp.wait_ge(s_summed, U * i + u + 1)
                        sp.dma_start(old[:, u, :], residual[bass.ds(P * (U * i + U + u), P), :]).then_inc(s_old[u], 16)
                for u in range(U):
                    t = U * (STEPS - 1) + u
                    n = LAST if t == NT - 1 else P
                    sp.wait_ge(s_summed, t - U + 1)
                    sp.dma_start(old[0:n, u, :], rows(residual, t, n)).then_inc(s_old[u], 16)



def route_to_experts(p):
    nc, v = p.nc, p.nc.vector
    with ExitStack() as outer:
        logits = p.sb("r_logits", [P, NT, EX], F32, outer)
        with ExitStack() as ctx:
            def put(t, slots):
                return [v.tensor_copy(slots[0], flat(p.xb[:, bass.ds(t, 1), :]))]

            def take(t, psum, c):
                c.link(v.tensor_tensor(flat(logits[:, bass.ds(t, 1), :]), psum[:, 0:EX], p.br[:], ALU.add))
                return p.norm_in.take(flat(p.xb[:, bass.ds(t, 1), :]), t)

            pr = Project(p, ctx, [[p.Wr[:, kb, :] for kb in range(KB)]], EX, put, take)
            s_dve = p.sem("r_s_dve", ctx)
            block = ctx.enter_context(nc.Block())

            @block.vector
            def _(dve):
                c = Chain(dve, s_dve)
                pr.dve(dve, c, 1)
                dve.wait_ge(pr.s_taken, NT + 3)
                p.norm_in.finish(dve, c)

            @block.tensor
            def _(pe):
                pr.pe(pe)

            @block.scalar
            def _(act):
                pr.act(act)
                p.norm_in.root(act)

        with ExitStack() as ctx:
            names = ("expert", "cap", "rest", "hot0", "hot1", "tmp", "place")
            expert, cap, rest, hot0, hot1, tmp, place = (p.sb("r_" + n, [P, NT, EX], F32, ctx) for n in names)
            top = [p.sb(f"r_top{k}", [P, NT], F32, ctx) for k in range(TOP)]
            first = p.sb("r_first", [P, NT], F32, ctx)
            gap = p.sb("r_gap", [P, NT], F32, ctx)
            past, valid, where = (p.sb("r_" + n, [P, NT], F32, ctx) for n in ("past", "valid", "where"))
            ones = p.sb("r_ones", [P, NT], F32, ctx)
            b = Binning(p, ctx, EX, MOE_TILES)
            s_dve, s_gap, s_exp = (p.sem("r2_" + n, ctx) for n in ("s_dve", "s_gap", "s_exp"))
            block = ctx.enter_context(nc.Block())

            def wide(ap):
                return ap.unsqueeze(2).to_broadcast([P, NT, EX])

            @block.tensor
            def _(pe):
                b.products(pe, 0, None, b.s_count)

            @block.scalar
            def _(act):
                act.wait_ge(s_gap, 1)
                nc.scalar.activation(gap[:], gap[:], ACT.Exp).then_inc(s_exp, 1)

            @block.vector
            def _(dve):
                c = Chain(dve, s_dve)
                c.link(v.tensor_scalar(expert[:, 0, :], p.iota[:, 0:EX], -float(EX), None, ALU.add))
                c.link(v.tensor_copy(expert[:, 1:NT, :], expert[:, 0:1, :].to_broadcast([P, NT - 1, EX])))
                c.done(v.memset(ones[:], 1.0))
                c.done(v.memset(p.place_i[:], 0))
                c.done(v.tensor_scalar(valid[:], p.node_no[:], float(N), None, ALU.is_lt))
                c.done(v.tensor_scalar(past[:], p.node_no[:], float(N), None, ALU.is_ge))
                c.done(v.tensor_scalar(gap[:, 0:1], p.part_no[:], float(MOE_TILES * FT), None, ALU.add))
                c.settle()
                c.link(v.tensor_scalar(past[:], past[:], gap[:, 0:1], None, ALU.mult))
                values = logits
                for k, hot in enumerate((hot0, hot1)):
                    c.link(v.tensor_reduce(top[k][:], values[:], AX, ALU.max))
                    c.link(v.tensor_tensor(tmp[:], values[:], wide(top[k][:]), ALU.is_equal))
                    c.link(v.tensor_tensor(tmp[:], tmp[:], expert[:], ALU.mult))
                    c.link(v.tensor_reduce(first[:], tmp[:], AX, ALU.min))
                    c.link(v.tensor_tensor(hot[:], expert[:], wide(first[:]), ALU.is_equal))
                    if k == 0:
                        c.link(v.tensor_scalar(cap[:], hot[:], -2.0, 1.0, ALU.mult, ALU.add))
                        c.link(v.tensor_scalar(cap[:], cap[:], 3.0e38, None, ALU.mult))
                        c.link(v.tensor_tensor(rest[:], logits[:], cap[:], ALU.min))
                        values = rest
                v.tensor_tensor(gap[:], top[1][:], top[0][:], ALU.subtract).then_inc(s_gap, 1)
                for hot in (hot0, hot1):
                    c.done(v.tensor_tensor(hot[:], hot[:], wide(valid[:]), ALU.mult))
                c.settle()
                c.link(v.tensor_tensor(tmp[:], hot0[:], hot1[:], ALU.add))
                v.tensor_reduce(b.count[:], tmp[:].rearrange("p t e -> p e t"), AX, ALU.add).then_inc(b.s_count, 1)
                b.starts(dve, c, 0, 8, FT)
                for e in range(EX):
                    c.done(v.tensor_tensor_scan(place[:, :, e], ones[:], tmp[:, :, e], b.start[:, e:e + 1],
                                                ALU.mult, ALU.add))
                c.settle()
                for k, hot in enumerate((hot0, hot1)):
                    c.link(v.tensor_tensor(tmp[:], hot[:], place[:], ALU.mult))
                    c.link(v.tensor_reduce(where[:], tmp[:], AX, ALU.add))
                    c.link(v.tensor_tensor(where[:], where[:], past[:], ALU.add))
                    c.link(v.tensor_copy(p.place_i[:, k, 0:NT], where[:]))
                b.table(dve, c, 0, p.expert_of)
                dve.wait_ge(s_exp, 1)
                c.link(v.tensor_scalar(p.share[:, 0, :], gap[:], 1.0, None, ALU.add))
                c.link(v.reciprocal(p.share[:, 0, :], p.share[:, 0, :]))
                c.link(v.tensor_tensor(p.share[:, 1, :], gap[:], p.share[:, 0, :], ALU.mult))


def dispatch(p, into, places, choices, normed):
    nc, v = p.nc, p.nc.vector
    with ExitStack() as ctx:
        row = p.sb("d_row", [P, U, D], F32, ctx)
        slot = p.sb("d_slot", [P, U, TOP], I32, ctx)
        s = lambda name: p.sem("d_" + name, ctx)
        s_idle, s_start = s("s_idle"), s("s_start")
        s_full = [s(f"s_full{u}") for u in range(U)]
        s_sent = [s(f"s_sent{u}") for u in range(U)]
        block = ctx.enter_context(nc.Block())

        @block.vector
        def _(dve):
            def fill(t, u):
                x = flat(p.xb[:, bass.ds(t, 1), :])
                if normed:
                    v.tensor_scalar(row[:, u, :], x, p.norm_in.mean[:, bass.ds(t, 1)],
                                    p.norm_in.rstd[:, bass.ds(t, 1)], ALU.subtract, ALU.mult).then_inc(s_full[u], 1)
                else:
                    v.tensor_copy(row[:, u, :], x).then_inc(s_full[u], 1)
                for k in range(choices):
                    v.tensor_copy(slot[:, u, k:k + 1], p.place_i[:, k, bass.ds(t, 1)]).then_inc(s_full[u], 1)

            for u in range(U):
                fill(u, u)
            with dve.Fori(0, STEPS - 1) as i:
                for u in range(U):
                    dve.wait_ge(s_sent[u], 16 * choices * i + 16 * choices)
                    fill(U * i + U + u, u)

        @block.gpsimd
        def _(pool):
            ready = PoolWait(p, pool, s_idle)
            with pool.Fori(0, STEPS) as i:
                for u in range(U):
                    ready(s_full[u], (choices + 1) * i + choices + 1, U * i + u)
                    for k in range(choices):
                        pool.indirect_dma_start(into[0:places, :], bass.IndirectOffsetOnAxis(ap=slot[:, u, k:k + 1], axis=0),
                                                row[:, u, :], None, bounds_check=places - 1,
                                                oob_is_err=False).then_inc(s_sent[u], 16)
            for u in range(U):
                pool.wait_ge(s_sent[u], 16 * choices * STEPS)


def combine(p, source, choices, add_xb, share, norm):
    nc, v = p.nc, p.nc.vector
    with ExitStack() as ctx:
        got = p.sb("c_got", [P, U, TOP, D], F32, ctx)
        slot = p.sb("c_slot", [P, U, TOP], I32, ctx)
        s = lambda name: p.sem("c_" + name, ctx)
        s_idle, s_dve = s("s_idle"), s("s_dve")
        s_slot = [s(f"s_slot{u}") for u in range(U)]
        s_got = [s(f"s_got{u}") for u in range(U)]
        block = ctx.enter_context(nc.Block())

        @block.vector
        def _(dve):
            c = Chain(dve, s_dve)

            def fill(t, u):
                for k in range(choices):
                    v.tensor_copy(slot[:, u, k:k + 1], p.place_i[:, k, bass.ds(t, 1)]).then_inc(s_slot[u], 1)

            for u in range(U):
                fill(u, u)
            per = choices + int(add_xb) + int(norm is not None)
            with dve.Fori(0, STEPS) as i:
                c.enter(i, U * per)
                for u in range(U):
                    t = U * i + u
                    x = flat(p.acc[:, bass.ds(t, 1), 0:D])
                    if add_xb:
                        c.link(v.tensor_tensor(x, x, flat(p.xb[:, bass.ds(t, 1), :]), ALU.add))
                    dve.wait_ge(s_got[u], 16 * choices * i + 16 * choices)
                    for k in range(choices):
                        c.link(v.scalar_tensor_tensor(out=x, in0=got[:, u, k, :], scalar=share[:, k, bass.ds(t, 1)],
                                                      in1=x, op0=ALU.mult, op1=ALU.add))
                    if norm is not None:
                        c.done(norm.take(x, t))
                    fill(t + U, u)
            c.leave(STEPS)
            if norm is not None:
                c.settle()
                norm.finish(dve, c)
                with dve.Fori(0, NT) as t:
                    v.tensor_scalar(flat(p.xb[:, bass.ds(t, 1), :]), flat(p.acc[:, bass.ds(t, 1), 0:D]),
                                    norm.mean[:, bass.ds(t, 1)], norm.rstd[:, bass.ds(t, 1)],
                                    ALU.subtract, ALU.mult).then_inc(s_dve, 1)
                c.n += NT
                c.settle()

        @block.gpsimd
        def _(pool):
            ready = PoolWait(p, pool, s_idle)
            with pool.Fori(0, STEPS) as i:
                for u in range(U):
                    ready(s_slot[u], choices * i + choices, U * i + u)
                    for k in range(choices):
                        pool.indirect_dma_start(got[:, u, k, :], None, source,
                                                bass.IndirectOffsetOnAxis(ap=slot[:, u, k:k + 1], axis=0)).then_inc(s_got[u], 16)

        if norm is not None:
            @block.scalar
            def _(act):
                norm.root(act)



def ffn(p, source, result, count, weights, experts, func, sort_second):
    nc, v = p.nc, p.nc.vector
    W1, W2, b1, b2 = weights
    with ExitStack() as ctx:
        wslots = 2 if experts else 1
        size = wslots * KB * H
        if experts:
            room = p.xb[:].rearrange("p t d -> p (t d)")
        else:
            room = p.sb("f_weights", [P, 2 * size], F32, ctx)
        w1 = room[:, 0:size].rearrange("p (s b h) -> p s b h", s=wslots, b=KB)
        w2 = room[:, size:2 * size].rearrange("p (s b d) -> p s b d", s=wslots, b=HB)
        xin = p.sb("f_xin", [P, 2, 2, D], F32, ctx)
        xT = p.sb("f_xT", [P, KB, FT], F32, ctx)
        hT = p.sb("f_hT", [P, 2, HB, FT], F32, ctx)
        y = p.sb("f_y", [P, 2, 2, D], F32, ctx)
        ps_x = p.ps("f_ps_x", [P, KB, FT], ctx)
        ps_h = [p.ps(f"f_ps_h{i}", [P, 512], ctx) for i in range(4)]
        ps_y = [p.ps(f"f_ps_y{i}", [P, 512], ctx) for i in range(2)]
        s = lambda name: p.sem("f_" + name, ctx)
        s_x = [s(f"s_x{i}") for i in range(2)]
        s_w = [s(f"s_w{i}") for i in range(2)]
        s_out = [s(f"s_out{i}") for i in range(2)]
        s_flip, s_xT, s_up, s_act, s_down, s_y = (s(n) for n in ("s_flip", "s_xT", "s_up", "s_act", "s_down", "s_y"))
        if sort_second:
            s_pool, s_idle = s("s_pool"), s("s_idle")
            s_scat = [s(f"s_scat{h}") for h in range(2)]
            s_slot = [s(f"s_slot{h}") for h in range(2)]
            slot_addr = p.sb("f_slot_addr", [P, 2 * EU], I32, ctx)
            slot_rec = p.sb("f_slot_rec", [P, 2 * EU, 2], I32, ctx)
        block = ctx.enter_context(nc.Block())
        pairs = (count - 3) // 2
        rest = count - 2 - 2 * pairs

        def over_tiles(eng, tile):
            for t in range(2):
                tile(t, t, 0, t == 0, False)
            with eng.Fori(0, pairs) as i:
                for k in range(2):
                    tile(2 * i + 2 + k, k, i + 1, False, False)
            for t in range(count - rest, count):
                tile(t, t % 2, t // 2, False, t == count - 1)

        def expert(eng, t):
            return eng.value_load(p.expert_of[0:1, bass.ds(t, 1)], min_val=0, max_val=EX - 1)

        @block.sync
        def _(sp):
            x_dram = source.rearrange("(t p c) d -> t p c d", p=P, c=2)
            y_dram = result[0:count * FT, :].rearrange("(t p c) d -> t p c d", p=P, c=2)

            def at(ap, t):
                return ap[bass.ds(t, 1)].rearrange("a p c d -> (a p) c d")

            def load(t, k):
                sp.dma_start(xin[:, k, :, :], at(x_dram, t)).then_inc(s_x[k], 16)
                if experts:
                    e = expert(sp, t)
                    sp.dma_start(w1[:, k, :, :], W1[bass.ds(e, 1)].rearrange("a (b p) h -> (a p) b h", p=P)).then_inc(s_w[k], 16)
                    sp.dma_start(w2[:, k, :, :], W2[bass.ds(e, 1)].rearrange("a (b p) d -> (a p) b d", p=P)).then_inc(s_w[k], 16)

            if not experts:
                sp.dma_start(w1[:, 0, :, :], W1.rearrange("(b p) h -> p b h", p=P)).then_inc(s_w[0], 16)
                sp.dma_start(w2[:, 0, :, :], W2.rearrange("(b p) d -> p b d", p=P)).then_inc(s_w[0], 16)
            load(0, 0)
            load(1, 1)

            def tile(t, k, uses, first, last, more=True):
                sp.wait_ge(s_down, t + 1)
                if more:
                    load(t + 2, k)
                sp.wait_ge(s_y, 2 * t + 2)
                sp.dma_start(at(y_dram, t), y[:, k, :, :]).then_inc(s_out[k], 16)

            ahead = (count - 2) // 2
            with sp.Fori(0, ahead) as i:
                for k in range(2):
                    tile(2 * i + k, k, None, False, False)
            for t in range(2 * ahead, count):
                tile(t, t % 2, None, False, False, more=t + 2 < count)
            for k in range(2):
                sp.wait_ge(s_out[k], 16 * ((count + 1 - k) // 2))

        @block.tensor
        def _(pe):
            def flip(t, k, uses):
                pe.wait_ge(s_x[k], 16 * uses + 16)
                for blk in range(2):
                    for kb in range(KB):
                        last = nc.tensor.transpose(ps_x[:, kb, blk * P:(blk + 1) * P],
                                                   xin[:, k, blk, kb * P:(kb + 1) * P], p.ident[:])
                last.then_inc(s_flip, 1)

            flip(0, 0, 0)

            def tile(t, k, uses, first, last):
                wk = k if experts else 0
                pe.wait_ge(s_xT, 2 * t + 2)
                pe.wait_ge(s_w[wk], 32 * uses + 32 if experts else 32)
                for j in range(HB):
                    if not (first and j < 4):
                        pe.wait_ge(s_act, HB * t + j - 3)
                    for kb in range(KB):
                        mm = nc.tensor.matmul(ps_h[j % 4][:, 0:FT], w1[:, wk, kb, j * P:(j + 1) * P], xT[:, kb, :],
                                              start=(kb == 0), stop=(kb == KB - 1))
                    mm.then_inc(s_up, 1)
                if not last:
                    flip(t + 1, 1 - k, uses + (1 if k == 1 else 0))
                if not first:
                    pe.wait_ge(s_y, 2 * t)
                for j in range(HB):
                    pe.wait_ge(s_act, HB * t + j + 1)
                    for blk in range(2):
                        mm = nc.tensor.matmul(ps_y[blk][:, 0:D], hT[:, k, j, blk * P:(blk + 1) * P], w2[:, wk, j, :],
                                              start=(j == 0), stop=(j == HB - 1))
                mm.then_inc(s_down, 1)

            over_tiles(pe, tile)

        @block.scalar
        def _(act):
            def tile(t, k, uses, first, last):
                if experts:
                    e = expert(act, t)
                for j in range(HB):
                    bias = flat(b1[:, bass.ds(e, 1), j:j + 1]) if experts else b1[:, j:j + 1]
                    act.wait_ge(s_up, HB * t + j + 1)
                    nc.scalar.activation(hT[:, k, j, :], ps_h[j % 4][:, 0:FT], func, bias=bias).then_inc(s_act, 1)

            over_tiles(act, tile)

        @block.vector
        def _(dve):
            def evacuate(t):
                if experts:
                    e = expert(dve, t)
                dve.wait_ge(s_flip, t + 1)
                for kb in range(KB):
                    if experts:
                        ins = v.tensor_scalar(xT[:, kb, :], ps_x[:, kb, :], p.ln_g[:, kb, bass.ds(e, 1)],
                                              p.ln_b[:, kb, bass.ds(e, 1)], ALU.mult, ALU.add)
                    else:
                        ins = v.tensor_copy(xT[:, kb, :], ps_x[:, kb, :])
                    ins.then_inc(s_xT, 1)

            evacuate(0)

            def tile(t, k, uses, first, last):
                if not last:
                    evacuate(t + 1)
                if experts:
                    e = expert(dve, t)
                dve.wait_ge(s_down, t + 1)
                if not (isinstance(uses, int) and uses == 0):
                    dve.wait_ge(s_out[k], 16 * uses)
                for blk in range(2):
                    bias = flat(b2[:, bass.ds(e, 1), :]) if experts else b2[:]
                    v.tensor_tensor(y[:, k, blk, :], ps_y[blk][:, 0:D], bias, ALU.add).then_inc(s_y, 1)

            over_tiles(dve, tile)

        if sort_second:
            @block.gpsimd
            def _(pool):
                ready = PoolWait(p, pool, s_idle)

                def fill(h, c0):
                    a, b = h * EU, (h + 1) * EU
                    for out, value in ((slot_addr[:, a:b], p.addr1[:, bass.ds(c0, EU)]),
                                       (slot_rec[:, a:b, 0], p.rec1[:, bass.ds(c0, EU)]),
                                       (slot_rec[:, a:b, 1].bitcast(F32), p.weight1[:, bass.ds(c0, EU)])):
                        nc.gpsimd.tensor_copy(out, value).then_inc(s_slot[h], 1)

                def send(h):
                    for u in range(h * EU, (h + 1) * EU):
                        pool.indirect_dma_start(p.table1, bass.IndirectOffsetOnAxis(ap=slot_addr[:, u:u + 1], axis=0),
                                                slot_rec[:, u, :], None, bounds_check=P * QW - 1,
                                                oob_is_err=False).then_inc(s_scat[h], 16)

                for h in range(2):
                    fill(h, h * EU)
                    pool.wait_ge(s_slot[h], 3)
                    send(h)
                with pool.Fori(0, EC // (2 * EU) - 1) as i:
                    for h in range(2):
                        ready(s_scat[h], 16 * EU * i + 16 * EU, 4 * i + 2 * h)
                        pool.wait_ge(s_idle, 4 * i + 2 * h + 2)
                        fill(h, 2 * EU * i + 2 * EU + h * EU)
                        ready(s_slot[h], 3 * i + 6, 4 * i + 2 * h + 1)
                        send(h)
                for h in range(2):
                    pool.wait_ge(s_scat[h], 16 * EU * (EC // (2 * EU)))



def choose_larger_half(p):
    nc, v = p.nc, p.nc.vector
    with ExitStack() as outer:
        weight = p.share[:, 0, :]
        with ExitStack() as ctx:
            def put(t, slots):
                return [v.tensor_copy(slots[0], flat(p.xb[:, bass.ds(t, 1), :]))]

            def take(t, psum, c):
                return v.tensor_tensor(p.share[:, 0, bass.ds(t, 1)], psum[:, 0:1], p.mod_br[:], ALU.add)

            pr = Project(p, ctx, [[p.mod_wr[:, kb, :] for kb in range(KB)]], 1, put, take)
            s_dve = p.sem("h_s_dve", ctx)
            block = ctx.enter_context(nc.Block())

            @block.vector
            def _(dve):
                pr.dve(dve, Chain(dve, s_dve), 0)

            @block.tensor
            def _(pe):
                pr.pe(pe)

            @block.scalar
            def _(act):
                pr.act(act)

        with ExitStack() as ctx:
            bits, sign, part = (p.sb("h_" + n, [P, NT], I32, ctx) for n in ("bits", "sign", "part"))
            high, low, hit, above, tie, ties, sel, ones, past, scan, carry = (
                p.sb("h_" + n, [P, NT], F32, ctx)
                for n in ("high", "low", "hit", "above", "tie", "ties", "sel", "ones", "past", "scan", "carry"))
            cell = p.sb("h_cell", [P, 12], F32, ctx)
            ps_n = p.ps("h_ps_n", [P, 512], ctx)
            s_dve, s_n, s_sum = (p.sem("h2_" + n, ctx) for n in ("s_dve", "s_n", "s_sum"))
            block = ctx.enter_context(nc.Block())
            at, step, try_, num, goal, keep, over, need, start = (cell[:, k:k + 1] for k in range(9))
            ROUNDS = 16

            @block.tensor
            def _(pe):
                for r in range(2):
                    with pe.Fori(0, ROUNDS) as i:
                        pe.wait_ge(s_n, (ROUNDS + 1) * r + i + 1)
                        nc.tensor.matmul(ps_n[:, 0:1], p.ones[:], num, start=True, stop=True).then_inc(s_sum, 1)
                    pe.wait_ge(s_n, (ROUNDS + 1) * (r + 1))
                    nc.tensor.matmul(ps_n[:, 0:1], p.ones[:], num, start=True, stop=True).then_inc(s_sum, 1)
                pe.wait_ge(s_n, 2 * ROUNDS + 3)
                nc.tensor.matmul(ps_n[:, 64:64 + NT], p.before[:], tie[:], start=True, stop=True)
                nc.tensor.matmul(ps_n[:, 128:128 + NT], p.ones[:], tie[:], start=True, stop=True).then_inc(s_sum, 1)
                pe.wait_ge(s_n, 2 * ROUNDS + 4)
                nc.tensor.matmul(ps_n[:, 0:1], p.before[:], num, start=True, stop=True).then_inc(s_sum, 1)

            @block.vector
            def _(dve):
                c = Chain(dve, s_dve)
                wi = weight.bitcast(I32)
                c.link(v.tensor_single_scalar(sign[:], wi, 31, ALU.arith_shift_right))
                c.link(v.tensor_single_scalar(sign[:], sign[:], 0x7FFFFFFF, ALU.bitwise_and))
                c.link(v.tensor_tensor(bits[:], wi, sign[:], ALU.bitwise_xor))
                c.link(v.tensor_single_scalar(part[:], bits[:], 16, ALU.arith_shift_right))
                c.link(v.tensor_copy(high[:], part[:]))
                c.link(v.tensor_single_scalar(part[:], bits[:], 0xFFFF, ALU.bitwise_and))
                c.link(v.tensor_copy(low[:], part[:]))
                c.link(v.tensor_scalar(past[:], p.node_no[:], float(N), None, ALU.is_ge))
                c.link(v.tensor_scalar(scan[:], past[:], -200000.0, None, ALU.mult))
                c.link(v.tensor_tensor(high[:], high[:], scan[:], ALU.add))
                c.done(v.memset(goal, float(KEEP)))
                c.done(v.memset(ones[:], 1.0))
                c.done(v.memset(p.place_i[:], 0))
                c.settle()

                def search(r, values, first, per):
                    c.done(v.memset(at, first))
                    c.done(v.memset(step, 32768.0))
                    c.settle()
                    with dve.Fori(0, ROUNDS) as i:
                        c.enter(i, 5)
                        c.link(v.tensor_tensor(try_, at, step, ALU.add))
                        v.tensor_scalar(hit[:], values, try_, None, ALU.is_ge, ALU.add, accum_out=num).then_inc(s_n, 1)
                        dve.wait_ge(s_sum, (ROUNDS + 1) * r + i + 1)
                        c.link(v.tensor_tensor(keep, ps_n[:, 0:1], goal, ALU.is_ge))
                        c.link(v.tensor_tensor(keep, keep, step, ALU.mult))
                        c.link(v.tensor_tensor(at, at, keep, ALU.add))
                        c.link(v.tensor_scalar(step, step, 0.5, None, ALU.mult))
                    c.leave(ROUNDS)
                    v.tensor_scalar(hit[:], values, at, None, ALU.is_gt, ALU.add, accum_out=num).then_inc(s_n, 1)
                    dve.wait_ge(s_sum, (ROUNDS + 1) * (r + 1))
                    c.link(v.tensor_tensor(goal, goal, ps_n[:, 0:1], ALU.subtract))

                search(0, high[:], -32768.0, 5)
                c.done(v.tensor_scalar(above[:], high[:], at, None, ALU.is_gt))
                c.done(v.tensor_scalar(tie[:], high[:], at, None, ALU.is_equal))
                c.settle()
                c.link(v.tensor_scalar(low[:], low[:], 1.0, None, ALU.add))
                c.link(v.tensor_tensor(low[:], low[:], tie[:], ALU.mult))
                c.link(v.tensor_scalar(low[:], low[:], -1.0, None, ALU.add))
                search(1, low[:], 0.0, 5)
                c.done(v.tensor_scalar(scan[:], low[:], at, None, ALU.is_gt))
                c.settle()
                c.link(v.tensor_tensor(above[:], above[:], scan[:], ALU.add))
                v.tensor_scalar(tie[:], low[:], at, None, ALU.is_equal).then_inc(s_n, 1)
                dve.wait_ge(s_sum, 2 * ROUNDS + 3)
                c.link(v.tensor_copy(carry[:], ps_n[:, 128:128 + NT]))
                c.link(v.tensor_tensor_scan(ties[:], ones[:], carry[:], 0.0, ALU.mult, ALU.add))
                c.link(v.tensor_tensor(ties[:], ties[:], carry[:], ALU.subtract))
                c.link(v.tensor_tensor(ties[:], ties[:], ps_n[:, 64:64 + NT], ALU.add))
                c.link(v.tensor_scalar(ties[:], ties[:], goal, None, ALU.is_lt))
                c.link(v.tensor_tensor(ties[:], ties[:], tie[:], ALU.mult))
                c.link(v.tensor_tensor(sel[:], above[:], ties[:], ALU.add))
                v.tensor_scalar(hit[:], sel[:], 0.0, None, ALU.add, ALU.add, accum_out=num).then_inc(s_n, 1)
                dve.wait_ge(s_sum, 2 * ROUNDS + 4)
                c.link(v.tensor_scalar(start, ps_n[:, 0:1], -1.0, None, ALU.add))
                c.link(v.tensor_tensor_scan(scan[:], ones[:], sel[:], start, ALU.mult, ALU.add))
                c.link(v.tensor_tensor(scan[:], scan[:], sel[:], ALU.mult))
                c.link(v.tensor_scalar(over, p.part_no[:], float(MOD_TILES * FT), None, ALU.add))
                c.link(v.tensor_scalar(hit[:], sel[:], -1.0, 1.0, ALU.mult, ALU.add))
                c.link(v.tensor_scalar(hit[:], hit[:], over, None, ALU.mult))
                c.link(v.tensor_tensor(scan[:], scan[:], hit[:], ALU.add))
                c.link(v.tensor_copy(p.place_i[:, 0, 0:NT], scan[:]))


def store(p, pairs):
    with ExitStack() as ctx:
        s_st = p.sem("st_s", ctx)
        block = ctx.enter_context(p.nc.Block())

        @block.sync
        def _(sp):
            for dst, source in pairs:
                sp.dma_start(dst, source).then_inc(s_st, 16)
            sp.wait_ge(s_st, 16 * len(pairs))



INS = ["x", "src", "dst", "edge_weight", "L0_gnn_W0", "L0_gnn_b0", "L0_gnn_g0", "L0_gnn_beta0", "L0_gnn_W1",
       "L0_gnn_b1", "L0_gnn_g1", "L0_gnn_beta1", "L0_ffn_Wr", "L0_ffn_br", "L0_ffn_ln_g", "L0_ffn_ln_b",
       "L0_ffn_W1", "L0_ffn_b1", "L0_ffn_W2", "L0_ffn_b2", "L1_gnn_W_self", "L1_gnn_b_self", "L1_gnn_W_msg",
       "L1_gnn_b_msg", "L1_gnn_ln_gamma", "L1_gnn_ln_beta", "L1_ffn_wr", "L1_ffn_br", "L1_ffn_w1", "L1_ffn_b1",
       "L1_ffn_w2", "L1_ffn_b2"]


def columns(ap):
    return ap.rearrange("(b p) -> p b", p=P)


def build(nc, io, out):
    dram = {name: nc.dram_tensor(name, shape, dt).ap() for name, shape, dt in (
        ("table0", (P * QW, 1), I32), ("table1", (P * QW, 2), I32), ("xn", (NT * P, D), F32),
        ("h1", (NT * P, D), F32), ("x2", (NT * P, D), F32),
        ("moe_in", (MOE_TILES * FT, D), F32), ("moe_out", (MOE_TILES * FT + P, D), F32),
        ("mod_in", (MOD_TILES * FT, D), F32), ("mod_out", (MOD_TILES * FT + P, D), F32))}
    with ExitStack() as ctx:
        p = Program(nc, ctx)
        p.ident, p.before, p.upto, p.ones, p.iota = (p.sb(n, [P, P]) for n in ("ident", "before", "upto", "ones", "iota"))
        p.chunk_no, p.part_no, p.node_no = p.sb("chunk_no", [P, NCH]), p.sb("part_no", [P, 1]), p.sb("node_no", [P, NT])
        p.eps, p.idle = p.sb("eps", [P, 1]), p.sb("idle", [1, 2])
        p.acc, p.xb = p.sb("acc", [P, NT, D + 1]), p.sb("xb", [P, NT, D])
        p.edge_row, p.edge_local, p.edge_weight = p.sb("edge_row", [P, QW], I32), p.sb("edge_local", [P, QW]), p.sb("edge_weight", [P, QW])
        p.addr1, p.rec1, p.weight1 = p.sb("addr1", [P, EC], I32), p.sb("rec1", [P, EC], I32), p.sb("weight1", [P, EC])
        p.place_i, p.share, p.expert_of = p.sb("place_i", [P, TOP, NT + U], I32), p.sb("share", [P, TOP, NT]), p.sb("expert_of", [1, MOE_TILES], I32)
        p.wT, p.Wr, p.mod_wr = p.sb("wT", [P, 4, KB, D]), p.sb("Wr", [P, KB, EX]), p.sb("mod_wr", [P, KB, 1])
        p.br, p.mod_br = p.sb("br", [P, EX]), p.sb("mod_br", [P, 1])
        p.ln_g, p.ln_b = p.sb("ln_g", [P, KB, EX]), p.sb("ln_b", [P, KB, EX])
        p.moe_b1, p.moe_b2, p.mod_b1 = p.sb("moe_b1", [P, EX, HB]), p.sb("moe_b2", [P, EX, D]), p.sb("mod_b1", [P, HB])
        row_params = {name: p.sb("row_" + name, [P, D]) for name in
                      ("L0_gnn_b0", "L0_gnn_b1", "L1_gnn_b_self", "L1_gnn_b_msg", "L0_gnn_g0", "L0_gnn_g1",
                       "L1_gnn_ln_gamma", "L0_gnn_beta0", "L0_gnn_beta1", "L1_gnn_ln_beta", "L1_ffn_b2")}
        p.tile_of = [p.sb(f"tile_of{k}", [1, NCH], I32) for k in range(2)]
        p.norm_in, p.norm_out = RowNorm(p, ctx), RowNorm(p, ctx)
        p.table1 = dram["table1"]
        p.small = [(p.Wr[:], io["L0_ffn_Wr"].rearrange("(b p) e -> p b e", p=P)),
                   (p.br[:], io["L0_ffn_br"].partition_broadcast(P)),
                   (p.mod_br[:], io["L1_ffn_br"].partition_broadcast(P)),
                   (p.mod_wr[:], io["L1_ffn_wr"].rearrange("(b p) e -> p b e", p=P)),
                   (p.mod_b1[:], columns(io["L1_ffn_b1"]))]
        for e in range(EX):
            p.small += [(p.ln_g[:, :, e], columns(io["L0_ffn_ln_g"][e, :])),
                        (p.ln_b[:, :, e], columns(io["L0_ffn_ln_b"][e, :])),
                        (p.moe_b1[:, e, :], columns(io["L0_ffn_b1"][e, :])),
                        (p.moe_b2[:, e, :], io["L0_ffn_b2"][e, :].partition_broadcast(P))]
        for name, row in row_params.items():
            p.small.append((row[:], io[name].partition_broadcast(P)))

        def stage(name, make, *args):
            p.stage = name + "_"
            with nc.cleanup_on_exit():
                make(p, *args)

        stage("sort", sort_edges_and_normalize, io, dram)
        stage("unpack0", unpack_table, dram["table0"], 1)
        stage("sum0", sum_over_edges, dram["xn"], 0, False)
        stage("gnn0", gnn_dense, [0], [row_params["L0_gnn_b0"]], row_params["L0_gnn_g0"], row_params["L0_gnn_beta0"], ACT.Silu, None)
        stage("h1", store, [(tiles(dram["h1"], 0, NT), p.xb[:])])
        stage("sum1", sum_over_edges, dram["h1"], 0, False)
        stage("gnn1", gnn_dense, [1], [row_params["L0_gnn_b1"]], row_params["L0_gnn_g1"], row_params["L0_gnn_beta1"], ACT.Silu, io["x"])
        stage("route", route_to_experts)
        stage("moe_in", dispatch, dram["moe_in"], MOE_TILES * FT, TOP, True)
        stage("moe", ffn, dram["moe_in"], dram["moe_out"], MOE_TILES,
              (io["L0_ffn_W1"], io["L0_ffn_W2"], p.moe_b1, p.moe_b2), True, ACT.Gelu, True)
        stage("moe_out", combine, dram["moe_out"], TOP, False, p.share, p.norm_out)
        stage("x2", store, [(tiles(dram["x2"], 0, NT), p.acc[:, :, 0:D]), (tiles(dram["xn"], 0, NT), p.xb[:])])
        stage("unpack1", unpack_table, dram["table1"], 2)
        stage("sum2", sum_over_edges, dram["xn"], 1, True)
        stage("gnn2", gnn_dense, [2, 3], [row_params["L1_gnn_b_self"], row_params["L1_gnn_b_msg"]],
              row_params["L1_gnn_ln_gamma"], row_params["L1_gnn_ln_beta"], ACT.Gelu, dram["x2"])
        stage("half", choose_larger_half)
        stage("half_in", dispatch, dram["mod_in"], MOD_TILES * FT, 1, False)
        stage("ffn", ffn, dram["mod_in"], dram["mod_out"], MOD_TILES,
              (io["L1_ffn_w1"], io["L1_ffn_w2"], p.mod_b1, row_params["L1_ffn_b2"]), False, ACT.Gelu_apprx_tanh, False)
        stage("half_out", combine, dram["mod_out"], 1, True, p.share, None)
        stage("out", store, [(tiles(out, 0, NT - 1), p.acc[:, 0:NT - 1, 0:D]),
                             (rows(out, NT - 1, LAST), p.acc[0:LAST, NT - 1, 0:D])])


def kernel(**inputs):
    import concourse.bacc as bacc
    from concourse.bass_utils import run_bass_kernel_spmd

    nc = bacc.Bacc("TRN2", target_bir_lowering=False, num_devices=1)
    arrays, io = {}, {}
    for name in INS:
        a = np.ascontiguousarray(inputs[name])
        arrays[f"in_{name}"] = a
        io[name] = nc.dram_tensor(f"in_{name}", a.shape, mybir.dt.from_np(a.dtype), kind="ExternalInput").ap()
    out = nc.dram_tensor("out", (N, D), F32, kind="ExternalOutput").ap()
    build(nc, io, out)
    r = run_bass_kernel_spmd(nc, [arrays], core_ids=[0])
    return r.results[0]["out"]
```

```python
from contextlib import ExitStack

import numpy as np
import concourse.bass as bass
from concourse import mybir

ALU = mybir.AluOpType
ACT = mybir.ActivationFunctionType
AX = mybir.AxisListType.X
F32 = mybir.dt.float32
BF16 = mybir.dt.bfloat16
U16 = mybir.dt.uint16
I32 = mybir.dt.int32

P = 128
N = 6250
D = 256
KB = D // P
H = 1024
HB = H // P
NT = -(-N // P)
LAST = N - (NT - 1) * P
E = 100000
EC = 784
EROWS = E // EC
ETAIL = E - EROWS * EC
EU = 8
GROUPS = 4
SU = GROUPS * EU
NCH = -(-((E + NT * (P - 1)) // P) // SU) * SU
QW = NCH + SU
SE = 14
SGROUPS = 4
SSTEP = SGROUPS * SE
PARTS = ((0, 112), (112, 336), (336, EC))
KEYBITS = 13
NONE = P
EX = 8
TOP = 2
FT = 256
MOE_TILES = (TOP * N + EX * (FT - 1)) // FT
KEEP = N // 2 - 1
MOD_TILES = -(-KEEP // FT)
EPS = 1e-5
ROUNDS, WAYS = 4, 15
U = 7
STEPS = NT // U
assert STEPS * U == NT and EC % SSTEP == 0 and MOE_TILES % 2 == 0


class Chain:

    def __init__(self, eng, sem):
        self.eng, self.sem, self.n, self.base = eng, sem, 0, 0

    def done(self, ins):
        ins.then_inc(self.sem, 1)
        self.n += 1

    def settle(self, but=0):
        self.eng.wait_ge(self.sem, self.base + self.n - but)

    def link(self, ins):
        self.done(ins)
        self.settle()

    def enter(self, i, per):
        self.start, self.per, self.base = self.n, per, i * per

    def leave(self, iterations):
        assert self.n - self.start == self.per, (self.n - self.start, self.per)
        self.n, self.base = self.start + iterations * self.per, 0


class PoolWait:

    def __init__(self, p, pool, sem):
        self.p, self.pool, self.sem = p, pool, sem
        p.nc.gpsimd.memset(p.idle[:], 0.0).then_inc(sem, 1)
        pool.wait_ge(sem, 1)

    def __call__(self, sem, value, before):
        self.pool.wait_ge(self.sem, before + 1)
        self.pool.wait_ge(sem, value)
        self.p.nc.gpsimd.tensor_tensor(self.p.idle[:, 0:1], self.p.idle[:, 1:2], self.p.idle[:, 1:2],
                                       ALU.add).then_inc(self.sem, 1)


def rows(dram, t, n=P):
    return dram[t * P:t * P + n, :]


def tiles(dram, a, b):
    return dram[a * P:b * P, :].rearrange("(t p) d -> p t d", p=P)


class Program:
    def __init__(self, nc, ctx):
        self.nc, self.ctx, self.names, self.stage = nc, ctx, 0, ""

    def sb(self, name, shape, dt=F32, ctx=None):
        return (ctx or self.ctx).enter_context(self.nc.sbuf_tensor(self.stage + name, shape, dt))

    def ps(self, name, shape, ctx):
        return ctx.enter_context(self.nc.psum_tensor(self.stage + name, shape, F32))

    def sem(self, name, ctx):
        return self.nc.alloc_semaphore(self.stage + name)



def sort_edges_and_normalize(p, io, dram):
    nc = p.nc
    with ExitStack() as ctx:
        key = [p.sb(f"key{k}", [P, EC], I32, ctx) for k in range(2)]
        weight = p.weight1
        win_i = p.sb("win_i", [P, EC], I32, ctx)
        win = p.sb("win", [P, EC], BF16, ctx)
        mask = p.sb("mask", [P, 2, EC], BF16, ctx)
        ones_row = p.sb("ones_row", [P, EC], BF16, ctx)
        pos = p.sb("pos", [P, EC], F32, ctx)
        pos_i = p.sb("pos_i", [P, EC], I32, ctx)
        lane = p.sb("lane", [P, EC], I32, ctx)
        local = p.sb("local_sh", [P, EC], I32, ctx)
        addr = [p.sb("addr0", [P, EC], I32, ctx), p.addr1]
        rec = [p.sb("rec0", [P, EC], I32, ctx), p.rec1]
        count = p.sb("count", [P, NT], F32, ctx)
        room = p.acc[:].rearrange("p t d -> p (t d)")
        fill = room[:, 0:2 * QW].bitcast(I32)
        zero = room[:, 2 * QW:2 * QW + 4 * D]
        wload = room[:, 2 * QW + 4 * D:2 * QW + 4 * D + 4 * KB * D].rearrange("p (k b d) -> p k b d", k=4, b=KB)
        slot_addr = p.sb("slot_addr", [P, SSTEP], I32, ctx)
        slot_rec = p.sb("slot_rec", [P, SSTEP], I32, ctx)
        xb = p.xb
        norm = RowNorm(p, ctx)
        used = 2 * QW + 4 * D + 4 * KB * D
        product = room[:, used:used + 2 * EC].rearrange("p (b c) -> p b c", b=2)
        rank = room[:, used + 2 * EC:used + 4 * EC].rearrange("p (b c) -> p b c", b=2)
        b = Binning(p, ctx, NT, NCH)
        psw = [p.ps(f"psw{i}", [P, 512], ctx) for i in range(2)]

        s = lambda name: p.sem(name, ctx)
        s_const, s_keys0, s_keys1, s_keyfill = s("s_const"), s("s_keys0"), s("s_keys1"), s("s_keyfill")
        s_dve, s_pe, s_addr, s_fill, s_prefill = s("s_dve"), s("s_pe"), s("s_addr"), s("s_fill"), s("s_prefill")
        s_zero, s_xpad, s_x, s_xn, s_xnout = (
            s("s_zero"), s("s_xpad"), s("s_x"), s("s_xn"), s("s_xnout"))
        s_slot = [s(f"s_slot{h}") for h in range(SGROUPS)]
        s_scat = [s(f"s_scat{h}") for h in range(SGROUPS)]
        s_wload, s_wT, s_wcopied = s("s_wload"), s("s_wT"), s("s_wcopied")
        s_pool, s_idle, s_small = s("s_pool"), s("s_idle"), s("s_small")
        block = ctx.enter_context(nc.Block())
        weights = [io["L0_gnn_W0"], io["L0_gnn_W1"], io["L1_gnn_W_self"], io["L1_gnn_W_msg"]]

        @block.gpsimd
        def _(pool):
            c = Chain(pool, s_pool)
            c.done(nc.gpsimd.memset(p.ident[:], 0.0))
            c.done(nc.gpsimd.memset(p.before[:], 1.0))
            c.done(nc.gpsimd.memset(p.upto[:], 1.0))
            c.done(nc.gpsimd.iota(p.iota[:], [[1, P]], base=0, channel_multiplier=0,
                                  allow_small_or_imprecise_dtypes=True))
            c.done(nc.gpsimd.iota(p.chunk_no[:], [[1, NCH]], base=0, channel_multiplier=0,
                                  allow_small_or_imprecise_dtypes=True))
            c.done(nc.gpsimd.iota(p.part_no[:], [[0, 1]], base=0, channel_multiplier=1,
                                  allow_small_or_imprecise_dtypes=True))
            c.done(nc.gpsimd.iota(p.node_no[:], [[P, NT]], base=0, channel_multiplier=1,
                                  allow_small_or_imprecise_dtypes=True))
            c.settle()
            nc.gpsimd.affine_select(out=p.ident[:], in_=p.ident[:], compare_op=ALU.not_equal, fill=1.0, base=0,
                                    pattern=[[-1, P]], channel_multiplier=1).then_inc(s_const, 1)
            nc.gpsimd.affine_select(out=p.before[:], in_=p.before[:], compare_op=ALU.is_gt, fill=0.0, base=0,
                                    pattern=[[1, P]], channel_multiplier=-1).then_inc(s_const, 1)
            nc.gpsimd.affine_select(out=p.upto[:], in_=p.upto[:], compare_op=ALU.is_ge, fill=0.0, base=0,
                                    pattern=[[1, P]], channel_multiplier=-1).then_inc(s_const, 1)
            pool.wait_ge(s_prefill, 32)
            ready = PoolWait(p, pool, s_idle)
            with pool.Fori(0, EC // SSTEP) as i:
                for h in range(SGROUPS):
                    ready(s_slot[h], 2 * i + 2, SGROUPS * i + h)
                    for u in range(h * SE, (h + 1) * SE):
                        pool.indirect_dma_start(
                            dram["table0"], bass.IndirectOffsetOnAxis(ap=slot_addr[:, u:u + 1], axis=0),
                            slot_rec[:, u:u + 1], None, bounds_check=P * QW - 1,
                            oob_is_err=False).then_inc(s_scat[h], 16)
            for h in range(SGROUPS):
                pool.wait_ge(s_scat[h], 16 * EC // SGROUPS)

        @block.scalar
        def _(act):
            for k in range(4):
                act.dma_start(wload[:, k, :, :], weights[k].rearrange("(b p) d -> p b d", p=P)).then_inc(s_wload, 16)
            for k in range(4):
                for kb in range(KB):
                    n = k * KB + kb
                    act.wait_ge(s_wT, n + 1)
                    nc.scalar.activation(p.wT[:, k, kb, :], psw[n % 2][:, 0:D], ACT.Copy).then_inc(s_wcopied, 1)

            def fill_slots(h, c0):
                slots = slice(h * SE, (h + 1) * SE)
                nc.scalar.activation(slot_addr[:, slots], addr[0][:, bass.ds(c0, SE)], ACT.Copy).then_inc(s_slot[h], 1)
                nc.scalar.activation(slot_rec[:, slots], rec[0][:, bass.ds(c0, SE)], ACT.Copy).then_inc(s_slot[h], 1)

            for n, (a, b_) in enumerate(PARTS):
                act.wait_ge(s_addr, n + 1)
                if n == 0:
                    for h in range(SGROUPS):
                        fill_slots(h, h * SE)
                with act.Fori(a // SSTEP + (n == 0), b_ // SSTEP) as i:
                    for h in range(SGROUPS):
                        act.wait_ge(s_scat[h], 16 * SE * i)
                        fill_slots(h, SSTEP * i + h * SE)
            norm.root(act)

        @block.sync
        def _(sp):
            sp.wait_ge(s_keyfill, 2)
            for k, (name, sem) in enumerate((("src", s_keys0), ("dst", s_keys1))):
                sp.dma_start(key[k][0:EROWS, :], io[name][0:EROWS * EC].rearrange("(p c) -> p c", c=EC)).then_inc(sem, 16)
                sp.dma_start(key[k][EROWS:EROWS + 1, 0:ETAIL],
                             io[name][EROWS * EC:E].rearrange("(a c) -> a c", a=1)).then_inc(sem, 16)
            sp.wait_ge(s_keyfill, 3)
            sp.dma_start(weight[0:EROWS, :], io["edge_weight"][0:EROWS * EC].rearrange("(p c) -> p c", c=EC)).then_inc(s_keys1, 16)
            sp.dma_start(weight[EROWS:EROWS + 1, 0:ETAIL],
                         io["edge_weight"][EROWS * EC:E].rearrange("(a c) -> a c", a=1)).then_inc(s_keys1, 16)
            sp.wait_ge(s_fill, 1)
            sp.dma_start(dram["table0"].rearrange("(p q) a -> p (q a)", p=P), fill[:, 0:QW]).then_inc(s_prefill, 16)
            sp.dma_start(dram["table1"].rearrange("(p q) a -> p (q a)", p=P), fill[:, :]).then_inc(s_prefill, 16)
            sp.wait_ge(s_xpad, 1)
            sp.dma_start(xb[:, 0:NT - 1, :], tiles(io["x"], 0, NT - 1)).then_inc(s_x, 16)
            sp.dma_start(xb[0:LAST, NT - 1, :], rows(io["x"], NT - 1, LAST)).then_inc(s_x, 16)
            sp.wait_ge(s_zero, 1)
            zeros = 0
            for name in ("moe_in", "moe_out", "mod_in", "mod_out"):
                flat = dram[name].rearrange("(g r) d -> g (r d)", r=4)
                total = flat.shape[0]
                first = 0 if name.endswith("in") else total - P // 4
                for g in range(first, total, P):
                    n = min(P, total - g)
                    sp.dma_start(flat[g:g + n, :], zero[0:n, :]).then_inc(s_zero, 16)
                    zeros += 1
            send_steps(sp, s_xn, dram["xn"], xb, s_xnout)
            sp.wait_ge(s_xnout, 16 * STEPS)
            small = 0
            with nc.allow_non_contiguous_dma("small parameters"):
                for dst, source in p.small:
                    sp.dma_start(dst, source).then_inc(s_small, 16)
                    small += 1
            sp.wait_ge(s_small, 16 * small)
            sp.wait_ge(s_zero, 1 + 16 * zeros)

        @block.tensor
        def _(pe):
            pe.wait_ge(s_const, 3)
            pe.wait_ge(s_wload, 64)
            for k in range(4):
                for kb in range(KB):
                    n = k * KB + kb
                    if n >= 2:
                        pe.wait_ge(s_wcopied, n - 1)
                    for jb in range(KB):
                        last = nc.tensor.transpose(psw[n % 2][:, jb * P:(jb + 1) * P],
                                                   wload[:, k, jb, kb * P:(kb + 1) * P], p.ident[:])
                    last.then_inc(s_wT, 1)
            for k in range(2):
                b.products(pe, k, count, b.s_count)

        @block.vector
        def _(dve):
            c = Chain(dve, s_dve)
            for k in range(2):
                nc.vector.memset(key[k][:], (NT + 14) * P).then_inc(s_keyfill, 1)
            nc.vector.memset(weight[:], 0.0).then_inc(s_keyfill, 1)
            nc.vector.memset(fill, NONE << KEYBITS).then_inc(s_fill, 1)
            nc.vector.memset(xb[:, NT - 1, :], 0.0).then_inc(s_xpad, 1)
            nc.vector.memset(zero, 0.0).then_inc(s_zero, 1)
            c.done(nc.vector.memset(p.ones[:], 1.0))
            c.done(nc.vector.memset(p.eps[:], EPS))
            c.done(nc.vector.memset(ones_row[:], 1.0))
            dve.wait_ge(s_keys0, 32)
            dve.wait_ge(s_keys1, 64)
            dve.wait_ge(s_const, 3)
            for k in range(2):
                mine, other = key[k], key[1 - k]
                c.done(nc.vector.tensor_single_scalar(win_i[:], mine[:], 7, ALU.arith_shift_right))
                c.done(nc.vector.tensor_scalar(local[:], mine[:], P - 1, KEYBITS, ALU.bitwise_and,
                                               ALU.logical_shift_left))
                c.done(nc.vector.memset(pos[:], 0.0))
                c.settle()
                c.done(nc.vector.tensor_copy(win[:], win_i[:]))
                c.link(nc.vector.tensor_tensor(rec[k][:], local[:], other[:], ALU.bitwise_or))
                with dve.Fori(0, STEPS) as i:
                    c.enter(i, U)
                    for u in range(U):
                        tile = bass.ds(U * i + u, 1)
                        if u > 1:
                            c.settle(but=1)
                        elif u == 0:
                            c.settle()
                        c.done(nc.vector.tensor_scalar(mask[:, u % 2, :], win[:], p.iota[:, tile], None, ALU.is_equal,
                                                       ALU.add, accum_out=count[:, tile]))
                c.leave(STEPS)
                c.settle()
                nc.vector.tensor_copy(b.count[:], count[:]).then_inc(b.s_count, 1)
                b.starts(dve, c, k, 7, P)
                for first, end in PARTS if k == 0 else ((0, EC),):
                    part = slice(first, end)
                    with dve.Fori(0, STEPS) as i:
                        c.enter(i, 5 * U)

                        def make_mask(u):
                            c.done(nc.vector.tensor_scalar(mask[:, u % 2, part], win[:, part],
                                                           p.iota[:, bass.ds(U * i + u, 1)], None, ALU.is_equal))

                        make_mask(0)
                        for u in range(U):
                            start = b.start[:, bass.ds(U * i + u, 1)]
                            c.settle()
                            c.done(nc.vector.tensor_tensor_scan(rank[:, u % 2, part], ones_row[:, part],
                                                                mask[:, u % 2, part], start, ALU.mult, ALU.add))
                            if u + 1 < U:
                                make_mask(u + 1)
                            if u:
                                c.done(nc.vector.tensor_tensor(pos[:, part], pos[:, part], product[:, (u - 1) % 2, part],
                                                               ALU.add))
                            c.settle(but=(u > 0) + (u + 1 < U))
                            c.done(nc.vector.tensor_scalar(start, rank[:, u % 2, end - 1:end], 0.0, None, ALU.add))
                            c.done(nc.vector.tensor_tensor(product[:, u % 2, part], rank[:, u % 2, part],
                                                           mask[:, u % 2, part], ALU.mult))
                        c.settle()
                        c.link(nc.vector.tensor_tensor(pos[:, part], pos[:, part], product[:, (U - 1) % 2, part],
                                                       ALU.add))
                    c.leave(STEPS)
                    c.link(nc.vector.tensor_scalar(rank[:, 0, part], win[:, part], float(NT), float(1 << 24), ALU.is_ge,
                                                   ALU.mult))
                    c.link(nc.vector.tensor_tensor(pos[:, part], pos[:, part], rank[:, 0, part], ALU.add))
                    c.link(nc.vector.tensor_copy(pos_i[:, part], pos[:, part]))
                    c.done(nc.vector.tensor_single_scalar(lane[:, part], pos_i[:, part], P - 1, ALU.bitwise_and))
                    c.link(nc.vector.tensor_single_scalar(win_i[:, part], pos_i[:, part], 7, ALU.arith_shift_right))
                    nc.vector.scalar_tensor_tensor(out=addr[k][:, part], in0=lane[:, part], scalar=float(QW),
                                                   in1=win_i[:, part], op0=ALU.mult, op1=ALU.add).then_inc(s_addr, 1)
                    dve.wait_ge(s_addr, len(PARTS) + 1 if k else PARTS.index((first, end)) + 1)
                b.table(dve, c, k, p.tile_of[k])
            dve.wait_ge(s_x, 32)
            with dve.Fori(0, STEPS) as i:
                for u in range(U):
                    norm.take(flat(xb[:, bass.ds(U * i + u, 1), :]), U * i + u).then_inc(s_dve, 1)
            c.n += NT
            c.settle()
            norm.finish(dve, c)
            norm.apply(dve, xb, xb, s_xn)


class RowNorm:

    def __init__(self, p, ctx):
        self.p = p
        tag = f"n{p.names}"
        p.names += 1
        self.stats = p.sb(tag + "stats", [P, NT, 6], F32, ctx)
        self.mean = p.sb(tag + "mean", [P, NT], F32, ctx)
        self.half = p.sb(tag + "half", [P, NT], F32, ctx)
        self.var = p.sb(tag + "var", [P, NT], F32, ctx)
        self.rstd = p.sb(tag + "rstd", [P, NT], F32, ctx)
        self.s_var = p.sem(tag + "s_var", ctx)
        self.s_std = p.sem(tag + "s_std", ctx)

    def take(self, row, t):
        return self.p.nc.vector.bn_stats(self.stats[:, bass.ds(t, 1), :].rearrange("p a s -> p (a s)"), row)

    def finish(self, dve, c):
        v, st = self.p.nc.vector, self.stats
        c.done(v.tensor_tensor(self.mean[:], st[:, :, 1], st[:, :, 4], ALU.add))
        c.done(v.tensor_tensor(self.half[:], st[:, :, 1], st[:, :, 4], ALU.subtract))
        c.done(v.tensor_tensor(self.var[:], st[:, :, 2], st[:, :, 5], ALU.add))
        c.settle()
        c.done(v.tensor_scalar(self.mean[:], self.mean[:], 0.5, None, ALU.mult))
        c.done(v.tensor_tensor(self.half[:], self.half[:], self.half[:], ALU.mult))
        c.done(v.tensor_scalar(self.var[:], self.var[:], 4.0 / D, None, ALU.mult))
        c.settle()
        c.link(v.tensor_tensor(self.var[:], self.var[:], self.half[:], ALU.add))
        v.tensor_scalar(self.var[:], self.var[:], 0.25, None, ALU.mult).then_inc(self.s_var, 1)
        dve.wait_ge(self.s_std, 1)
        c.link(v.reciprocal(self.rstd[:], self.rstd[:]))

    def apply(self, dve, buf, out, sem):
        with dve.Fori(0, STEPS) as i:
            for u in range(U):
                t = bass.ds(U * i + u, 1)
                self.p.nc.vector.tensor_scalar(flat(out[:, t, :]), flat(buf[:, t, 0:D]), self.mean[:, t],
                                               self.rstd[:, t], ALU.subtract, ALU.mult).then_inc(sem, 1)

    def root(self, act):
        act.wait_ge(self.s_var, 1)
        self.p.nc.scalar.activation(self.rstd[:], self.var[:], ACT.Sqrt, bias=self.p.eps[:, 0:1]).then_inc(self.s_std, 1)


def flat(ap):
    return ap.rearrange("p a d -> p (a d)")


def send_steps(sp, made, dram, buf, sem):
    with sp.Fori(0, STEPS) as i:
        sp.wait_ge(made, U * i + U)
        sp.dma_start(dram[bass.ds(P * U * i, P * U), :].rearrange("(t p) d -> p t d", p=P),
                     buf[:, bass.ds(U * i, U), 0:D]).then_inc(sem, 16)


class Binning:

    def __init__(self, p, ctx, bins, chunks):
        self.p, self.bins, self.chunks = p, bins, chunks
        tag = f"b{p.names}"
        p.names += 1
        self.count = p.sb(tag + "count", [P, bins], F32, ctx)
        self.start = p.sb(tag + "start", [P, bins], F32, ctx)
        self.total = p.sb(tag + "total", [P, 2 * bins + 2], F32, ctx)
        self.total_i = p.sb(tag + "total_i", [P, bins + 1], I32, ctx)
        self.full = p.sb(tag + "full", [P, bins + 1], F32, ctx)
        self.cum = p.sb(tag + "cum", [P, bins], F32, ctx)
        self.onesb = p.sb(tag + "onesb", [P, bins], F32, ctx)
        self.ended = p.sb(tag + "ended", [P, chunks], F32, ctx)
        self.ps = p.ps(tag + "ps", [P, 512], ctx)
        self.psrow = p.ps(tag + "psrow", [P, 1024], ctx)
        self.s_count = p.sem(tag + "s_count", ctx)
        self.s_sums = p.sem(tag + "s_sums", ctx)
        self.s_whole = p.sem(tag + "s_whole", ctx)
        self.s_cum = p.sem(tag + "s_cum", ctx)
        self.s_ended = p.sem(tag + "s_ended", ctx)
        self.s_row = p.sem(tag + "s_row", ctx)

    def products(self, pe, k, count, s_count):
        p, nc, B = self.p, self.p.nc, self.bins
        pe.wait_ge(s_count, k + 1)
        nc.tensor.matmul(self.ps[:, 0:B], p.before[:], self.count[:], start=True, stop=True)
        nc.tensor.matmul(self.ps[:, 64:64 + B], p.ones[:], self.count[:], start=True, stop=True)
        nc.tensor.matmul(self.ps[0:B, 128:129], self.count[:], p.ones[:, 0:1], start=True, stop=True).then_inc(self.s_sums, 1)
        pe.wait_ge(self.s_whole, k + 1)
        nc.tensor.matmul(self.ps[0:B, 192:193], p.upto[0:B, 0:B], self.full[0:B, B:B + 1],
                         start=True, stop=True).then_inc(self.s_cum, 1)
        pe.wait_ge(self.s_ended, k + 1)
        for a in range(0, self.chunks, 512):
            n = min(512, self.chunks - a)
            last = nc.tensor.matmul(self.psrow[0:1, a:a + n], p.ones[0:B, 0:1], self.ended[0:B, a:a + n],
                                    start=True, stop=True)
        last.then_inc(self.s_row, 1)

    def starts(self, dve, c, k, shift, chunk):
        p, nc, B = self.p, self.p.nc, self.bins
        c.done(nc.vector.memset(self.onesb[:], 1.0))
        c.done(nc.vector.memset(self.total[:], 0.0))
        c.settle()
        dve.wait_ge(self.s_sums, k + 1)
        c.done(nc.vector.tensor_copy(self.start[:], self.ps[:, 0:B]))
        c.done(nc.vector.tensor_scalar(self.total[:, 0:B], self.ps[:, 64:64 + B], float(chunk - 1), None, ALU.add))
        c.done(nc.vector.tensor_scalar(self.total[0:B, B:B + 1], self.ps[0:B, 128:129], float(chunk - 1), None, ALU.add))
        c.settle()
        c.link(nc.vector.tensor_copy(self.total_i[:], self.total[:, 0:B + 1]))
        c.link(nc.vector.tensor_single_scalar(self.total_i[:], self.total_i[:], shift, ALU.arith_shift_right))
        c.link(nc.vector.tensor_copy(self.full[:], self.total_i[:]))
        nc.vector.tensor_tensor_scan(self.cum[:], self.onesb[:], self.full[:, 0:B], 0.0,
                                     ALU.mult, ALU.add).then_inc(self.s_whole, 1)
        dve.wait_ge(self.s_whole, k + 1)
        c.link(nc.vector.tensor_tensor(self.cum[:], self.cum[:], self.full[:, 0:B], ALU.subtract))
        c.link(nc.vector.tensor_scalar(self.cum[:], self.cum[:], float(chunk), -1.0, ALU.mult, ALU.add))
        c.link(nc.vector.tensor_tensor(self.start[:], self.start[:], self.cum[:], ALU.add))

    def table(self, dve, c, k, row):
        p, nc, B, M = self.p, self.p.nc, self.bins, self.chunks
        dve.wait_ge(self.s_cum, k + 1)
        c.link(nc.vector.tensor_copy(self.total[0:B, B + 1:B + 2], self.ps[0:B, 192:193]))
        nc.vector.tensor_scalar(self.ended[0:B, :], p.chunk_no[0:B, 0:M], self.total[0:B, B + 1:B + 2], None,
                                ALU.is_ge).then_inc(self.s_ended, 1)
        dve.wait_ge(self.s_row, k + 1)
        c.link(nc.vector.tensor_scalar(row[0:1, 0:M], self.psrow[0:1, 0:M], float(B - 1), None, ALU.min))



def unpack_table(p, table, fields):
    nc = p.nc
    with ExitStack() as ctx:
        raw = p.sb(f"raw{fields}", [P, QW, fields], I32, ctx)
        loc_i = p.sb(f"loc_i{fields}", [P, QW], I32, ctx)
        s_raw, s_dve = p.sem("s_raw", ctx), p.sem("s_dve", ctx)
        block = ctx.enter_context(nc.Block())

        @block.sync
        def _(sp):
            sp.dma_start(raw[:], table.rearrange("(p q) a -> p q a", p=P)).then_inc(s_raw, 16)

        @block.vector
        def _(dve):
            c = Chain(dve, s_dve)
            dve.wait_ge(s_raw, 16)
            c.done(nc.vector.tensor_single_scalar(p.edge_row[:], raw[:, :, 0], (1 << KEYBITS) - 1, ALU.bitwise_and))
            c.done(nc.vector.tensor_single_scalar(loc_i[:], raw[:, :, 0], KEYBITS, ALU.arith_shift_right))
            if fields == 2:
                c.done(nc.vector.tensor_copy(p.edge_weight[:], raw[:, :, 1].bitcast(F32)))
            c.settle()
            c.link(nc.vector.tensor_copy(p.edge_local[:], loc_i[:]))


def sum_over_edges(p, source, order, weighted):
    nc = p.nc
    with ExitStack() as ctx:
        row_slot = p.sb("row_slot", [P, SU], I32, ctx)
        got = p.sb("got", [P, SU, D + 1], F32, ctx)
        onehot = p.sb("onehot", [P, 4, P], F32, ctx)
        sums = [p.ps(f"sums{i}", [P, 512], ctx) for i in range(4)]
        s = lambda name: p.sem(name, ctx)
        s_rows = [s(f"s_rows{h}") for h in range(GROUPS)]
        s_got = [s(f"s_got{h}") for h in range(GROUPS)]
        s_idle, s_ready, s_onehot, s_sum, s_added = s("s_idle"), s("s_ready"), s("s_onehot"), s("s_sum"), s("s_added")
        block = ctx.enter_context(nc.Block())
        STEPE = NCH // SU

        @block.scalar
        def _(act):
            def fill(h, c0):
                nc.scalar.activation(row_slot[:, h * EU:(h + 1) * EU], p.edge_row[:, bass.ds(c0, EU)],
                                     ACT.Copy).then_inc(s_rows[h], 1)
            for h in range(GROUPS):
                fill(h, h * EU)
            with act.Fori(0, STEPE) as i:
                for h in range(GROUPS):
                    act.wait_ge(s_sum, SU * i + (h + 1) * EU)
                    fill(h, SU * i + SU + h * EU)

        @block.gpsimd
        def _(pool):
            pool.wait_ge(s_ready, 2)
            ready = PoolWait(p, pool, s_idle)
            with pool.Fori(0, STEPE) as i:
                for h in range(GROUPS):
                    ready(s_rows[h], i + 1, GROUPS * i + h)
                    for u in range(h * EU, (h + 1) * EU):
                        pool.indirect_dma_start(
                            got[:, u, 0:D], None, source,
                            bass.IndirectOffsetOnAxis(ap=row_slot[:, u:u + 1], axis=0)).then_inc(s_got[h], 16)

        @block.tensor
        def _(pe):
            pe.wait_ge(s_ready, 2)
            with pe.Fori(0, STEPE) as i:
                for h in range(GROUPS):
                    pe.wait_ge(s_got[h], 16 * EU * i + 16 * EU)
                    for u in range(EU):
                        n = h * EU + u
                        pe.wait_ge(s_onehot, SU * i + n + 1)
                        pe.wait_ge(s_added, SU * i + n + 1)
                        nc.tensor.matmul(sums[n % 4][:, 0:D + 1], onehot[:, n % 4, :], got[:, n, :],
                                         start=True, stop=True).then_inc(s_sum, 1)

        @block.vector
        def _(dve):
            nc.vector.memset(got[:], 1.0).then_inc(s_ready, 1)
            nc.vector.memset(p.acc[:], 0.0).then_inc(s_ready, 1)
            dve.wait_ge(s_ready, 2)
            for _i in range(4):
                nc.vector.memset(onehot[:, _i, 0:1], 0.0).then_inc(s_added, 1)
            dve.wait_ge(s_added, 4)

            def build(n, c):
                if weighted:
                    ins = nc.vector.tensor_scalar(onehot[:, n % 4, :], p.iota[:], p.edge_local[:, bass.ds(c, 1)],
                                                  p.edge_weight[:, bass.ds(c, 1)], ALU.is_equal, ALU.mult)
                else:
                    ins = nc.vector.tensor_scalar(onehot[:, n % 4, :], p.iota[:], p.edge_local[:, bass.ds(c, 1)],
                                                  None, ALU.is_equal)
                ins.then_inc(s_onehot, 1)

            build(0, 0)
            build(1, 1)
            with dve.Fori(0, STEPE) as i:
                for n in range(SU):
                    if n % EU == 0:
                        _, tile_regs = nc.values_load_multi_w_load_instructions(
                            p.tile_of[order][0:1, bass.ds(SU * i + n, EU)], (mybir.EngineType.DVE,), min_val=0,
                            max_val=NT - 1)
                    build(n + 2, SU * i + n + 2)
                    dve.wait_ge(s_sum, SU * i + n + 1)
                    dve.wait_ge(s_added, SU * i + n + 4)
                    a = p.acc[:, bass.ds(tile_regs[n % EU], 1), :].rearrange("p a d -> p (a d)")
                    nc.vector.tensor_tensor(a, a, sums[n % 4][:, 0:D + 1], ALU.add).then_inc(s_added, 1)



BANK = [0, 1, 2, 0, 1, 2, 3]


class Project:

    def __init__(self, p, ctx, rhs, cols, put, take, then):
        self.p, self.rhs, self.cols, self.put, self.take, self.then = p, rhs, cols, put, take, then
        n = len(rhs)
        self.slots = p.sb("pr_rows", [P, U, n, D], F32, ctx)
        self.flip = p.sb("pr_flip", [P, U, n * D], F32, ctx)
        self.spare = p.sb("pr_spare", [P, 6], F32, ctx)
        self.ps_flip = [p.ps(f"pr_psflip{i}", [P, 512], ctx) for i in range(4)]
        self.ps_out = [p.ps(f"pr_psout{i}", [P, 512], ctx) for i in range(4)]
        self.s_put, self.s_flip, self.s_copied, self.s_out, self.s_taken = (
            p.sem(f"pr_{x}", ctx) for x in ("s_put", "s_flip", "s_copied", "s_out", "s_taken"))

    def steps(self, eng, tile):
        with eng.Fori(0, STEPS - 1) as i:
            self.i = i
            for u in range(U):
                tile(U * i + u, u, U)
        self.i = STEPS - 1
        for u in range(U):
            tile(U * (STEPS - 1) + u, u, U - 1 - u)

    PUT, FLIP = 4, 2

    def dve(self, dve, c):
        p, n = self.p, len(self.rhs)
        follows = self.then is not None

        def put(t, u):
            for ins in self.put(t, [self.slots[:, u, k, :] for k in range(n)]):
                ins.then_inc(self.s_put, 1)

        for k in range(3):
            p.nc.vector.memset(self.spare[:, k:k + 1], 0.0).then_inc(self.s_taken, 1)
        for t in range(self.PUT):
            put(t, t)

        def tile(t, u, more):
            if u == 0 and follows:
                if isinstance(self.i, int):
                    c.leave(STEPS - 1)
                else:
                    c.enter(self.i, U)
            dve.wait_ge(self.s_out, t + 1)
            self.take(t, self.ps_out[BANK[u]]).then_inc(self.s_taken, 1)
            if more >= self.PUT:
                put(t + self.PUT, (u + self.PUT) % U)
            if follows:
                dve.wait_ge(self.s_taken, t + 4)
                c.done(self.then(t))

        self.steps(dve, tile)
        c.settle()
        dve.wait_ge(self.s_taken, NT + 3)

    def pe(self, pe):
        nc, n = self.p.nc, len(self.rhs)

        def flip(t, u):
            pe.wait_ge(self.s_put, n * t + n)
            pe.wait_ge(self.s_copied, t + 1)
            for k in range(n):
                for kb in range(KB):
                    last = nc.tensor.transpose(self.ps_flip[BANK[u]][:, (k * KB + kb) * P:(k * KB + kb + 1) * P],
                                               self.slots[:, u, k, kb * P:(kb + 1) * P], self.p.ident[:])
            last.then_inc(self.s_flip, 1)

        for t in range(self.FLIP):
            flip(t, t)

        def tile(t, u, more):
            if more >= self.FLIP:
                flip(t + self.FLIP, (u + self.FLIP) % U)
            pe.wait_ge(self.s_copied, t + 4)
            pe.wait_ge(self.s_taken, t + 1)
            for k in range(n):
                for kb in range(KB):
                    last = nc.tensor.matmul(self.ps_out[BANK[u]][:, 0:self.cols],
                                            self.flip[:, u, (k * KB + kb) * P:(k * KB + kb + 1) * P],
                                            self.rhs[k][kb], start=(k + kb == 0), stop=(k == n - 1 and kb == KB - 1))
            last.then_inc(self.s_out, 1)

        self.steps(pe, tile)

    def act(self, act):
        nc, n = self.p.nc, len(self.rhs)
        for k in range(3):
            nc.scalar.activation(self.spare[:, 3 + k:4 + k], self.p.eps[:], ACT.Copy).then_inc(self.s_copied, 1)

        def tile(t, u, more):
            act.wait_ge(self.s_flip, t + 1)
            nc.scalar.activation(self.flip[:, u, :], self.ps_flip[BANK[u]][:, 0:n * D], ACT.Copy).then_inc(self.s_copied, 1)

        self.steps(act, tile)


class SecondScatter:

    def __init__(self, p, ctx, first, end):
        self.p, self.first, self.end = p, first, end
        self.addr = p.sb("sc_addr", [P, SSTEP], I32, ctx)
        self.rec = p.sb("sc_rec", [P, SSTEP, 2], I32, ctx)
        self.s_idle = p.sem("sc_s_idle", ctx)
        self.s_slot = [p.sem(f"sc_s_slot{h}", ctx) for h in range(SGROUPS)]
        self.s_sent = [p.sem(f"sc_s_sent{h}", ctx) for h in range(SGROUPS)]

    def run(self, pool):
        p = self.p
        ready = PoolWait(p, pool, self.s_idle)

        def fill(h, step):
            slots, columns = slice(h * SE, (h + 1) * SE), bass.ds(SSTEP * step + h * SE, SE)
            for out, value in ((self.addr[:, slots], p.addr1[:, columns]),
                               (self.rec[:, slots, 0], p.rec1[:, columns]),
                               (self.rec[:, slots, 1].bitcast(F32), p.weight1[:, columns])):
                p.nc.gpsimd.tensor_copy(out, value).then_inc(self.s_slot[h], 1)

        def send(h):
            for u in range(h * SE, (h + 1) * SE):
                pool.indirect_dma_start(p.table1, bass.IndirectOffsetOnAxis(ap=self.addr[:, u:u + 1], axis=0),
                                        self.rec[:, u, :], None, bounds_check=P * QW - 1,
                                        oob_is_err=False).then_inc(self.s_sent[h], 16)

        for h in range(SGROUPS):
            fill(h, self.first)
            pool.wait_ge(self.s_slot[h], 3)
            send(h)
        with pool.Fori(0, self.end - self.first - 1) as i:
            for h in range(SGROUPS):
                ready(self.s_sent[h], 16 * SE * i + 16 * SE, 2 * (SGROUPS * i + h))
                pool.wait_ge(self.s_idle, 2 * (SGROUPS * i + h) + 2)
                fill(h, self.first + 1 + i)
                ready(self.s_slot[h], 3 * i + 6, 2 * (SGROUPS * i + h) + 1)
                send(h)
        for h in range(SGROUPS):
            pool.wait_ge(self.s_sent[h], 16 * SE * (self.end - self.first))


def gnn_dense(p, wk, biases, gamma, beta, func, residual, copy, scatters):
    nc, v = p.nc, p.nc.vector
    mean_of_edges = len(wk) == 1
    with ExitStack() as ctx:
        bias = p.sb("g_bias", [P, D], F32, ctx)
        deg = p.sb("g_deg", [P, NT], F32, ctx)
        norm, norm2 = RowNorm(p, ctx), RowNorm(p, ctx)

        def put(t, slots):
            a, x = flat(p.acc[:, bass.ds(t, 1), 0:D]), flat(p.xb[:, bass.ds(t, 1), :])
            if mean_of_edges:
                return [v.scalar_tensor_tensor(out=slots[0], in0=a, scalar=deg[:, bass.ds(t, 1)], in1=x,
                                               op0=ALU.mult, op1=ALU.add)]
            return [v.tensor_copy(slots[0], x), v.tensor_copy(slots[1], a)]

        def take(t, psum):
            return v.tensor_tensor(flat(p.acc[:, bass.ds(t, 1), 0:D]), psum[:, 0:D], bias[:], ALU.add)

        def then(t):
            return norm.take(flat(p.acc[:, bass.ds(t, 1), 0:D]), t)

        pr = Project(p, ctx, [[p.wT[:, k, kb, :] for kb in range(KB)] for k in wk], D, put, take, then)
        old, scaled = pr.slots[:, :, 0, :], pr.flip[:, :, 0:D]
        if len(wk) == 2:
            active, centered = pr.slots[:, :, 1, :], pr.flip[:, :, D:2 * D]
        else:
            active, centered = p.sb("g_active", [P, U, D], F32, ctx), p.sb("g_centered", [P, U, D], F32, ctx)
        s = lambda name: p.sem("g_" + name, ctx)
        s_dve, s_scaled, s_active = s("s_dve"), s("s_scaled"), s("s_active")
        s_summed, s_centered, s_applied, s_copy = s("s_summed"), s("s_centered"), s("s_applied"), s("s_copy")
        s_old = [s(f"s_old{u}") for u in range(U)]
        if scatters is not None:
            scatter = SecondScatter(p, ctx, *scatters)
        block = ctx.enter_context(nc.Block())

        @block.vector
        def _(dve):
            c = Chain(dve, s_dve)
            if mean_of_edges:
                c.link(v.tensor_scalar(deg[:], p.acc[:, :, D], 1.0, None, ALU.max))
                c.link(v.reciprocal(deg[:], deg[:]))
            if len(biases) == 2:
                c.link(v.tensor_tensor(bias[:], biases[0][:], biases[1][:], ALU.add))
            else:
                c.link(v.tensor_copy(bias[:], biases[0][:]))
            pr.dve(dve, c)
            norm.finish(dve, c)

            def center(t, u):
                v.scalar_tensor_tensor(out=centered[:, u, :], in0=flat(p.acc[:, bass.ds(t, 1), 0:D]),
                                       scalar=norm.mean[:, bass.ds(t, 1)], in1=gamma[:], op0=ALU.subtract,
                                       op1=ALU.mult).then_inc(s_centered, 1)

            def scale(t, u):
                dve.wait_ge(s_centered, t + 1)
                v.scalar_tensor_tensor(out=scaled[:, u, :], in0=centered[:, u, :], scalar=norm.rstd[:, bass.ds(t, 1)],
                                       in1=beta[:], op0=ALU.mult, op1=ALU.add).then_inc(s_scaled, 1)

            center(0, 0)
            center(1, 1)
            scale(0, 0)

            def tile(t, u, more):
                x = flat(p.acc[:, bass.ds(t, 1), 0:D])
                if more >= 1:
                    scale(t + 1, (u + 1) % U)
                dve.wait_ge(s_active, t + 1)
                if residual is not None:
                    dve.wait_ge(s_old[u], 16 * pr.i + 16)
                    v.tensor_tensor(x, active[:, u, :], old[:, u, :], ALU.add).then_inc(s_summed, 1)
                if more >= 2:
                    center(t + 2, (u + 2) % U)
                if residual is not None:
                    dve.wait_ge(s_summed, t + 1)
                    if u == 0:
                        if isinstance(pr.i, int):
                            c.leave(STEPS - 1)
                        else:
                            c.enter(pr.i, U)
                    c.done(norm2.take(x, t))

            pr.steps(dve, tile)
            if residual is not None:
                c.settle()
                norm2.finish(dve, c)
                norm2.apply(dve, p.acc, p.xb, s_applied)

        @block.tensor
        def _(pe):
            pr.pe(pe)

        @block.scalar
        def _(act):
            pr.act(act)
            norm.root(act)
            with act.Fori(0, STEPS) as i:
                for u in range(U):
                    act.wait_ge(s_scaled, U * i + u + 1)
                    out = flat(p.xb[:, bass.ds(U * i + u, 1), :]) if residual is None else active[:, u, :]
                    nc.scalar.activation(out, scaled[:, u, :], func).then_inc(s_active, 1)
            if residual is not None:
                norm2.root(act)

        if scatters is not None:
            @block.gpsimd
            def _(pool):
                scatter.run(pool)

        if residual is None:
            @block.sync
            def _(sp):
                send_steps(sp, s_active, copy, p.xb, s_copy)
                sp.wait_ge(s_copy, 16 * STEPS)
        else:
            @block.sync
            def _(sp):
                sp.wait_ge(pr.s_taken, NT + 3)
                for u in range(U):
                    sp.dma_start(old[:, u, :], rows(residual, u)).then_inc(s_old[u], 16)
                with sp.Fori(0, STEPS - 2) as i:
                    for u in range(U):
                        sp.wait_ge(s_summed, U * i + u + 1)
                        sp.dma_start(old[:, u, :], residual[bass.ds(P * (U * i + U + u), P), :]).then_inc(s_old[u], 16)
                for u in range(U):
                    t = U * (STEPS - 1) + u
                    n = LAST if t == NT - 1 else P
                    sp.wait_ge(s_summed, t - U + 1)
                    sp.dma_start(old[0:n, u, :], rows(residual, t, n)).then_inc(s_old[u], 16)



def route_to_experts(p):
    nc, v = p.nc, p.nc.vector
    with ExitStack() as outer:
        logits = p.sb("r_logits", [P, NT, EX], F32, outer)
        with ExitStack() as ctx:
            def put(t, slots):
                return [v.tensor_copy(slots[0], flat(p.xb[:, bass.ds(t, 1), :]))]

            def take(t, psum):
                return v.tensor_tensor(flat(logits[:, bass.ds(t, 1), :]), psum[:, 0:EX], p.br[:], ALU.add)

            def then(t):
                return p.norm_in.take(flat(p.xb[:, bass.ds(t, 1), :]), t)

            pr = Project(p, ctx, [[p.Wr[:, kb, :] for kb in range(KB)]], EX, put, take, then)
            s_dve = p.sem("r_s_dve", ctx)
            block = ctx.enter_context(nc.Block())

            @block.vector
            def _(dve):
                c = Chain(dve, s_dve)
                pr.dve(dve, c)
                p.norm_in.finish(dve, c)

            @block.tensor
            def _(pe):
                pr.pe(pe)

            @block.scalar
            def _(act):
                pr.act(act)
                p.norm_in.root(act)

        with ExitStack() as ctx:
            names = ("expert", "cap", "rest", "hot0", "hot1", "tmp", "place")
            expert, cap, rest, hot0, hot1, tmp, place = (p.sb("r_" + n, [P, NT, EX], F32, ctx) for n in names)
            top = [p.sb(f"r_top{k}", [P, NT], F32, ctx) for k in range(TOP)]
            first = p.sb("r_first", [P, NT], F32, ctx)
            gap = p.sb("r_gap", [P, NT], F32, ctx)
            past, valid, where = (p.sb("r_" + n, [P, NT], F32, ctx) for n in ("past", "valid", "where"))
            ones = p.sb("r_ones", [P, NT], F32, ctx)
            b = Binning(p, ctx, EX, MOE_TILES)
            s_dve, s_gap, s_exp = (p.sem("r2_" + n, ctx) for n in ("s_dve", "s_gap", "s_exp"))
            block = ctx.enter_context(nc.Block())

            def wide(ap):
                return ap.unsqueeze(2).to_broadcast([P, NT, EX])

            @block.tensor
            def _(pe):
                b.products(pe, 0, None, b.s_count)

            @block.scalar
            def _(act):
                act.wait_ge(s_gap, 1)
                nc.scalar.activation(gap[:], gap[:], ACT.Exp).then_inc(s_exp, 1)

            @block.vector
            def _(dve):
                c = Chain(dve, s_dve)
                c.link(v.tensor_scalar(expert[:, 0, :], p.iota[:, 0:EX], -float(EX), None, ALU.add))
                c.link(v.tensor_copy(expert[:, 1:NT, :], expert[:, 0:1, :].to_broadcast([P, NT - 1, EX])))
                c.done(v.memset(ones[:], 1.0))
                c.done(v.memset(p.place_i[:], 0))
                c.done(v.tensor_scalar(valid[:], p.node_no[:], float(N), None, ALU.is_lt))
                c.done(v.tensor_scalar(past[:], p.node_no[:], float(N), None, ALU.is_ge))
                c.done(v.tensor_scalar(gap[:, 0:1], p.part_no[:], float(MOE_TILES * FT), None, ALU.add))
                c.settle()
                c.link(v.tensor_scalar(past[:], past[:], gap[:, 0:1], None, ALU.mult))
                values = logits
                for k, hot in enumerate((hot0, hot1)):
                    c.link(v.tensor_reduce(top[k][:], values[:], AX, ALU.max))
                    c.link(v.tensor_tensor(tmp[:], values[:], wide(top[k][:]), ALU.is_equal))
                    c.link(v.tensor_tensor(tmp[:], tmp[:], expert[:], ALU.mult))
                    c.link(v.tensor_reduce(first[:], tmp[:], AX, ALU.min))
                    c.link(v.tensor_tensor(hot[:], expert[:], wide(first[:]), ALU.is_equal))
                    if k == 0:
                        c.link(v.tensor_scalar(cap[:], hot[:], -2.0, 1.0, ALU.mult, ALU.add))
                        c.link(v.tensor_scalar(cap[:], cap[:], 3.0e38, None, ALU.mult))
                        c.link(v.tensor_tensor(rest[:], logits[:], cap[:], ALU.min))
                        values = rest
                v.tensor_tensor(gap[:], top[1][:], top[0][:], ALU.subtract).then_inc(s_gap, 1)
                for hot in (hot0, hot1):
                    c.done(v.tensor_tensor(hot[:], hot[:], wide(valid[:]), ALU.mult))
                c.settle()
                c.link(v.tensor_tensor(tmp[:], hot0[:], hot1[:], ALU.add))
                v.tensor_reduce(b.count[:], tmp[:].rearrange("p t e -> p e t"), AX, ALU.add).then_inc(b.s_count, 1)
                b.starts(dve, c, 0, 8, FT)
                for e in range(EX):
                    c.done(v.tensor_tensor_scan(place[:, :, e], ones[:], tmp[:, :, e], b.start[:, e:e + 1],
                                                ALU.mult, ALU.add))
                c.settle()
                for k, hot in enumerate((hot0, hot1)):
                    c.link(v.tensor_tensor(tmp[:], hot[:], place[:], ALU.mult))
                    c.link(v.tensor_reduce(where[:], tmp[:], AX, ALU.add))
                    c.link(v.tensor_tensor(where[:], where[:], past[:], ALU.add))
                    c.link(v.tensor_copy(p.place_i[:, k, 0:NT], where[:]))
                b.table(dve, c, 0, p.expert_of)
                dve.wait_ge(s_exp, 1)
                c.link(v.tensor_scalar(p.share[:, 0, :], gap[:], 1.0, None, ALU.add))
                c.link(v.reciprocal(p.share[:, 0, :], p.share[:, 0, :]))
                c.link(v.tensor_tensor(p.share[:, 1, :], gap[:], p.share[:, 0, :], ALU.mult))


def dispatch(p, into, places, choices, normed):
    nc, v = p.nc, p.nc.vector
    with ExitStack() as ctx:
        row = p.sb("d_row", [P, U, D], F32, ctx)
        slot = p.sb("d_slot", [P, U, TOP], I32, ctx)
        s = lambda name: p.sem("d_" + name, ctx)
        s_idle, s_start = s("s_idle"), s("s_start")
        s_full = [s(f"s_full{u}") for u in range(U)]
        s_sent = [s(f"s_sent{u}") for u in range(U)]
        block = ctx.enter_context(nc.Block())

        @block.vector
        def _(dve):
            def fill(t, u):
                x = flat(p.xb[:, bass.ds(t, 1), :])
                if normed:
                    v.tensor_scalar(row[:, u, :], x, p.norm_in.mean[:, bass.ds(t, 1)],
                                    p.norm_in.rstd[:, bass.ds(t, 1)], ALU.subtract, ALU.mult).then_inc(s_full[u], 1)
                else:
                    v.tensor_copy(row[:, u, :], x).then_inc(s_full[u], 1)
                for k in range(choices):
                    v.tensor_copy(slot[:, u, k:k + 1], p.place_i[:, k, bass.ds(t, 1)]).then_inc(s_full[u], 1)

            for u in range(U):
                fill(u, u)
            with dve.Fori(0, STEPS - 1) as i:
                for u in range(U):
                    dve.wait_ge(s_sent[u], 16 * choices * i + 16 * choices)
                    fill(U * i + U + u, u)

        @block.gpsimd
        def _(pool):
            ready = PoolWait(p, pool, s_idle)
            with pool.Fori(0, STEPS) as i:
                for u in range(U):
                    ready(s_full[u], (choices + 1) * i + choices + 1, U * i + u)
                    for k in range(choices):
                        pool.indirect_dma_start(into[0:places, :], bass.IndirectOffsetOnAxis(ap=slot[:, u, k:k + 1], axis=0),
                                                row[:, u, :], None, bounds_check=places - 1,
                                                oob_is_err=False).then_inc(s_sent[u], 16)
            for u in range(U):
                pool.wait_ge(s_sent[u], 16 * choices * STEPS)


def combine(p, source, choices, add_xb, share, norm, sent, normed, last):
    nc, v = p.nc, p.nc.vector
    with ExitStack() as ctx:
        got = p.sb("c_got", [P, U, TOP, D], F32, ctx)
        slot = p.sb("c_slot", [P, U, TOP], I32, ctx)
        s = lambda name: p.sem("c_" + name, ctx)
        s_idle, s_dve, s_applied, s_sent = s("s_idle"), s("s_dve"), s("s_applied"), s("s_sent")
        per_tile = choices + int(add_xb) + int(norm is not None)
        s_slot = [s(f"s_slot{u}") for u in range(U)]
        s_got = [s(f"s_got{u}") for u in range(U)]
        block = ctx.enter_context(nc.Block())

        @block.vector
        def _(dve):
            c = Chain(dve, s_dve)

            def fill(t, u):
                for k in range(choices):
                    v.tensor_copy(slot[:, u, k:k + 1], p.place_i[:, k, bass.ds(t, 1)]).then_inc(s_slot[u], 1)

            for u in range(U):
                fill(u, u)
            with dve.Fori(0, STEPS) as i:
                c.enter(i, U * per_tile)
                for u in range(U):
                    t = U * i + u
                    x = flat(p.acc[:, bass.ds(t, 1), 0:D])
                    if add_xb:
                        c.link(v.tensor_tensor(x, x, flat(p.xb[:, bass.ds(t, 1), :]), ALU.add))
                    dve.wait_ge(s_got[u], 16 * choices * i + 16 * choices)
                    for k in range(choices - 1):
                        c.link(v.scalar_tensor_tensor(out=x, in0=got[:, u, k, :], scalar=share[:, k, bass.ds(t, 1)],
                                                      in1=x, op0=ALU.mult, op1=ALU.add))
                    k = choices - 1
                    c.done(v.scalar_tensor_tensor(out=x, in0=got[:, u, k, :], scalar=share[:, k, bass.ds(t, 1)],
                                                  in1=x, op0=ALU.mult, op1=ALU.add))
                    c.settle()
                    fill(t + U, u)
                    if norm is not None:
                        c.done(norm.take(x, t))
            c.leave(STEPS)
            if norm is not None:
                c.settle()
                norm.finish(dve, c)
                norm.apply(dve, p.acc, p.xb, s_applied)

        @block.sync
        def _(sp):
            done_per = U * per_tile
            with sp.Fori(0, STEPS - 1) as i:
                sp.wait_ge(s_dve, done_per * i + done_per)
                sp.dma_start(sent[bass.ds(P * U * i, P * U), :].rearrange("(t p) d -> p t d", p=P),
                             p.acc[:, bass.ds(U * i, U), 0:D]).then_inc(s_sent, 16)
            sp.wait_ge(s_dve, done_per * STEPS)
            first = U * (STEPS - 1)
            sp.dma_start(tiles(sent, first, NT - 1), p.acc[:, first:NT - 1, 0:D]).then_inc(s_sent, 16)
            sp.dma_start(rows(sent, NT - 1, last), p.acc[0:last, NT - 1, 0:D]).then_inc(s_sent, 16)
            sends = STEPS + 1
            if norm is not None:
                send_steps(sp, s_applied, normed, p.xb, s_sent)
                sends += STEPS
            sp.wait_ge(s_sent, 16 * sends)

        @block.gpsimd
        def _(pool):
            ready = PoolWait(p, pool, s_idle)
            with pool.Fori(0, STEPS) as i:
                for u in range(U):
                    ready(s_slot[u], choices * i + choices, U * i + u)
                    for k in range(choices):
                        pool.indirect_dma_start(got[:, u, k, :], None, source,
                                                bass.IndirectOffsetOnAxis(ap=slot[:, u, k:k + 1], axis=0)).then_inc(s_got[u], 16)

        if norm is not None:
            @block.scalar
            def _(act):
                norm.root(act)



def ffn(p, source, result, count, weights, experts, func, scatters):
    nc, v = p.nc, p.nc.vector
    W1, W2, b1, b2 = weights
    with ExitStack() as ctx:
        wslots = 2 if experts else 1
        size = wslots * KB * H
        if experts:
            room = p.xb[:].rearrange("p t d -> p (t d)")
        else:
            room = p.sb("f_weights", [P, 2 * size], F32, ctx)
        w1 = room[:, 0:size].rearrange("p (s b h) -> p s b h", s=wslots, b=KB)
        w2 = room[:, size:2 * size].rearrange("p (s b d) -> p s b d", s=wslots, b=HB)
        xin = p.sb("f_xin", [P, 2, 2, D], F32, ctx)
        xT = p.sb("f_xT", [P, KB, FT], F32, ctx)
        hT = p.sb("f_hT", [P, 2, HB, FT], F32, ctx)
        y = p.sb("f_y", [P, 2, 2, D], F32, ctx)
        ps_x = p.ps("f_ps_x", [P, KB, FT], ctx)
        ps_h = [p.ps(f"f_ps_h{i}", [P, 512], ctx) for i in range(4)]
        ps_y = [p.ps(f"f_ps_y{i}", [P, 512], ctx) for i in range(2)]
        s = lambda name: p.sem("f_" + name, ctx)
        s_x = [s(f"s_x{i}") for i in range(2)]
        s_w = [s(f"s_w{i}") for i in range(2)]
        s_out = [s(f"s_out{i}") for i in range(2)]
        s_flip, s_xT, s_up, s_act, s_down, s_y = (s(n) for n in ("s_flip", "s_xT", "s_up", "s_act", "s_down", "s_y"))
        if scatters is not None:
            scatter = SecondScatter(p, ctx, *scatters)
        block = ctx.enter_context(nc.Block())
        pairs = (count - 3) // 2
        rest = count - 2 - 2 * pairs

        def over_tiles(eng, tile):
            for t in range(2):
                tile(t, t, 0, t == 0, False)
            with eng.Fori(0, pairs) as i:
                for k in range(2):
                    tile(2 * i + 2 + k, k, i + 1, False, False)
            for t in range(count - rest, count):
                tile(t, t % 2, t // 2, False, t == count - 1)

        def expert(eng, t):
            return eng.value_load(p.expert_of[0:1, bass.ds(t, 1)], min_val=0, max_val=EX - 1)

        @block.sync
        def _(sp):
            x_dram = source.rearrange("(t p c) d -> t p c d", p=P, c=2)
            y_dram = result[0:count * FT, :].rearrange("(t p c) d -> t p c d", p=P, c=2)

            def at(ap, t):
                return ap[bass.ds(t, 1)].rearrange("a p c d -> (a p) c d")

            def load(t, k):
                sp.dma_start(xin[:, k, :, :], at(x_dram, t)).then_inc(s_x[k], 16)
                if experts:
                    e = expert(sp, t)
                    sp.dma_start(w1[:, k, :, :], W1[bass.ds(e, 1)].rearrange("a (b p) h -> (a p) b h", p=P)).then_inc(s_w[k], 16)
                    sp.dma_start(w2[:, k, :, :], W2[bass.ds(e, 1)].rearrange("a (b p) d -> (a p) b d", p=P)).then_inc(s_w[k], 16)

            if not experts:
                sp.dma_start(w1[:, 0, :, :], W1.rearrange("(b p) h -> p b h", p=P)).then_inc(s_w[0], 16)
                sp.dma_start(w2[:, 0, :, :], W2.rearrange("(b p) d -> p b d", p=P)).then_inc(s_w[0], 16)
            load(0, 0)
            load(1, 1)

            def tile(t, k, uses, first, last, more=True):
                sp.wait_ge(s_down, t + 1)
                if more:
                    load(t + 2, k)
                sp.wait_ge(s_y, 2 * t + 2)
                sp.dma_start(at(y_dram, t), y[:, k, :, :]).then_inc(s_out[k], 16)

            ahead = (count - 2) // 2
            with sp.Fori(0, ahead) as i:
                for k in range(2):
                    tile(2 * i + k, k, None, False, False)
            for t in range(2 * ahead, count):
                tile(t, t % 2, None, False, False, more=t + 2 < count)
            for k in range(2):
                sp.wait_ge(s_out[k], 16 * ((count + 1 - k) // 2))

        @block.tensor
        def _(pe):
            def flip(t, k, uses):
                pe.wait_ge(s_x[k], 16 * uses + 16)
                for blk in range(2):
                    for kb in range(KB):
                        last = nc.tensor.transpose(ps_x[:, kb, blk * P:(blk + 1) * P],
                                                   xin[:, k, blk, kb * P:(kb + 1) * P], p.ident[:])
                last.then_inc(s_flip, 1)

            flip(0, 0, 0)

            def tile(t, k, uses, first, last):
                wk = k if experts else 0
                pe.wait_ge(s_xT, 2 * t + 2)
                pe.wait_ge(s_w[wk], 32 * uses + 32 if experts else 32)
                for j in range(HB):
                    if not (first and j < 4):
                        pe.wait_ge(s_act, HB * t + j - 3)
                    for kb in range(KB):
                        mm = nc.tensor.matmul(ps_h[j % 4][:, 0:FT], w1[:, wk, kb, j * P:(j + 1) * P], xT[:, kb, :],
                                              start=(kb == 0), stop=(kb == KB - 1))
                    mm.then_inc(s_up, 1)
                if not last:
                    flip(t + 1, 1 - k, uses + (1 if k == 1 else 0))
                if not first:
                    pe.wait_ge(s_y, 2 * t)
                for j in range(HB):
                    pe.wait_ge(s_act, HB * t + j + 1)
                    for blk in range(2):
                        mm = nc.tensor.matmul(ps_y[blk][:, 0:D], hT[:, k, j, blk * P:(blk + 1) * P], w2[:, wk, j, :],
                                              start=(j == 0), stop=(j == HB - 1))
                mm.then_inc(s_down, 1)

            over_tiles(pe, tile)

        @block.scalar
        def _(act):
            def tile(t, k, uses, first, last):
                if experts:
                    e = expert(act, t)
                for j in range(HB):
                    bias = flat(b1[:, bass.ds(e, 1), j:j + 1]) if experts else b1[:, j:j + 1]
                    act.wait_ge(s_up, HB * t + j + 1)
                    nc.scalar.activation(hT[:, k, j, :], ps_h[j % 4][:, 0:FT], func, bias=bias).then_inc(s_act, 1)

            over_tiles(act, tile)

        @block.vector
        def _(dve):
            def evacuate(t):
                if experts:
                    e = expert(dve, t)
                dve.wait_ge(s_flip, t + 1)
                for kb in range(KB):
                    if experts:
                        ins = v.tensor_scalar(xT[:, kb, :], ps_x[:, kb, :], p.ln_g[:, kb, bass.ds(e, 1)],
                                              p.ln_b[:, kb, bass.ds(e, 1)], ALU.mult, ALU.add)
                    else:
                        ins = v.tensor_copy(xT[:, kb, :], ps_x[:, kb, :])
                    ins.then_inc(s_xT, 1)

            evacuate(0)

            def tile(t, k, uses, first, last):
                if not last:
                    evacuate(t + 1)
                if experts:
                    e = expert(dve, t)
                dve.wait_ge(s_down, t + 1)
                if not (isinstance(uses, int) and uses == 0):
                    dve.wait_ge(s_out[k], 16 * uses)
                for blk in range(2):
                    bias = flat(b2[:, bass.ds(e, 1), :]) if experts else b2[:]
                    v.tensor_tensor(y[:, k, blk, :], ps_y[blk][:, 0:D], bias, ALU.add).then_inc(s_y, 1)

            over_tiles(dve, tile)

        if scatters is not None:
            @block.gpsimd
            def _(pool):
                scatter.run(pool)



def choose_larger_half(p):
    nc, v = p.nc, p.nc.vector
    with ExitStack() as outer:
        weight = p.share[:, 0, :]
        with ExitStack() as ctx:
            def put(t, slots):
                return [v.tensor_copy(slots[0], flat(p.xb[:, bass.ds(t, 1), :]))]

            def take(t, psum):
                return v.tensor_tensor(p.share[:, 0, bass.ds(t, 1)], psum[:, 0:1], p.mod_br[:], ALU.add)

            pr = Project(p, ctx, [[p.mod_wr[:, kb, :] for kb in range(KB)]], 1, put, take, None)
            s_dve = p.sem("h_s_dve", ctx)
            block = ctx.enter_context(nc.Block())

            @block.vector
            def _(dve):
                pr.dve(dve, Chain(dve, s_dve))

            @block.tensor
            def _(pe):
                pr.pe(pe)

            @block.scalar
            def _(act):
                pr.act(act)

        with ExitStack() as ctx:
            bits, sign, part = (p.sb("h_" + n, [P, NT], I32, ctx) for n in ("bits", "sign", "part"))
            high, low, hit, above, tie, ties, sel, ones, past, scan, carry = (
                p.sb("h_" + n, [P, NT], F32, ctx)
                for n in ("high", "low", "hit", "above", "tie", "ties", "sel", "ones", "past", "scan", "carry"))
            cell = p.sb("h_cell", [P, 12], F32, ctx)
            many = p.sb("h_many", [P, WAYS, NT], F32, ctx)
            nums, enough, steps_up = (p.sb("h_" + n, [P, WAYS], F32, ctx)
                                              for n in ("nums", "enough", "steps_up"))
            ps_n = p.ps("h_ps_n", [P, 512], ctx)
            s_dve, s_n, s_sum = (p.sem("h2_" + n, ctx) for n in ("s_dve", "s_n", "s_sum"))
            block = ctx.enter_context(nc.Block())
            at, num, goal, over, start = (cell[:, k:k + 1] for k in range(5))

            @block.tensor
            def _(pe):
                for r in range(2):
                    for n in range(ROUNDS):
                        pe.wait_ge(s_n, (ROUNDS + 1) * r + n + 1)
                        nc.tensor.matmul(ps_n[:, 0:WAYS], p.ones[:], nums[:], start=True, stop=True).then_inc(s_sum, 1)
                    pe.wait_ge(s_n, (ROUNDS + 1) * (r + 1))
                    nc.tensor.matmul(ps_n[:, 0:1], p.ones[:], num, start=True, stop=True).then_inc(s_sum, 1)
                pe.wait_ge(s_n, 2 * ROUNDS + 3)
                nc.tensor.matmul(ps_n[:, 64:64 + NT], p.before[:], tie[:], start=True, stop=True)
                nc.tensor.matmul(ps_n[:, 128:128 + NT], p.ones[:], tie[:], start=True, stop=True).then_inc(s_sum, 1)
                pe.wait_ge(s_n, 2 * ROUNDS + 4)
                nc.tensor.matmul(ps_n[:, 0:1], p.before[:], num, start=True, stop=True).then_inc(s_sum, 1)

            @block.vector
            def _(dve):
                c = Chain(dve, s_dve)
                wi = weight.bitcast(I32)
                c.link(v.tensor_single_scalar(sign[:], wi, 31, ALU.arith_shift_right))
                c.link(v.tensor_single_scalar(sign[:], sign[:], 0x7FFFFFFF, ALU.bitwise_and))
                c.link(v.tensor_tensor(bits[:], wi, sign[:], ALU.bitwise_xor))
                c.link(v.tensor_single_scalar(part[:], bits[:], 16, ALU.arith_shift_right))
                c.link(v.tensor_copy(high[:], part[:]))
                c.link(v.tensor_single_scalar(part[:], bits[:], 0xFFFF, ALU.bitwise_and))
                c.link(v.tensor_copy(low[:], part[:]))
                c.link(v.tensor_scalar(past[:], p.node_no[:], float(N), None, ALU.is_ge))
                c.link(v.tensor_scalar(scan[:], past[:], -200000.0, None, ALU.mult))
                c.link(v.tensor_tensor(high[:], high[:], scan[:], ALU.add))
                c.done(v.memset(goal, float(KEEP)))
                c.done(v.memset(ones[:], 1.0))
                c.done(v.memset(p.place_i[:], 0))
                c.settle()

                def search(r, values, first):
                    c.link(v.memset(at, first))
                    for n in range(ROUNDS):
                        step = float((WAYS + 1) ** (ROUNDS - 1 - n))
                        c.link(v.tensor_scalar(steps_up[:], p.iota[:, 1:WAYS + 1], step, at, ALU.mult, ALU.add))
                        c.link(v.tensor_tensor(many[:], values.unsqueeze(1).to_broadcast([P, WAYS, NT]),
                                               steps_up[:].unsqueeze(2).to_broadcast([P, WAYS, NT]), ALU.is_ge))
                        v.tensor_reduce(nums[:], many[:], AX, ALU.add).then_inc(s_n, 1)
                        dve.wait_ge(s_sum, (ROUNDS + 1) * r + n + 1)
                        c.link(v.tensor_scalar(enough[:], ps_n[:, 0:WAYS], goal, None, ALU.is_ge, ALU.add,
                                               accum_out=over))
                        c.link(v.scalar_tensor_tensor(out=at, in0=over, scalar=step, in1=at, op0=ALU.mult,
                                                      op1=ALU.add))
                    v.tensor_scalar(hit[:], values, at, None, ALU.is_gt, ALU.add, accum_out=num).then_inc(s_n, 1)
                    dve.wait_ge(s_sum, (ROUNDS + 1) * (r + 1))
                    c.link(v.tensor_tensor(goal, goal, ps_n[:, 0:1], ALU.subtract))

                search(0, high[:], -32768.0)
                c.done(v.tensor_scalar(above[:], high[:], at, None, ALU.is_gt))
                c.done(v.tensor_scalar(tie[:], high[:], at, None, ALU.is_equal))
                c.settle()
                c.link(v.tensor_scalar(low[:], low[:], 1.0, None, ALU.add))
                c.link(v.tensor_tensor(low[:], low[:], tie[:], ALU.mult))
                c.link(v.tensor_scalar(low[:], low[:], -1.0, None, ALU.add))
                search(1, low[:], 0.0)
                c.done(v.tensor_scalar(scan[:], low[:], at, None, ALU.is_gt))
                c.settle()
                c.link(v.tensor_tensor(above[:], above[:], scan[:], ALU.add))
                v.tensor_scalar(tie[:], low[:], at, None, ALU.is_equal).then_inc(s_n, 1)
                dve.wait_ge(s_sum, 2 * ROUNDS + 3)
                c.link(v.tensor_copy(carry[:], ps_n[:, 128:128 + NT]))
                c.link(v.tensor_tensor_scan(ties[:], ones[:], carry[:], 0.0, ALU.mult, ALU.add))
                c.link(v.tensor_tensor(ties[:], ties[:], carry[:], ALU.subtract))
                c.link(v.tensor_tensor(ties[:], ties[:], ps_n[:, 64:64 + NT], ALU.add))
                c.link(v.tensor_scalar(ties[:], ties[:], goal, None, ALU.is_lt))
                c.link(v.tensor_tensor(ties[:], ties[:], tie[:], ALU.mult))
                c.link(v.tensor_tensor(sel[:], above[:], ties[:], ALU.add))
                v.tensor_scalar(hit[:], sel[:], 0.0, None, ALU.add, ALU.add, accum_out=num).then_inc(s_n, 1)
                dve.wait_ge(s_sum, 2 * ROUNDS + 4)
                c.link(v.tensor_scalar(start, ps_n[:, 0:1], -1.0, None, ALU.add))
                c.link(v.tensor_tensor_scan(scan[:], ones[:], sel[:], start, ALU.mult, ALU.add))
                c.link(v.tensor_tensor(scan[:], scan[:], sel[:], ALU.mult))
                c.link(v.tensor_scalar(over, p.part_no[:], float(MOD_TILES * FT), None, ALU.add))
                c.link(v.tensor_scalar(hit[:], sel[:], -1.0, 1.0, ALU.mult, ALU.add))
                c.link(v.tensor_scalar(hit[:], hit[:], over, None, ALU.mult))
                c.link(v.tensor_tensor(scan[:], scan[:], hit[:], ALU.add))
                c.link(v.tensor_copy(p.place_i[:, 0, 0:NT], scan[:]))



INS = ["x", "src", "dst", "edge_weight", "L0_gnn_W0", "L0_gnn_b0", "L0_gnn_g0", "L0_gnn_beta0", "L0_gnn_W1",
       "L0_gnn_b1", "L0_gnn_g1", "L0_gnn_beta1", "L0_ffn_Wr", "L0_ffn_br", "L0_ffn_ln_g", "L0_ffn_ln_b",
       "L0_ffn_W1", "L0_ffn_b1", "L0_ffn_W2", "L0_ffn_b2", "L1_gnn_W_self", "L1_gnn_b_self", "L1_gnn_W_msg",
       "L1_gnn_b_msg", "L1_gnn_ln_gamma", "L1_gnn_ln_beta", "L1_ffn_wr", "L1_ffn_br", "L1_ffn_w1", "L1_ffn_b1",
       "L1_ffn_w2", "L1_ffn_b2"]


def columns(ap):
    return ap.rearrange("(b p) -> p b", p=P)


def build(nc, io, out):
    dram = {name: nc.dram_tensor(name, shape, dt).ap() for name, shape, dt in (
        ("table0", (P * QW, 1), I32), ("table1", (P * QW, 2), I32), ("xn", (NT * P, D), F32),
        ("h1", (NT * P, D), F32), ("x2", (NT * P, D), F32),
        ("moe_in", (MOE_TILES * FT, D), F32), ("moe_out", (MOE_TILES * FT + P, D), F32),
        ("mod_in", (MOD_TILES * FT, D), F32), ("mod_out", (MOD_TILES * FT + P, D), F32))}
    with ExitStack() as ctx:
        p = Program(nc, ctx)
        p.ident, p.before, p.upto, p.ones, p.iota = (p.sb(n, [P, P]) for n in ("ident", "before", "upto", "ones", "iota"))
        p.chunk_no, p.part_no, p.node_no = p.sb("chunk_no", [P, NCH]), p.sb("part_no", [P, 1]), p.sb("node_no", [P, NT])
        p.eps, p.idle = p.sb("eps", [P, 1]), p.sb("idle", [1, 2])
        p.acc, p.xb = p.sb("acc", [P, NT, D + 1]), p.sb("xb", [P, NT, D])
        p.edge_row, p.edge_local, p.edge_weight = p.sb("edge_row", [P, QW], I32), p.sb("edge_local", [P, QW]), p.sb("edge_weight", [P, QW])
        p.addr1, p.rec1, p.weight1 = p.sb("addr1", [P, EC], I32), p.sb("rec1", [P, EC], I32), p.sb("weight1", [P, EC])
        p.place_i, p.share, p.expert_of = p.sb("place_i", [P, TOP, NT + U], I32), p.sb("share", [P, TOP, NT]), p.sb("expert_of", [1, MOE_TILES], I32)
        p.wT, p.Wr, p.mod_wr = p.sb("wT", [P, 4, KB, D]), p.sb("Wr", [P, KB, EX]), p.sb("mod_wr", [P, KB, 1])
        p.br, p.mod_br = p.sb("br", [P, EX]), p.sb("mod_br", [P, 1])
        p.ln_g, p.ln_b = p.sb("ln_g", [P, KB, EX]), p.sb("ln_b", [P, KB, EX])
        p.moe_b1, p.moe_b2, p.mod_b1 = p.sb("moe_b1", [P, EX, HB]), p.sb("moe_b2", [P, EX, D]), p.sb("mod_b1", [P, HB])
        row_params = {name: p.sb("row_" + name, [P, D]) for name in
                      ("L0_gnn_b0", "L0_gnn_b1", "L1_gnn_b_self", "L1_gnn_b_msg", "L0_gnn_g0", "L0_gnn_g1",
                       "L1_gnn_ln_gamma", "L0_gnn_beta0", "L0_gnn_beta1", "L1_gnn_ln_beta", "L1_ffn_b2")}
        p.tile_of = [p.sb(f"tile_of{k}", [1, NCH], I32) for k in range(2)]
        p.norm_in, p.norm_out = RowNorm(p, ctx), RowNorm(p, ctx)
        p.table1 = dram["table1"]
        p.small = [(p.Wr[:], io["L0_ffn_Wr"].rearrange("(b p) e -> p b e", p=P)),
                   (p.br[:], io["L0_ffn_br"].partition_broadcast(P)),
                   (p.mod_br[:], io["L1_ffn_br"].partition_broadcast(P)),
                   (p.mod_wr[:], io["L1_ffn_wr"].rearrange("(b p) e -> p b e", p=P)),
                   (p.mod_b1[:], columns(io["L1_ffn_b1"]))]
        for e in range(EX):
            p.small += [(p.ln_g[:, :, e], columns(io["L0_ffn_ln_g"][e, :])),
                        (p.ln_b[:, :, e], columns(io["L0_ffn_ln_b"][e, :])),
                        (p.moe_b1[:, e, :], columns(io["L0_ffn_b1"][e, :])),
                        (p.moe_b2[:, e, :], io["L0_ffn_b2"][e, :].partition_broadcast(P))]
        for name, row in row_params.items():
            p.small.append((row[:], io[name].partition_broadcast(P)))

        def stage(name, make, *args):
            p.stage = name + "_"
            with nc.cleanup_on_exit():
                make(p, *args)

        stage("sort", sort_edges_and_normalize, io, dram)
        stage("unpack0", unpack_table, dram["table0"], 1)
        stage("sum0", sum_over_edges, dram["xn"], 0, False)
        stage("gnn0", gnn_dense, [0], [row_params["L0_gnn_b0"]], row_params["L0_gnn_g0"],
              row_params["L0_gnn_beta0"], ACT.Silu, None, dram["h1"], (0, 2))
        stage("sum1", sum_over_edges, dram["h1"], 0, False)
        stage("gnn1", gnn_dense, [1], [row_params["L0_gnn_b1"]], row_params["L0_gnn_g1"],
              row_params["L0_gnn_beta1"], ACT.Silu, io["x"], None, (2, 4))
        stage("route", route_to_experts)
        stage("moe_in", dispatch, dram["moe_in"], MOE_TILES * FT, TOP, True)
        stage("moe", ffn, dram["moe_in"], dram["moe_out"], MOE_TILES,
              (io["L0_ffn_W1"], io["L0_ffn_W2"], p.moe_b1, p.moe_b2), True, ACT.Gelu, (4, EC // SSTEP))
        stage("moe_out", combine, dram["moe_out"], TOP, False, p.share, p.norm_out, dram["x2"], dram["xn"], P)
        stage("unpack1", unpack_table, dram["table1"], 2)
        stage("sum2", sum_over_edges, dram["xn"], 1, True)
        stage("gnn2", gnn_dense, [2, 3], [row_params["L1_gnn_b_self"], row_params["L1_gnn_b_msg"]],
              row_params["L1_gnn_ln_gamma"], row_params["L1_gnn_ln_beta"], ACT.Gelu, dram["x2"], None, None)
        stage("half", choose_larger_half)
        stage("half_in", dispatch, dram["mod_in"], MOD_TILES * FT, 1, False)
        stage("ffn", ffn, dram["mod_in"], dram["mod_out"], MOD_TILES,
              (io["L1_ffn_w1"], io["L1_ffn_w2"], p.mod_b1, row_params["L1_ffn_b2"]), False, ACT.Gelu_apprx_tanh, None)
        stage("half_out", combine, dram["mod_out"], 1, True, p.share, None, out, None, LAST)


def kernel(**inputs):
    import concourse.bacc as bacc
    from concourse.bass_utils import run_bass_kernel_spmd

    nc = bacc.Bacc("TRN2", target_bir_lowering=False, num_devices=1)
    arrays, io = {}, {}
    for name in INS:
        a = np.ascontiguousarray(inputs[name])
        arrays[f"in_{name}"] = a
        io[name] = nc.dram_tensor(f"in_{name}", a.shape, mybir.dt.from_np(a.dtype), kind="ExternalInput").ap()
    out = nc.dram_tensor("out", (N, D), F32, kind="ExternalOutput").ap()
    build(nc, io, out)
    r = run_bass_kernel_spmd(nc, [arrays], core_ids=[0])
    return r.results[0]["out"]
```

```python
from contextlib import ExitStack

import numpy as np
import concourse.bass as bass
from concourse import mybir

ALU = mybir.AluOpType
ACT = mybir.ActivationFunctionType
AX = mybir.AxisListType.X
F32 = mybir.dt.float32
BF16 = mybir.dt.bfloat16
F16 = mybir.dt.float16
U16 = mybir.dt.uint16
I32 = mybir.dt.int32

P = 128
N = 6250
D = 256
KB = D // P
H = 1024
HB = H // P
NT = -(-N // P)
LAST = N - (NT - 1) * P
E = 100000
EC = 784
EROWS = E // EC
ETAIL = E - EROWS * EC
EU = 8
GROUPS = 4
SU = GROUPS * EU
NCH = -(-((E + NT * (P - 1)) // P) // SU) * SU
QW = NCH + SU
SE = 7
SGROUPS = 7
SSTEP = SGROUPS * SE
PARTS = ((0, 98), (98, 441), (441, EC))
SENT = PARTS[-1][0]
KEYBITS = 13
NONE = P
LOWBITS = 9
LOW = 1 << LOWBITS
EX = 8
TOP = 2
FT = 256
MOE_TILES = (TOP * N + EX * (FT - 1)) // FT
KEEP = N // 2 - 1
MOD_TILES = -(-KEEP // FT)
EPS = 1e-5
ROUNDS, WAYS = 4, 15
U = 7
STEPS = NT // U
PLACED = (EC - SENT) // NT
assert PLACED * NT == EC - SENT and SENT % SSTEP == 0
assert STEPS * U == NT and EC % SSTEP == 0 and MOE_TILES % 2 == 0


class Chain:

    def __init__(self, eng, sem):
        self.eng, self.sem, self.n, self.base = eng, sem, 0, 0

    def done(self, ins):
        ins.then_inc(self.sem, 1)
        self.n += 1

    def settle(self, but=0):
        self.eng.wait_ge(self.sem, self.base + self.n - but)

    def link(self, ins):
        self.done(ins)
        self.settle()

    def enter(self, i, per):
        self.start, self.per, self.base = self.n, per, i * per

    def leave(self, iterations):
        assert self.n - self.start == self.per, (self.n - self.start, self.per)
        self.n, self.base = self.start + iterations * self.per, 0


class PoolWait:

    def __init__(self, p, pool, sem):
        self.p, self.pool, self.sem = p, pool, sem
        p.nc.gpsimd.memset(p.idle[:], 0.0).then_inc(sem, 1)
        pool.wait_ge(sem, 1)

    def __call__(self, sem, value, before):
        self.pool.wait_ge(self.sem, before + 1)
        self.pool.wait_ge(sem, value)
        self.p.nc.gpsimd.tensor_tensor(self.p.idle[:, 0:1], self.p.idle[:, 1:2], self.p.idle[:, 1:2],
                                       ALU.add).then_inc(self.sem, 1)


def rows(dram, t, n=P):
    return dram[t * P:t * P + n, :]


def tiles(dram, a, b):
    return dram[a * P:b * P, :].rearrange("(t p) d -> p t d", p=P)


class Program:
    def __init__(self, nc, ctx):
        self.nc, self.ctx, self.names, self.stage = nc, ctx, 0, ""

    def sb(self, name, shape, dt=F32, ctx=None):
        return (ctx or self.ctx).enter_context(self.nc.sbuf_tensor(self.stage + name, shape, dt))

    def ps(self, name, shape, ctx):
        return ctx.enter_context(self.nc.psum_tensor(self.stage + name, shape, F32))

    def sem(self, name, ctx):
        return self.nc.alloc_semaphore(self.stage + name)



def sort_edges_and_normalize(p, io, dram):
    nc = p.nc
    with ExitStack() as ctx:
        key = [p.sb(f"key{k}", [P, EC], I32, ctx) for k in range(2)]
        weight = p.weight1
        win_i = p.sb("win_i", [P, EC], I32, ctx)
        win = p.sb("win", [P, EC], BF16, ctx)
        mask = p.sb("mask", [P, 3, EC], BF16, ctx)
        ones_row = p.sb("ones_row", [P, EC], BF16, ctx)
        pos = p.sb("pos", [P, EC], F32, ctx)
        pos_i = p.sb("pos_i", [P, EC], I32, ctx)
        lane = p.sb("lane", [P, EC], I32, ctx)
        local = p.sb("local_sh", [P, EC], I32, ctx)
        addr = [p.sb("addr0", [P, EC], I32, ctx), p.addr1]
        rec = [p.sb("rec0", [P, EC], I32, ctx), p.rec1]
        count = p.sb("count", [P, NT], F32, ctx)
        room = p.acc[:].rearrange("p t d -> p (t d)")
        fill = room[:, 0:2 * QW].bitcast(I32)
        zero = room[:, 2 * QW:2 * QW + 4 * D]
        wload = room[:, 2 * QW + 4 * D:2 * QW + 4 * D + 4 * KB * D].rearrange("p (k b d) -> p k b d", k=4, b=KB)
        xb = p.xb
        norm = RowNorm(p, ctx)
        spare = p.sb("spare", [P, PLACED], F32, ctx)
        used = 2 * QW + 4 * D + 4 * KB * D
        rank = room[:, used:used + 2 * EC].rearrange("p (b c) -> p b c", b=2)
        used += 2 * EC
        hot = room[:, used:used + PLACED * (NCH + 3 * P) // 2].bitcast(F16).rearrange("p (b c) -> p b c", b=PLACED)
        edge_col, edge_lane = (p.edge_weight[:, k * (EC - SENT):(k + 1) * (EC - SENT)] for k in range(2))
        edge_high, edge_low = (p.edge_row[:, k * (EC - SENT):(k + 1) * (EC - SENT)].bitcast(F32) for k in range(2))
        numbers = p.edge_local[:, 0:NCH // 2].bitcast(F16)
        placed = [p.ps(f"placed{k}", [P, 2, 512], ctx) for k in range(2)]
        b = Binning(p, ctx, NT, NCH)
        psw = [p.ps("psw", [P, 512], ctx), b.psrow[:, 512:1024]]

        s = lambda name: p.sem(name, ctx)
        s_const, s_keys0, s_keys1, s_keyfill = s("s_const"), s("s_keys0"), s("s_keys1"), s("s_keyfill")
        s_dve, s_pe, s_addr, s_fill, s_prefill = s("s_dve"), s("s_pe"), s("s_addr"), s("s_fill"), s("s_prefill")
        s_zero, s_xpad, s_x, s_xnout = s("s_zero"), s("s_xpad"), s("s_x"), s("s_xnout")
        scatter = Scatter(p, ctx, dram["table0"], addr[0], [rec[0]])
        s_wload, s_wT, s_wcopied = s("s_wload"), s("s_wT"), s("s_wcopied")
        s_pool, s_small = s("s_pool"), s("s_small")
        s_lane, s_scaled, s_hot, s_placed, s_whole = (
            s("s_lane"), s("s_scaled"), s("s_hot"), s("s_placed"), s("s_whole"))
        block = ctx.enter_context(nc.Block())
        weights = [io["L0_gnn_W0"], io["L0_gnn_W1"], io["L1_gnn_W_self"], io["L1_gnn_W_msg"]]

        @block.gpsimd
        def _(pool):
            c = Chain(pool, s_pool)
            c.done(nc.gpsimd.memset(p.ident[:], 0.0))
            c.done(nc.gpsimd.memset(p.before[:], 1.0))
            c.done(nc.gpsimd.memset(p.upto[:], 1.0))
            c.done(nc.gpsimd.iota(p.iota[:], [[1, P]], base=0, channel_multiplier=0,
                                  allow_small_or_imprecise_dtypes=True))
            c.done(nc.gpsimd.iota(p.chunk_no[:], [[1, NCH]], base=0, channel_multiplier=0,
                                  allow_small_or_imprecise_dtypes=True))
            c.done(nc.gpsimd.iota(p.part_no[:], [[0, 1]], base=0, channel_multiplier=1,
                                  allow_small_or_imprecise_dtypes=True))
            c.done(nc.gpsimd.iota(p.node_no[:], [[P, NT]], base=0, channel_multiplier=1,
                                  allow_small_or_imprecise_dtypes=True))
            c.settle()
            nc.gpsimd.affine_select(out=p.ident[:], in_=p.ident[:], compare_op=ALU.not_equal, fill=1.0, base=0,
                                    pattern=[[-1, P]], channel_multiplier=1).then_inc(s_const, 1)
            nc.gpsimd.affine_select(out=p.before[:], in_=p.before[:], compare_op=ALU.is_gt, fill=0.0, base=0,
                                    pattern=[[1, P]], channel_multiplier=-1).then_inc(s_const, 1)
            nc.gpsimd.affine_select(out=p.upto[:], in_=p.upto[:], compare_op=ALU.is_ge, fill=0.0, base=0,
                                    pattern=[[1, P]], channel_multiplier=-1).then_inc(s_const, 1)
            pool.wait_ge(s_prefill, 32)
            scatter.run(pool, [(first // SSTEP, end // SSTEP, (s_addr, n + 1)) for n, (first, end) in enumerate(PARTS[:-1])])

        @block.scalar
        def _(act):
            for k in range(4):
                act.dma_start(wload[:, k, :, :], weights[k].rearrange("(b p) d -> p b d", p=P)).then_inc(s_wload, 16)
            for k in range(4):
                for kb in range(KB):
                    n = k * KB + kb
                    act.wait_ge(s_wT, n + 1)
                    nc.scalar.activation(p.wT[:, k, kb, :], psw[n % 2][:, 0:D], ACT.Copy).then_inc(s_wcopied, 1)

            with act.Fori(0, STEPS) as i:
                for u in range(U):
                    for j in range(PLACED):
                        n = PLACED * (U * i + u) + j
                        act.wait_ge(s_lane, n + 1)
                        for part, value in enumerate((edge_high, edge_low)):
                            nc.scalar.activation(hot[:, j, NCH + part * P:NCH + (part + 1) * P],
                                                 hot[:, j, NCH + 2 * P:NCH + 3 * P], ACT.Copy,
                                                 scale=value[:, bass.ds(n, 1)]).then_inc(s_scaled, 1)
            act.wait_ge(s_placed, PLACED + EC - SENT + 2)
            nc.scalar.activation(p.edge_local[:, 0:NCH].rearrange("p (b c) -> p b c", b=2),
                                 placed[0][:, :, 0:NCH // 2], ACT.Copy, scale=float(LOW)).then_inc(s_whole, 1)
            norm.root(act)
            norm.apply_rest(act, xb, xb)

        @block.sync
        def _(sp):
            sp.wait_ge(s_keyfill, 2)
            for k, (name, sem) in enumerate((("src", s_keys0), ("dst", s_keys1))):
                sp.dma_start(key[k][0:EROWS, :], io[name][0:EROWS * EC].rearrange("(p c) -> p c", c=EC)).then_inc(sem, 16)
                sp.dma_start(key[k][EROWS:EROWS + 1, 0:ETAIL],
                             io[name][EROWS * EC:E].rearrange("(a c) -> a c", a=1)).then_inc(sem, 16)
            sp.wait_ge(s_keyfill, 3)
            sp.dma_start(weight[0:EROWS, :], io["edge_weight"][0:EROWS * EC].rearrange("(p c) -> p c", c=EC)).then_inc(s_keys1, 16)
            sp.dma_start(weight[EROWS:EROWS + 1, 0:ETAIL],
                         io["edge_weight"][EROWS * EC:E].rearrange("(a c) -> a c", a=1)).then_inc(s_keys1, 16)
            sp.wait_ge(s_fill, 1)
            sp.dma_start(dram["table0"].rearrange("(p q) a -> p (q a)", p=P), fill[:, 0:QW]).then_inc(s_prefill, 16)
            sp.dma_start(dram["table1"].rearrange("(p q) a -> p (q a)", p=P), fill[:, :]).then_inc(s_prefill, 16)
            sp.wait_ge(s_xpad, 1)
            sp.dma_start(xb[:, 0:NT - 1, :], tiles(io["x"], 0, NT - 1)).then_inc(s_x, 16)
            sp.dma_start(xb[0:LAST, NT - 1, :], rows(io["x"], NT - 1, LAST)).then_inc(s_x, 16)
            sp.wait_ge(s_zero, 1)
            zeros = 0
            for name in ("moe_in", "moe_out", "mod_in", "mod_out"):
                flat = dram[name].rearrange("(g r) d -> g (r d)", r=4)
                total = flat.shape[0]
                first = 0 if name.endswith("in") else total - P // 4
                for g in range(first, total, P):
                    n = min(P, total - g)
                    sp.dma_start(flat[g:g + n, :], zero[0:n, :]).then_inc(s_zero, 16)
                    zeros += 1
            send_steps(sp, norm.made(), dram["xn"], xb, s_xnout)
            sp.wait_ge(s_xnout, 16 * STEPS)
            small = 0
            with nc.allow_non_contiguous_dma("small parameters"):
                for dst, source in p.small:
                    sp.dma_start(dst, source).then_inc(s_small, 16)
                    small += 1
            sp.wait_ge(s_small, 16 * small)
            sp.wait_ge(s_zero, 1 + 16 * zeros)

        @block.tensor
        def _(pe):
            def place(slot, start=False, stop=False):
                for part in range(2):
                    for half in range(2):
                        mm = nc.tensor.matmul(placed[part][:, half, 0:NCH // 2],
                                              hot[:, slot, NCH + part * P:NCH + (part + 1) * P],
                                              hot[:, slot, half * (NCH // 2):(half + 1) * (NCH // 2)],
                                              start=start, stop=stop)
                return mm

            pe.wait_ge(s_const, 3)
            pe.wait_ge(s_wload, 64)
            for k in range(4):
                for kb in range(KB):
                    n = k * KB + kb
                    if n >= 2:
                        pe.wait_ge(s_wcopied, n - 1)
                    for jb in range(KB):
                        last = nc.tensor.transpose(psw[n % 2][:, jb * P:(jb + 1) * P],
                                                   wload[:, k, jb, kb * P:(kb + 1) * P], p.ident[:])
                    last.then_inc(s_wT, 1)
            pe.wait_ge(s_hot, 1)
            place(0, start=True).then_inc(s_placed, 1)
            pe.wait_ge(s_wcopied, 4 * KB)
            for k in range(2):
                b.products(pe, k, count, b.s_count)

            with pe.Fori(0, STEPS) as i:
                for u in range(U):
                    for j in range(PLACED):
                        pe.wait_ge(s_hot, PLACED * (U * i + u) + j + 2)
                        pe.wait_ge(s_scaled, 2 * (PLACED * (U * i + u) + j) + 2)
                        place(j).then_inc(s_placed, 1)
            pe.wait_ge(s_hot, EC - SENT + 2)
            place(0, stop=True).then_inc(s_placed, 1)

        @block.vector
        def _(dve):
            c = Chain(dve, s_dve)

            def spread(n, slot):
                dve.wait_ge(s_placed, n + 2)
                at = bass.ds(n, 1)
                nc.vector.tensor_scalar(hot[:, slot, NCH + 2 * P:NCH + 3 * P], numbers[:, 0:P], edge_lane[:, at], None,
                                        ALU.is_equal).then_inc(s_lane, 1)
                nc.vector.tensor_scalar(hot[:, slot, 0:NCH], numbers, edge_col[:, at], None,
                                        ALU.is_equal).then_inc(s_hot, 1)

            for k in range(2):
                nc.vector.memset(key[k][:], (NT + 14) * P).then_inc(s_keyfill, 1)
            nc.vector.memset(weight[:], 0.0).then_inc(s_keyfill, 1)
            nc.vector.memset(fill, NONE << KEYBITS).then_inc(s_fill, 1)
            nc.vector.memset(xb[:, NT - 1, :], 0.0).then_inc(s_xpad, 1)
            nc.vector.memset(zero, 0.0).then_inc(s_zero, 1)
            c.done(nc.vector.memset(p.ones[:], 1.0))
            c.done(nc.vector.memset(p.eps[:], EPS))
            c.done(nc.vector.memset(ones_row[:], 1.0))
            dve.wait_ge(s_keys0, 32)
            dve.wait_ge(s_keys1, 64)
            dve.wait_ge(s_const, 3)
            c.done(nc.vector.tensor_copy(numbers, p.chunk_no[:]))
            c.done(nc.vector.memset(p.edge_local[:, NCH:], 0.0))
            nc.vector.memset(hot, 0.0).then_inc(s_hot, 1)
            dve.wait_ge(s_hot, 1)
            for k in range(PLACED):
                nc.vector.memset(spare[:, k:k + 1], 0.0).then_inc(s_placed, 1)
            for k in range(2):
                mine, other = key[k], key[1 - k]
                c.done(nc.vector.tensor_single_scalar(win_i[:], mine[:], 7, ALU.arith_shift_right))
                c.done(nc.vector.tensor_scalar(local[:], mine[:], P - 1, KEYBITS, ALU.bitwise_and,
                                               ALU.logical_shift_left))
                c.done(nc.vector.memset(pos[:], 0.0))
                c.settle()
                c.done(nc.vector.tensor_copy(win[:], win_i[:]))
                c.link(nc.vector.tensor_tensor(rec[k][:], local[:], other[:], ALU.bitwise_or))
                with dve.Fori(0, STEPS) as i:
                    c.enter(i, U)
                    for u in range(U):
                        tile = bass.ds(U * i + u, 1)
                        if u > 1:
                            c.settle(but=1)
                        elif u == 0:
                            c.settle()
                        c.done(nc.vector.tensor_scalar(mask[:, u % 2, :], win[:], p.iota[:, tile], None, ALU.is_equal,
                                                       ALU.add, accum_out=count[:, tile]))
                c.leave(STEPS)
                c.settle()
                nc.vector.tensor_copy(b.count[:], count[:]).then_inc(b.s_count, 1)
                b.starts(dve, c, k, 7, P)
                if k == 1:
                    b.table(dve, c, k, p.tile_of[k])
                    dve.wait_ge(s_placed, PLACED + 1)
                for first, end in PARTS if k == 0 else ((0, EC),):
                    part = slice(first, end)
                    with dve.Fori(0, STEPS) as i:
                        c.enter(i, 4 * U)

                        def make_mask(u):
                            c.done(nc.vector.tensor_scalar(mask[:, u % 3, part], win[:, part],
                                                           p.iota[:, bass.ds(U * i + u, 1)], None, ALU.is_equal))

                        make_mask(0)
                        for u in range(U):
                            start = b.start[:, bass.ds(U * i + u, 1)]
                            c.settle(but=2 * (u > 0))
                            c.done(nc.vector.tensor_tensor_scan(rank[:, u % 2, part], ones_row[:, part],
                                                                mask[:, u % 3, part], start, ALU.mult, ALU.add))
                            if k == 1:
                                for j in range(PLACED // 2):
                                    spread(PLACED * (U * i + u) + j, j)
                            if u + 1 < U:
                                make_mask(u + 1)
                            c.settle(but=(u + 1 < U))
                            c.done(nc.vector.tensor_scalar(start, rank[:, u % 2, end - 1:end], 0.0, None, ALU.add))
                            c.done(nc.vector.copy_predicated(pos[:, part], mask[:, u % 3, part].bitcast(U16),
                                                             rank[:, u % 2, part]))
                            if k == 1:
                                for j in range(PLACED // 2, PLACED):
                                    spread(PLACED * (U * i + u) + j, j)
                        c.settle()
                    c.leave(STEPS)
                    c.link(nc.vector.tensor_scalar(rank[:, 0, part], win[:, part], float(NT), float(1 << 24), ALU.is_ge,
                                                   ALU.mult))
                    c.link(nc.vector.tensor_tensor(pos[:, part], pos[:, part], rank[:, 0, part], ALU.add))
                    c.link(nc.vector.tensor_copy(pos_i[:, part], pos[:, part]))
                    c.done(nc.vector.tensor_single_scalar(lane[:, part], pos_i[:, part], P - 1, ALU.bitwise_and))
                    c.link(nc.vector.tensor_single_scalar(win_i[:, part], pos_i[:, part], 7, ALU.arith_shift_right))
                    if k == 0 and first == SENT:
                        c.done(nc.vector.tensor_copy(edge_lane, lane[:, part]))
                        c.done(nc.vector.tensor_copy(edge_col, win_i[:, part]))
                        c.link(nc.vector.tensor_single_scalar(pos_i[:, part], rec[0][:, part], LOWBITS,
                                                              ALU.arith_shift_right))
                        c.done(nc.vector.tensor_single_scalar(lane[:, part], rec[0][:, part], LOW - 1, ALU.bitwise_and))
                        c.link(nc.vector.tensor_scalar(edge_high, pos_i[:, part], -float(NONE << (KEYBITS - LOWBITS)),
                                                       None, ALU.add))
                        nc.vector.tensor_copy(edge_low, lane[:, part]).then_inc(s_addr, 1)
                    else:
                        nc.vector.scalar_tensor_tensor(out=addr[k][:, part], in0=lane[:, part], scalar=float(QW),
                                                       in1=win_i[:, part], op0=ALU.mult,
                                                       op1=ALU.add).then_inc(s_addr, 1)
                    dve.wait_ge(s_addr, len(PARTS) + 1 if k else PARTS.index((first, end)) + 1)
                if k == 0:
                    b.table(dve, c, k, p.tile_of[k])
            dve.wait_ge(s_placed, PLACED + EC - SENT + 1)
            nc.vector.memset(hot[:, 0, :], 0.0).then_inc(s_hot, 1)
            dve.wait_ge(s_x, 32)
            with dve.Fori(0, STEPS) as i:
                for u in range(U):
                    norm.take(flat(xb[:, bass.ds(U * i + u, 1), :]), U * i + u).then_inc(s_dve, 1)
            c.n += NT
            c.settle()
            norm.finish(dve, c)
            norm.apply(dve, xb, xb)
            dve.wait_ge(s_whole, 1)
            whole = p.edge_local[:, 0:NCH].rearrange("p (b c) -> p b c", b=2)
            nc.vector.tensor_tensor(whole, whole, placed[1][:, :, 0:NCH // 2], ALU.add).then_inc(s_whole, 1)


class RowNorm:

    def __init__(self, p, ctx):
        self.p = p
        tag = f"n{p.names}"
        p.names += 1
        self.stats = p.sb(tag + "stats", [P, NT, 6], F32, ctx)
        self.mean = p.sb(tag + "mean", [P, NT], F32, ctx)
        self.half = p.sb(tag + "half", [P, NT], F32, ctx)
        self.var = p.sb(tag + "var", [P, NT], F32, ctx)
        self.rstd = p.sb(tag + "rstd", [P, NT], F32, ctx)
        self.s_var = p.sem(tag + "s_var", ctx)
        self.s_std = p.sem(tag + "s_std", ctx)
        self.shift = p.sb(tag + "shift", [P, NT], F32, ctx)
        self.s_shift, self.s_by_dve, self.s_by_act = (p.sem(tag + x, ctx) for x in ("s_shift", "s_by_dve", "s_by_act"))

    def take(self, row, t):
        return self.p.nc.vector.bn_stats(self.stats[:, bass.ds(t, 1), :].rearrange("p a s -> p (a s)"), row)

    def finish(self, dve, c):
        v, st = self.p.nc.vector, self.stats
        c.done(v.tensor_tensor(self.mean[:], st[:, :, 1], st[:, :, 4], ALU.add))
        c.done(v.tensor_tensor(self.half[:], st[:, :, 1], st[:, :, 4], ALU.subtract))
        c.done(v.tensor_tensor(self.var[:], st[:, :, 2], st[:, :, 5], ALU.add))
        c.settle()
        c.done(v.tensor_scalar(self.mean[:], self.mean[:], 0.5, None, ALU.mult))
        c.done(v.tensor_tensor(self.half[:], self.half[:], self.half[:], ALU.mult))
        c.done(v.tensor_scalar(self.var[:], self.var[:], 4.0 / D, None, ALU.mult))
        c.settle()
        c.link(v.tensor_tensor(self.var[:], self.var[:], self.half[:], ALU.add))
        v.tensor_scalar(self.var[:], self.var[:], 0.25, None, ALU.mult).then_inc(self.s_var, 1)
        dve.wait_ge(self.s_std, 1)
        c.link(v.reciprocal(self.rstd[:], self.rstd[:]))

    BY_DVE = 4

    def apply(self, dve, buf, out):
        v = self.p.nc.vector
        v.scalar_tensor_tensor(out=self.shift[:], in0=self.mean[:], scalar=-1.0, in1=self.rstd[:],
                               op0=ALU.mult, op1=ALU.mult).then_inc(self.s_shift, 1)
        with dve.Fori(0, STEPS) as i:
            for u in range(self.BY_DVE):
                t = bass.ds(U * i + u, 1)
                v.tensor_scalar(flat(out[:, t, :]), flat(buf[:, t, 0:D]), self.mean[:, t], self.rstd[:, t],
                                ALU.subtract, ALU.mult).then_inc(self.s_by_dve, 1)

    def apply_rest(self, act, buf, out):
        act.wait_ge(self.s_shift, 1)
        with act.Fori(0, STEPS) as i:
            for u in range(self.BY_DVE, U):
                t = bass.ds(U * i + u, 1)
                self.p.nc.scalar.activation(flat(out[:, t, :]), flat(buf[:, t, 0:D]), ACT.Identity,
                                            bias=self.shift[:, t], scale=self.rstd[:, t]).then_inc(self.s_by_act, 1)

    def made(self):
        return [(self.s_by_dve, self.BY_DVE), (self.s_by_act, U - self.BY_DVE)]

    def root(self, act):
        act.wait_ge(self.s_var, 1)
        self.p.nc.scalar.activation(self.rstd[:], self.var[:], ACT.Sqrt, bias=self.p.eps[:, 0:1]).then_inc(self.s_std, 1)


def flat(ap):
    return ap.rearrange("p a d -> p (a d)")


def send_steps(sp, made, dram, buf, sem):
    with sp.Fori(0, STEPS) as i:
        for counted, per in made:
            sp.wait_ge(counted, per * i + per)
        sp.dma_start(dram[bass.ds(P * U * i, P * U), :].rearrange("(t p) d -> p t d", p=P),
                     buf[:, bass.ds(U * i, U), 0:D]).then_inc(sem, 16)


class Binning:

    def __init__(self, p, ctx, bins, chunks):
        self.p, self.bins, self.chunks = p, bins, chunks
        tag = f"b{p.names}"
        p.names += 1
        self.count = p.sb(tag + "count", [P, bins], F32, ctx)
        self.start = p.sb(tag + "start", [P, bins], F32, ctx)
        self.total = p.sb(tag + "total", [P, 2 * bins + 2], F32, ctx)
        self.total_i = p.sb(tag + "total_i", [P, bins + 1], I32, ctx)
        self.full = p.sb(tag + "full", [P, bins + 1], F32, ctx)
        self.cum = p.sb(tag + "cum", [P, bins], F32, ctx)
        self.onesb = p.sb(tag + "onesb", [P, bins], F32, ctx)
        self.ended = p.sb(tag + "ended", [P, chunks], F32, ctx)
        self.ps = p.ps(tag + "ps", [P, 512], ctx)
        self.psrow = p.ps(tag + "psrow", [P, 1024], ctx)
        self.s_count = p.sem(tag + "s_count", ctx)
        self.s_sums = p.sem(tag + "s_sums", ctx)
        self.s_whole = p.sem(tag + "s_whole", ctx)
        self.s_cum = p.sem(tag + "s_cum", ctx)
        self.s_ended = p.sem(tag + "s_ended", ctx)
        self.s_row = p.sem(tag + "s_row", ctx)

    def products(self, pe, k, count, s_count):
        p, nc, B = self.p, self.p.nc, self.bins
        pe.wait_ge(s_count, k + 1)
        nc.tensor.matmul(self.ps[:, 0:B], p.before[:], self.count[:], start=True, stop=True)
        nc.tensor.matmul(self.ps[:, 64:64 + B], p.ones[:], self.count[:], start=True, stop=True)
        nc.tensor.matmul(self.ps[0:B, 128:129], self.count[:], p.ones[:, 0:1], start=True, stop=True).then_inc(self.s_sums, 1)
        pe.wait_ge(self.s_whole, k + 1)
        nc.tensor.matmul(self.ps[0:B, 192:193], p.upto[0:B, 0:B], self.full[0:B, B:B + 1],
                         start=True, stop=True).then_inc(self.s_cum, 1)
        pe.wait_ge(self.s_ended, k + 1)
        for a in range(0, self.chunks, 512):
            n = min(512, self.chunks - a)
            last = nc.tensor.matmul(self.psrow[0:1, a:a + n], p.ones[0:B, 0:1], self.ended[0:B, a:a + n],
                                    start=True, stop=True)
        last.then_inc(self.s_row, 1)

    def starts(self, dve, c, k, shift, chunk):
        p, nc, B = self.p, self.p.nc, self.bins
        c.done(nc.vector.memset(self.onesb[:], 1.0))
        c.done(nc.vector.memset(self.total[:], 0.0))
        c.settle()
        dve.wait_ge(self.s_sums, k + 1)
        c.done(nc.vector.tensor_copy(self.start[:], self.ps[:, 0:B]))
        c.done(nc.vector.tensor_scalar(self.total[:, 0:B], self.ps[:, 64:64 + B], float(chunk - 1), None, ALU.add))
        c.done(nc.vector.tensor_scalar(self.total[0:B, B:B + 1], self.ps[0:B, 128:129], float(chunk - 1), None, ALU.add))
        c.settle()
        c.link(nc.vector.tensor_copy(self.total_i[:], self.total[:, 0:B + 1]))
        c.link(nc.vector.tensor_single_scalar(self.total_i[:], self.total_i[:], shift, ALU.arith_shift_right))
        c.link(nc.vector.tensor_copy(self.full[:], self.total_i[:]))
        nc.vector.tensor_tensor_scan(self.cum[:], self.onesb[:], self.full[:, 0:B], 0.0,
                                     ALU.mult, ALU.add).then_inc(self.s_whole, 1)
        dve.wait_ge(self.s_whole, k + 1)
        c.link(nc.vector.tensor_tensor(self.cum[:], self.cum[:], self.full[:, 0:B], ALU.subtract))
        c.link(nc.vector.tensor_scalar(self.cum[:], self.cum[:], float(chunk), -1.0, ALU.mult, ALU.add))
        c.link(nc.vector.tensor_tensor(self.start[:], self.start[:], self.cum[:], ALU.add))

    def table(self, dve, c, k, row):
        p, nc, B, M = self.p, self.p.nc, self.bins, self.chunks
        dve.wait_ge(self.s_cum, k + 1)
        c.link(nc.vector.tensor_copy(self.total[0:B, B + 1:B + 2], self.ps[0:B, 192:193]))
        nc.vector.tensor_scalar(self.ended[0:B, :], p.chunk_no[0:B, 0:M], self.total[0:B, B + 1:B + 2], None,
                                ALU.is_ge).then_inc(self.s_ended, 1)
        dve.wait_ge(self.s_row, k + 1)
        c.link(nc.vector.tensor_scalar(row[0:1, 0:M], self.psrow[0:1, 0:M], float(B - 1), None, ALU.min))



def unpack_table(p, table, fields):
    nc = p.nc
    with ExitStack() as ctx:
        raw = p.sb(f"raw{fields}", [P, QW, fields], I32, ctx)
        loc_i = p.sb(f"loc_i{fields}", [P, QW], I32, ctx)
        s_raw, s_dve = p.sem("s_raw", ctx), p.sem("s_dve", ctx)
        block = ctx.enter_context(nc.Block())

        @block.sync
        def _(sp):
            sp.dma_start(raw[:], table.rearrange("(p q) a -> p q a", p=P)).then_inc(s_raw, 16)

        @block.vector
        def _(dve):
            c = Chain(dve, s_dve)
            dve.wait_ge(s_raw, 16)
            if fields == 1:
                c.link(nc.vector.tensor_tensor(p.edge_local[:], p.edge_local[:], raw[:, :, 0], ALU.add))
                c.link(nc.vector.tensor_copy(raw[:, :, 0], p.edge_local[:]))
            c.done(nc.vector.tensor_single_scalar(p.edge_row[:], raw[:, :, 0], (1 << KEYBITS) - 1, ALU.bitwise_and))
            c.done(nc.vector.tensor_single_scalar(loc_i[:], raw[:, :, 0], KEYBITS, ALU.arith_shift_right))
            if fields == 2:
                c.done(nc.vector.tensor_copy(p.edge_weight[:], raw[:, :, 1].bitcast(F32)))
            c.settle()
            c.link(nc.vector.tensor_copy(p.edge_local[:], loc_i[:]))


def sum_over_edges(p, source, order, weighted, own=None):
    nc = p.nc
    with ExitStack() as ctx:
        row_slot = p.sb("row_slot", [P, SU], I32, ctx)
        got = p.sb("got", [P, SU, D + 1], F32, ctx)
        onehot = p.sb("onehot", [P, 4, P], F32, ctx)
        spare = p.sb("spare", [P, 3], F32, ctx)
        sums = [p.ps(f"sums{i}", [P, 512], ctx) for i in range(4)]
        s = lambda name: p.sem(name, ctx)
        s_rows = [s(f"s_rows{h}") for h in range(GROUPS)]
        s_got = [s(f"s_got{h}") for h in range(GROUPS)]
        s_idle, s_ready, s_onehot, s_sum, s_added = s("s_idle"), s("s_ready"), s("s_onehot"), s("s_sum"), s("s_added")
        if own is not None:
            own_rhs, own_biases = own
            own_row, own_flip = p.sb("own_row", [P, 2, D], F32, ctx), p.sb("own_flip", [P, 2, D], F32, ctx)
            own_bias, own_spare = p.sb("own_bias", [P, D], F32, ctx), p.sb("own_spare", [P, 2], F32, ctx)
            ps_flip = [p.ps(f"own_ps_flip{q}", [P, 512], ctx) for q in range(2)]
            ps_own = [p.ps(f"own_ps{q}", [P, 512], ctx) for q in range(2)]
            s_put, s_flip, s_copied, s_own, s_kept = (s("own_" + x) for x in
                                                      ("s_put", "s_flip", "s_copied", "s_own", "s_kept"))
        block = ctx.enter_context(nc.Block())
        STEPE = NCH // SU
        assert STEPE > NT // 2

        def over_steps(eng, step):
            if own is None:
                with eng.Fori(0, STEPE) as i:
                    step(i, 0)
            else:
                with eng.Fori(0, NT // 2) as i:
                    step(i, 2)
                for i in range(NT // 2, STEPE):
                    step(i, NT % 2 if i == NT // 2 else 0)

        def due(n, after, owns):
            return n // (SU // 2) if n % (SU // 2) == after and n // (SU // 2) < owns else None

        @block.scalar
        def _(act):
            def fill(h, c0):
                nc.scalar.activation(row_slot[:, h * EU:(h + 1) * EU], p.edge_row[:, bass.ds(c0, EU)],
                                     ACT.Copy).then_inc(s_rows[h], 1)
            for h in range(GROUPS):
                fill(h, h * EU)

            def step(i, owns):
                for h in range(GROUPS):
                    act.wait_ge(s_sum, SU * i + (h + 1) * EU)
                    fill(h, SU * i + SU + h * EU)
                    q = due(h * EU, 0, owns)
                    if q is not None:
                        act.wait_ge(s_flip, 2 * i + q + 1)
                        nc.scalar.activation(own_flip[:, q, :], ps_flip[q][:, 0:D], ACT.Copy).then_inc(s_copied, 1)

            over_steps(act, step)

        @block.gpsimd
        def _(pool):
            ready = PoolWait(p, pool, s_idle)
            with pool.Fori(0, STEPE) as i:
                for h in range(GROUPS):
                    ready(s_rows[h], i + 1, GROUPS * i + h)
                    for u in range(h * EU, (h + 1) * EU):
                        pool.indirect_dma_start(
                            got[:, u, 0:D], None, source,
                            bass.IndirectOffsetOnAxis(ap=row_slot[:, u:u + 1], axis=0)).then_inc(s_got[h], 16)

        @block.tensor
        def _(pe):
            pe.wait_ge(s_ready, 1)

            def step(i, owns):
                for h in range(GROUPS):
                    pe.wait_ge(s_got[h], 16 * EU * i + 16 * EU)
                    for u in range(EU):
                        n = h * EU + u
                        pe.wait_ge(s_onehot, SU * i + n + 1)
                        pe.wait_ge(s_added, SU * i + n + 1)
                        nc.tensor.matmul(sums[n % 4][:, 0:D + 1], onehot[:, n % 4, :], got[:, n, :],
                                         start=True, stop=True).then_inc(s_sum, 1)
                        q = due(n, 3, owns)
                        if q is not None:
                            pe.wait_ge(s_put, 2 * i + q + 1)
                            for kb in range(KB):
                                last = nc.tensor.transpose(ps_flip[q][:, kb * P:(kb + 1) * P],
                                                           own_row[:, q, kb * P:(kb + 1) * P], p.ident[:])
                            last.then_inc(s_flip, 1)
                        q = due(n, 10, owns)
                        if q is not None:
                            pe.wait_ge(s_copied, 2 * i + q + 1)
                            pe.wait_ge(s_kept, 2 * i + q + 1)
                            for kb in range(KB):
                                last = nc.tensor.matmul(ps_own[q][:, 0:D], own_flip[:, q, kb * P:(kb + 1) * P],
                                                        own_rhs[kb], start=(kb == 0), stop=(kb == KB - 1))
                            last.then_inc(s_own, 1)

            over_steps(pe, step)

        @block.vector
        def _(dve):
            nc.vector.memset(got[:, :, D:D + 1], 1.0).then_inc(s_ready, 1)

            def build(n, c):
                if weighted:
                    ins = nc.vector.tensor_scalar(onehot[:, n % 4, :], p.iota[:], p.edge_local[:, bass.ds(c, 1)],
                                                  p.edge_weight[:, bass.ds(c, 1)], ALU.is_equal, ALU.mult)
                else:
                    ins = nc.vector.tensor_scalar(onehot[:, n % 4, :], p.iota[:], p.edge_local[:, bass.ds(c, 1)],
                                                  None, ALU.is_equal)
                ins.then_inc(s_onehot, 1)

            build(0, 0)
            build(1, 1)
            for _i in range(3):
                nc.vector.memset(spare[:, _i:_i + 1], 0.0).then_inc(s_added, 1)
            nc.vector.memset(p.acc[:], 0.0).then_inc(s_added, 1)
            if own is not None:
                for q in range(2):
                    nc.vector.memset(own_spare[:, q:q + 1], 0.0).then_inc(s_kept, 1)
                nc.vector.tensor_tensor(own_bias[:], own_biases[0][:], own_biases[1][:], ALU.add).then_inc(s_ready, 1)
                dve.wait_ge(s_ready, 2)

            def step(i, owns):
                for n in range(SU):
                    if n % EU == 0:
                        _, tile_regs = nc.values_load_multi_w_load_instructions(
                            p.tile_of[order][0:1, bass.ds(SU * i + n, EU)], (mybir.EngineType.DVE,), min_val=0,
                            max_val=NT - 1)
                    build(n + 2, SU * i + n + 2)
                    dve.wait_ge(s_sum, SU * i + n + 1)
                    dve.wait_ge(s_added, SU * i + n + 4)
                    a = p.acc[:, bass.ds(tile_regs[n % EU], 1), :].rearrange("p a d -> p (a d)")
                    nc.vector.tensor_tensor(a, a, sums[n % 4][:, 0:D + 1], ALU.add).then_inc(s_added, 1)
                    q = due(n, 1, owns)
                    if q is not None:
                        nc.vector.tensor_scalar(own_row[:, q, :], flat(p.xb[:, bass.ds(2 * i + q, 1), :]), 0.0, None,
                                                ALU.add).then_inc(s_put, 1)
                    q = due(n, SU // 2 - 1, owns)
                    if q is not None:
                        dve.wait_ge(s_own, 2 * i + q + 1)
                        nc.vector.tensor_tensor(flat(p.xb[:, bass.ds(2 * i + q, 1), :]), ps_own[q][:, 0:D],
                                                own_bias[:], ALU.add).then_inc(s_kept, 1)

            over_steps(dve, step)



BANK = [0, 1, 2, 0, 1, 2, 3]


class Project:

    def __init__(self, p, ctx, rhs, cols, put, take, then):
        self.p, self.rhs, self.cols, self.put, self.take, self.then = p, rhs, cols, put, take, then
        n = len(rhs)
        self.slots = p.sb("pr_rows", [P, U, n, D], F32, ctx)
        self.flip = p.sb("pr_flip", [P, U, n * D], F32, ctx)
        self.spare = p.sb("pr_spare", [P, 6], F32, ctx)
        self.ps_flip = [p.ps(f"pr_psflip{i}", [P, 512], ctx) for i in range(4)]
        self.ps_out = [p.ps(f"pr_psout{i}", [P, 512], ctx) for i in range(4)]
        self.s_put, self.s_flip, self.s_copied, self.s_out, self.s_taken = (
            p.sem(f"pr_{x}", ctx) for x in ("s_put", "s_flip", "s_copied", "s_out", "s_taken"))

    def steps(self, eng, tile):
        with eng.Fori(0, STEPS - 1) as i:
            self.i = i
            for u in range(U):
                tile(U * i + u, u, U)
        self.i = STEPS - 1
        for u in range(U):
            tile(U * (STEPS - 1) + u, u, U - 1 - u)

    PUT, FLIP = 4, 2

    def dve(self, dve, c):
        p, n = self.p, len(self.rhs)
        follows = self.then is not None

        def put(t, u):
            for ins in self.put(t, [self.slots[:, u, k, :] for k in range(n)]):
                ins.then_inc(self.s_put, 1)

        for k in range(3):
            p.nc.vector.memset(self.spare[:, k:k + 1], 0.0).then_inc(self.s_taken, 1)
        for t in range(self.PUT):
            put(t, t)

        def tile(t, u, more):
            if u == 0 and follows:
                if isinstance(self.i, int):
                    c.leave(STEPS - 1)
                else:
                    c.enter(self.i, U)
            dve.wait_ge(self.s_out, t + 1)
            self.take(t, self.ps_out[BANK[u]]).then_inc(self.s_taken, 1)
            if more >= self.PUT:
                put(t + self.PUT, (u + self.PUT) % U)
            if follows:
                dve.wait_ge(self.s_taken, t + 4)
                c.done(self.then(t))

        self.steps(dve, tile)
        c.settle()
        dve.wait_ge(self.s_taken, NT + 3)

    def pe(self, pe):
        nc, n = self.p.nc, len(self.rhs)

        def flip(t, u):
            pe.wait_ge(self.s_put, n * t + n)
            pe.wait_ge(self.s_copied, t + 1)
            for k in range(n):
                for kb in range(KB):
                    last = nc.tensor.transpose(self.ps_flip[BANK[u]][:, (k * KB + kb) * P:(k * KB + kb + 1) * P],
                                               self.slots[:, u, k, kb * P:(kb + 1) * P], self.p.ident[:])
            last.then_inc(self.s_flip, 1)

        for t in range(self.FLIP):
            flip(t, t)

        def tile(t, u, more):
            if more >= self.FLIP:
                flip(t + self.FLIP, (u + self.FLIP) % U)
            pe.wait_ge(self.s_copied, t + 4)
            pe.wait_ge(self.s_taken, t + 1)
            for k in range(n):
                for kb in range(KB):
                    last = nc.tensor.matmul(self.ps_out[BANK[u]][:, 0:self.cols],
                                            self.flip[:, u, (k * KB + kb) * P:(k * KB + kb + 1) * P],
                                            self.rhs[k][kb], start=(k + kb == 0), stop=(k == n - 1 and kb == KB - 1))
            last.then_inc(self.s_out, 1)

        self.steps(pe, tile)

    def act(self, act):
        nc, n = self.p.nc, len(self.rhs)
        for k in range(3):
            nc.scalar.activation(self.spare[:, 3 + k:4 + k], self.p.eps[:], ACT.Copy).then_inc(self.s_copied, 1)

        def tile(t, u, more):
            act.wait_ge(self.s_flip, t + 1)
            nc.scalar.activation(self.flip[:, u, :], self.ps_flip[BANK[u]][:, 0:n * D], ACT.Copy).then_inc(self.s_copied, 1)

        self.steps(act, tile)


class Scatter:

    def __init__(self, p, ctx, table, addr, fields):
        self.p, self.table, self.source, self.fields = p, table, addr, fields
        self.addr = p.sb("sc_addr", [P, SSTEP], I32, ctx)
        self.rec = p.sb("sc_rec", [P, SSTEP, len(fields)], I32, ctx)
        self.s_idle = p.sem("sc_s_idle", ctx)
        self.s_slot = [p.sem(f"sc_s_slot{h}", ctx) for h in range(SGROUPS)]
        self.s_sent = [p.sem(f"sc_s_sent{h}", ctx) for h in range(SGROUPS)]

    def run(self, pool, parts):
        p, copies = self.p, 1 + len(self.fields)
        start = parts[0][0]
        ready = PoolWait(p, pool, self.s_idle)

        def fill(h, step):
            slots, columns = slice(h * SE, (h + 1) * SE), bass.ds(SSTEP * step + h * SE, SE)
            pairs = [(self.addr[:, slots], self.source[:, columns])]
            pairs += [(self.rec[:, slots, k], field[:, columns]) for k, field in enumerate(self.fields)]
            for out, value in pairs:
                if value.dtype == F32:
                    out = out.bitcast(F32)
                p.nc.gpsimd.tensor_copy(out, value).then_inc(self.s_slot[h], 1)

        def send(h):
            for u in range(h * SE, (h + 1) * SE):
                pool.indirect_dma_start(self.table, bass.IndirectOffsetOnAxis(ap=self.addr[:, u:u + 1], axis=0),
                                        self.rec[:, u, :], None, bounds_check=P * QW - 1,
                                        oob_is_err=False).then_inc(self.s_sent[h], 16)

        for n, (first, end, gate) in enumerate(parts):
            if gate is not None:
                pool.wait_ge(*gate)
            if n == 0:
                for h in range(SGROUPS):
                    fill(h, start)
                    pool.wait_ge(self.s_slot[h], copies)
                    send(h)
                first += 1
            with pool.Fori(first - start - 1, end - start - 1) as k:
                for h in range(SGROUPS):
                    ready(self.s_sent[h], 16 * SE * k + 16 * SE, 2 * (SGROUPS * k + h))
                    pool.wait_ge(self.s_idle, 2 * (SGROUPS * k + h) + 2)
                    fill(h, start + 1 + k)
                    ready(self.s_slot[h], copies * k + 2 * copies, 2 * (SGROUPS * k + h) + 1)
                    send(h)
        for h in range(SGROUPS):
            pool.wait_ge(self.s_sent[h], 16 * SE * (parts[-1][1] - start))


def second_scatter(p, ctx):
    return Scatter(p, ctx, p.table1, p.addr1, [p.rec1, p.weight1])


def gnn_dense(p, wk, mean_of_edges, row_bias, gamma, beta, func, residual, copy, scatters):
    nc, v = p.nc, p.nc.vector
    with ExitStack() as ctx:
        deg = p.sb("g_deg", [P, NT], F32, ctx)
        norm, norm2 = RowNorm(p, ctx), RowNorm(p, ctx)

        def put(t, slots):
            a, x = flat(p.acc[:, bass.ds(t, 1), 0:D]), flat(p.xb[:, bass.ds(t, 1), :])
            if mean_of_edges:
                return [v.scalar_tensor_tensor(out=slots[0], in0=a, scalar=deg[:, bass.ds(t, 1)], in1=x,
                                               op0=ALU.mult, op1=ALU.add)]
            return [v.tensor_copy(slots[0], a)]

        def take(t, psum):
            plus = row_bias[:] if mean_of_edges else flat(p.xb[:, bass.ds(t, 1), :])
            return v.tensor_tensor(flat(p.acc[:, bass.ds(t, 1), 0:D]), psum[:, 0:D], plus, ALU.add)

        def then(t):
            return norm.take(flat(p.acc[:, bass.ds(t, 1), 0:D]), t)

        pr = Project(p, ctx, [[p.wT[:, wk, kb, :] for kb in range(KB)]], D, put, take, then)
        old, scaled = pr.slots[:, :, 0, :], pr.flip[:, :, 0:D]
        active, centered = p.sb("g_active", [P, U, D], F32, ctx), p.sb("g_centered", [P, U, D], F32, ctx)
        s = lambda name: p.sem("g_" + name, ctx)
        s_dve, s_scaled, s_active = s("s_dve"), s("s_scaled"), s("s_active")
        s_summed, s_centered, s_copy = s("s_summed"), s("s_centered"), s("s_copy")
        s_old = [s(f"s_old{u}") for u in range(U)]
        if scatters is not None:
            scatter = second_scatter(p, ctx)
        block = ctx.enter_context(nc.Block())

        @block.vector
        def _(dve):
            c = Chain(dve, s_dve)
            if mean_of_edges:
                c.link(v.tensor_scalar(deg[:], p.acc[:, :, D], 1.0, None, ALU.max))
                c.link(v.reciprocal(deg[:], deg[:]))
            pr.dve(dve, c)
            norm.finish(dve, c)

            def center(t, u):
                v.scalar_tensor_tensor(out=centered[:, u, :], in0=flat(p.acc[:, bass.ds(t, 1), 0:D]),
                                       scalar=norm.mean[:, bass.ds(t, 1)], in1=gamma[:], op0=ALU.subtract,
                                       op1=ALU.mult).then_inc(s_centered, 1)

            def scale(t, u):
                dve.wait_ge(s_centered, t + 1)
                v.scalar_tensor_tensor(out=scaled[:, u, :], in0=centered[:, u, :], scalar=norm.rstd[:, bass.ds(t, 1)],
                                       in1=beta[:], op0=ALU.mult, op1=ALU.add).then_inc(s_scaled, 1)

            center(0, 0)
            center(1, 1)
            scale(0, 0)

            def tile(t, u, more):
                x = flat(p.acc[:, bass.ds(t, 1), 0:D])
                if more >= 1:
                    scale(t + 1, (u + 1) % U)
                dve.wait_ge(s_active, t + 1)
                if residual is not None:
                    dve.wait_ge(s_old[u], 16 * pr.i + 16)
                    v.tensor_tensor(x, active[:, u, :], old[:, u, :], ALU.add).then_inc(s_summed, 1)
                if more >= 2:
                    center(t + 2, (u + 2) % U)
                if residual is not None:
                    dve.wait_ge(s_summed, t + 1)
                    if u == 0:
                        if isinstance(pr.i, int):
                            c.leave(STEPS - 1)
                        else:
                            c.enter(pr.i, U)
                    c.done(norm2.take(x, t))

            pr.steps(dve, tile)
            if residual is not None:
                c.settle()
                norm2.finish(dve, c)
                norm2.apply(dve, p.acc, p.xb)

        @block.tensor
        def _(pe):
            pr.pe(pe)

        @block.scalar
        def _(act):
            pr.act(act)
            norm.root(act)
            with act.Fori(0, STEPS) as i:
                for u in range(U):
                    act.wait_ge(s_scaled, U * i + u + 1)
                    out = flat(p.xb[:, bass.ds(U * i + u, 1), :]) if residual is None else active[:, u, :]
                    nc.scalar.activation(out, scaled[:, u, :], func).then_inc(s_active, 1)
            if residual is not None:
                norm2.root(act)
                norm2.apply_rest(act, p.acc, p.xb)

        if scatters is not None:
            @block.gpsimd
            def _(pool):
                scatter.run(pool, [(*scatters, None)])

        if residual is None:
            @block.sync
            def _(sp):
                send_steps(sp, [(s_active, U)], copy, p.xb, s_copy)
                sp.wait_ge(s_copy, 16 * STEPS)
        else:
            @block.sync
            def _(sp):
                sp.wait_ge(pr.s_taken, NT + 3)
                for u in range(U):
                    sp.dma_start(old[:, u, :], rows(residual, u)).then_inc(s_old[u], 16)
                with sp.Fori(0, STEPS - 2) as i:
                    for u in range(U):
                        sp.wait_ge(s_summed, U * i + u + 1)
                        sp.dma_start(old[:, u, :], residual[bass.ds(P * (U * i + U + u), P), :]).then_inc(s_old[u], 16)
                for u in range(U):
                    t = U * (STEPS - 1) + u
                    n = LAST if t == NT - 1 else P
                    sp.wait_ge(s_summed, t - U + 1)
                    sp.dma_start(old[0:n, u, :], rows(residual, t, n)).then_inc(s_old[u], 16)



def route_to_experts(p):
    nc, v = p.nc, p.nc.vector
    with ExitStack() as outer:
        logits = p.sb("r_logits", [P, NT, EX], F32, outer)
        with ExitStack() as ctx:
            def put(t, slots):
                return [v.tensor_copy(slots[0], flat(p.xb[:, bass.ds(t, 1), :]))]

            def take(t, psum):
                return v.tensor_tensor(flat(logits[:, bass.ds(t, 1), :]), psum[:, 0:EX], p.br[:], ALU.add)

            def then(t):
                return p.norm_in.take(flat(p.xb[:, bass.ds(t, 1), :]), t)

            pr = Project(p, ctx, [[p.Wr[:, kb, :] for kb in range(KB)]], EX, put, take, then)
            s_dve = p.sem("r_s_dve", ctx)
            block = ctx.enter_context(nc.Block())

            @block.vector
            def _(dve):
                c = Chain(dve, s_dve)
                pr.dve(dve, c)
                p.norm_in.finish(dve, c)

            @block.tensor
            def _(pe):
                pr.pe(pe)

            @block.scalar
            def _(act):
                pr.act(act)
                p.norm_in.root(act)

        with ExitStack() as ctx:
            names = ("expert", "cap", "rest", "hot0", "hot1", "tmp", "place")
            expert, cap, rest, hot0, hot1, tmp, place = (p.sb("r_" + n, [P, NT, EX], F32, ctx) for n in names)
            top = [p.sb(f"r_top{k}", [P, NT], F32, ctx) for k in range(TOP)]
            first = p.sb("r_first", [P, NT], F32, ctx)
            gap = p.sb("r_gap", [P, NT], F32, ctx)
            past, valid, where = (p.sb("r_" + n, [P, NT], F32, ctx) for n in ("past", "valid", "where"))
            ones = p.sb("r_ones", [P, NT], F32, ctx)
            b = Binning(p, ctx, EX, MOE_TILES)
            s_dve, s_gap, s_exp = (p.sem("r2_" + n, ctx) for n in ("s_dve", "s_gap", "s_exp"))
            block = ctx.enter_context(nc.Block())

            def wide(ap):
                return ap.unsqueeze(2).to_broadcast([P, NT, EX])

            @block.tensor
            def _(pe):
                b.products(pe, 0, None, b.s_count)

            @block.scalar
            def _(act):
                act.wait_ge(s_gap, 1)
                nc.scalar.activation(gap[:], gap[:], ACT.Exp).then_inc(s_exp, 1)

            @block.vector
            def _(dve):
                c = Chain(dve, s_dve)
                c.link(v.tensor_scalar(expert[:, 0, :], p.iota[:, 0:EX], -float(EX), None, ALU.add))
                c.link(v.tensor_copy(expert[:, 1:NT, :], expert[:, 0:1, :].to_broadcast([P, NT - 1, EX])))
                c.done(v.memset(ones[:], 1.0))
                c.done(v.memset(p.place_i[:], 0))
                c.done(v.tensor_scalar(valid[:], p.node_no[:], float(N), None, ALU.is_lt))
                c.done(v.tensor_scalar(past[:], p.node_no[:], float(N), None, ALU.is_ge))
                c.done(v.tensor_scalar(gap[:, 0:1], p.part_no[:], float(MOE_TILES * FT), None, ALU.add))
                c.settle()
                c.link(v.tensor_scalar(past[:], past[:], gap[:, 0:1], None, ALU.mult))
                values = logits
                for k, hot in enumerate((hot0, hot1)):
                    c.link(v.tensor_reduce(top[k][:], values[:], AX, ALU.max))
                    c.link(v.tensor_tensor(tmp[:], values[:], wide(top[k][:]), ALU.is_equal))
                    c.link(v.tensor_tensor(tmp[:], tmp[:], expert[:], ALU.mult))
                    c.link(v.tensor_reduce(first[:], tmp[:], AX, ALU.min))
                    c.link(v.tensor_tensor(hot[:], expert[:], wide(first[:]), ALU.is_equal))
                    if k == 0:
                        c.link(v.tensor_scalar(cap[:], hot[:], -2.0, 1.0, ALU.mult, ALU.add))
                        c.link(v.tensor_scalar(cap[:], cap[:], 3.0e38, None, ALU.mult))
                        c.link(v.tensor_tensor(rest[:], logits[:], cap[:], ALU.min))
                        values = rest
                v.tensor_tensor(gap[:], top[1][:], top[0][:], ALU.subtract).then_inc(s_gap, 1)
                for hot in (hot0, hot1):
                    c.done(v.tensor_tensor(hot[:], hot[:], wide(valid[:]), ALU.mult))
                c.settle()
                c.link(v.tensor_tensor(tmp[:], hot0[:], hot1[:], ALU.add))
                v.tensor_reduce(b.count[:], tmp[:].rearrange("p t e -> p e t"), AX, ALU.add).then_inc(b.s_count, 1)
                b.starts(dve, c, 0, 8, FT)
                for e in range(EX):
                    c.done(v.tensor_tensor_scan(place[:, :, e], ones[:], tmp[:, :, e], b.start[:, e:e + 1],
                                                ALU.mult, ALU.add))
                c.settle()
                for k, hot in enumerate((hot0, hot1)):
                    c.link(v.tensor_tensor(tmp[:], hot[:], place[:], ALU.mult))
                    c.link(v.tensor_reduce(where[:], tmp[:], AX, ALU.add))
                    c.link(v.tensor_tensor(where[:], where[:], past[:], ALU.add))
                    c.link(v.tensor_copy(p.place_i[:, k, 0:NT], where[:]))
                b.table(dve, c, 0, p.expert_of)
                dve.wait_ge(s_exp, 1)
                c.link(v.tensor_scalar(p.share[:, 0, :], gap[:], 1.0, None, ALU.add))
                c.link(v.reciprocal(p.share[:, 0, :], p.share[:, 0, :]))
                c.link(v.tensor_tensor(p.share[:, 1, :], gap[:], p.share[:, 0, :], ALU.mult))


def dispatch(p, into, places, choices, normed):
    nc, v = p.nc, p.nc.vector
    with ExitStack() as ctx:
        row = p.sb("d_row", [P, U, D], F32, ctx)
        slot = p.sb("d_slot", [P, U, TOP], I32, ctx)
        s = lambda name: p.sem("d_" + name, ctx)
        s_idle, s_start = s("s_idle"), s("s_start")
        s_full = [s(f"s_full{u}") for u in range(U)]
        s_sent = [s(f"s_sent{u}") for u in range(U)]
        block = ctx.enter_context(nc.Block())

        @block.vector
        def _(dve):
            def fill(t, u):
                x = flat(p.xb[:, bass.ds(t, 1), :])
                if normed:
                    v.tensor_scalar(row[:, u, :], x, p.norm_in.mean[:, bass.ds(t, 1)],
                                    p.norm_in.rstd[:, bass.ds(t, 1)], ALU.subtract, ALU.mult).then_inc(s_full[u], 1)
                else:
                    v.tensor_copy(row[:, u, :], x).then_inc(s_full[u], 1)
                for k in range(choices):
                    v.tensor_copy(slot[:, u, k:k + 1], p.place_i[:, k, bass.ds(t, 1)]).then_inc(s_full[u], 1)

            for u in range(U):
                fill(u, u)
            with dve.Fori(0, STEPS - 1) as i:
                for u in range(U):
                    dve.wait_ge(s_sent[u], 16 * choices * i + 16 * choices)
                    fill(U * i + U + u, u)

        @block.gpsimd
        def _(pool):
            ready = PoolWait(p, pool, s_idle)
            with pool.Fori(0, STEPS) as i:
                for u in range(U):
                    ready(s_full[u], (choices + 1) * i + choices + 1, U * i + u)
                    for k in range(choices):
                        pool.indirect_dma_start(into[0:places, :], bass.IndirectOffsetOnAxis(ap=slot[:, u, k:k + 1], axis=0),
                                                row[:, u, :], None, bounds_check=places - 1,
                                                oob_is_err=False).then_inc(s_sent[u], 16)
            for u in range(U):
                pool.wait_ge(s_sent[u], 16 * choices * STEPS)


def combine(p, source, choices, add_xb, share, norm, sent, normed, last):
    nc, v = p.nc, p.nc.vector
    with ExitStack() as ctx:
        got = p.sb("c_got", [P, U, TOP, D], F32, ctx)
        slot = p.sb("c_slot", [P, U, TOP], I32, ctx)
        s = lambda name: p.sem("c_" + name, ctx)
        s_idle, s_dve, s_sent = s("s_idle"), s("s_dve"), s("s_sent")
        per_tile = choices + int(add_xb) + int(norm is not None)
        s_slot = [s(f"s_slot{u}") for u in range(U)]
        s_got = [s(f"s_got{u}") for u in range(U)]
        block = ctx.enter_context(nc.Block())

        @block.vector
        def _(dve):
            c = Chain(dve, s_dve)

            def fill(t, u):
                for k in range(choices):
                    v.tensor_copy(slot[:, u, k:k + 1], p.place_i[:, k, bass.ds(t, 1)]).then_inc(s_slot[u], 1)

            for u in range(U):
                fill(u, u)
            with dve.Fori(0, STEPS) as i:
                c.enter(i, U * per_tile)
                for u in range(U):
                    t = U * i + u
                    x = flat(p.acc[:, bass.ds(t, 1), 0:D])
                    if add_xb:
                        c.link(v.tensor_tensor(x, x, flat(p.xb[:, bass.ds(t, 1), :]), ALU.add))
                    dve.wait_ge(s_got[u], 16 * choices * i + 16 * choices)
                    for k in range(choices - 1):
                        c.link(v.scalar_tensor_tensor(out=x, in0=got[:, u, k, :], scalar=share[:, k, bass.ds(t, 1)],
                                                      in1=x, op0=ALU.mult, op1=ALU.add))
                    k = choices - 1
                    c.done(v.scalar_tensor_tensor(out=x, in0=got[:, u, k, :], scalar=share[:, k, bass.ds(t, 1)],
                                                  in1=x, op0=ALU.mult, op1=ALU.add))
                    c.settle()
                    fill(t + U, u)
                    if norm is not None:
                        c.done(norm.take(x, t))
            c.leave(STEPS)
            if norm is not None:
                c.settle()
                norm.finish(dve, c)
                norm.apply(dve, p.acc, p.xb)

        @block.sync
        def _(sp):
            done_per = U * per_tile
            with sp.Fori(0, STEPS - 1) as i:
                sp.wait_ge(s_dve, done_per * i + done_per)
                sp.dma_start(sent[bass.ds(P * U * i, P * U), :].rearrange("(t p) d -> p t d", p=P),
                             p.acc[:, bass.ds(U * i, U), 0:D]).then_inc(s_sent, 16)
            sp.wait_ge(s_dve, done_per * STEPS)
            first = U * (STEPS - 1)
            sp.dma_start(tiles(sent, first, NT - 1), p.acc[:, first:NT - 1, 0:D]).then_inc(s_sent, 16)
            sp.dma_start(rows(sent, NT - 1, last), p.acc[0:last, NT - 1, 0:D]).then_inc(s_sent, 16)
            sends = STEPS + 1
            if norm is not None:
                send_steps(sp, norm.made(), normed, p.xb, s_sent)
                sends += STEPS
            sp.wait_ge(s_sent, 16 * sends)

        @block.gpsimd
        def _(pool):
            ready = PoolWait(p, pool, s_idle)
            with pool.Fori(0, STEPS) as i:
                for u in range(U):
                    ready(s_slot[u], choices * i + choices, U * i + u)
                    for k in range(choices):
                        pool.indirect_dma_start(got[:, u, k, :], None, source,
                                                bass.IndirectOffsetOnAxis(ap=slot[:, u, k:k + 1], axis=0)).then_inc(s_got[u], 16)

        if norm is not None:
            @block.scalar
            def _(act):
                norm.root(act)
                norm.apply_rest(act, p.acc, p.xb)



def ffn(p, source, result, count, weights, experts, func, scatters):
    nc, v = p.nc, p.nc.vector
    W1, W2, b1, b2 = weights
    with ExitStack() as ctx:
        wslots = 2 if experts else 1
        size = wslots * KB * H
        if experts:
            room = p.xb[:].rearrange("p t d -> p (t d)")
        else:
            room = p.sb("f_weights", [P, 2 * size], F32, ctx)
        w1 = room[:, 0:size].rearrange("p (s b h) -> p s b h", s=wslots, b=KB)
        w2 = room[:, size:2 * size].rearrange("p (s b d) -> p s b d", s=wslots, b=HB)
        xin = p.sb("f_xin", [P, 2, 2, D], F32, ctx)
        xT = p.sb("f_xT", [P, KB, FT], F32, ctx)
        hT = p.sb("f_hT", [P, 2, HB, FT], F32, ctx)
        y = p.sb("f_y", [P, 2, 2, D], F32, ctx)
        ps_x = p.ps("f_ps_x", [P, KB, FT], ctx)
        ps_h = [p.ps(f"f_ps_h{i}", [P, 512], ctx) for i in range(4)]
        ps_y = [p.ps(f"f_ps_y{i}", [P, 512], ctx) for i in range(2)]
        s = lambda name: p.sem("f_" + name, ctx)
        s_x = [s(f"s_x{i}") for i in range(2)]
        s_w = [s(f"s_w{i}") for i in range(2)]
        s_out = [s(f"s_out{i}") for i in range(2)]
        s_flip, s_xT, s_up, s_act, s_down, s_y = (s(n) for n in ("s_flip", "s_xT", "s_up", "s_act", "s_down", "s_y"))
        if scatters is not None:
            scatter = second_scatter(p, ctx)
        block = ctx.enter_context(nc.Block())
        pairs = (count - 3) // 2
        rest = count - 2 - 2 * pairs

        def over_tiles(eng, tile):
            for t in range(2):
                tile(t, t, 0, t == 0, False)
            with eng.Fori(0, pairs) as i:
                for k in range(2):
                    tile(2 * i + 2 + k, k, i + 1, False, False)
            for t in range(count - rest, count):
                tile(t, t % 2, t // 2, False, t == count - 1)

        def expert(eng, t):
            return eng.value_load(p.expert_of[0:1, bass.ds(t, 1)], min_val=0, max_val=EX - 1)

        @block.sync
        def _(sp):
            x_dram = source.rearrange("(t p c) d -> t p c d", p=P, c=2)
            y_dram = result[0:count * FT, :].rearrange("(t p c) d -> t p c d", p=P, c=2)

            def at(ap, t):
                return ap[bass.ds(t, 1)].rearrange("a p c d -> (a p) c d")

            def load(t, k):
                sp.dma_start(xin[:, k, :, :], at(x_dram, t)).then_inc(s_x[k], 16)
                if experts:
                    e = expert(sp, t)
                    sp.dma_start(w1[:, k, :, :], W1[bass.ds(e, 1)].rearrange("a (b p) h -> (a p) b h", p=P)).then_inc(s_w[k], 16)
                    sp.dma_start(w2[:, k, :, :], W2[bass.ds(e, 1)].rearrange("a (b p) d -> (a p) b d", p=P)).then_inc(s_w[k], 16)

            if not experts:
                sp.dma_start(w1[:, 0, :, :], W1.rearrange("(b p) h -> p b h", p=P)).then_inc(s_w[0], 16)
                sp.dma_start(w2[:, 0, :, :], W2.rearrange("(b p) d -> p b d", p=P)).then_inc(s_w[0], 16)
            load(0, 0)
            load(1, 1)

            def tile(t, k, uses, first, last, more=True):
                sp.wait_ge(s_down, t + 1)
                if more:
                    load(t + 2, k)
                sp.wait_ge(s_y, 2 * t + 2)
                sp.dma_start(at(y_dram, t), y[:, k, :, :]).then_inc(s_out[k], 16)

            ahead = (count - 2) // 2
            with sp.Fori(0, ahead) as i:
                for k in range(2):
                    tile(2 * i + k, k, None, False, False)
            for t in range(2 * ahead, count):
                tile(t, t % 2, None, False, False, more=t + 2 < count)
            for k in range(2):
                sp.wait_ge(s_out[k], 16 * ((count + 1 - k) // 2))

        @block.tensor
        def _(pe):
            def flip(t, k, uses):
                pe.wait_ge(s_x[k], 16 * uses + 16)
                for blk in range(2):
                    for kb in range(KB):
                        last = nc.tensor.transpose(ps_x[:, kb, blk * P:(blk + 1) * P],
                                                   xin[:, k, blk, kb * P:(kb + 1) * P], p.ident[:])
                last.then_inc(s_flip, 1)

            flip(0, 0, 0)

            def tile(t, k, uses, first, last):
                wk = k if experts else 0
                pe.wait_ge(s_xT, 2 * t + 2)
                pe.wait_ge(s_w[wk], 32 * uses + 32 if experts else 32)
                for j in range(HB):
                    if not (first and j < 4):
                        pe.wait_ge(s_act, HB * t + j - 3)
                    for kb in range(KB):
                        mm = nc.tensor.matmul(ps_h[j % 4][:, 0:FT], w1[:, wk, kb, j * P:(j + 1) * P], xT[:, kb, :],
                                              start=(kb == 0), stop=(kb == KB - 1))
                    mm.then_inc(s_up, 1)
                if not last:
                    flip(t + 1, 1 - k, uses + (1 if k == 1 else 0))
                if not first:
                    pe.wait_ge(s_y, 2 * t)
                for j in range(HB):
                    pe.wait_ge(s_act, HB * t + j + 1)
                    for blk in range(2):
                        mm = nc.tensor.matmul(ps_y[blk][:, 0:D], hT[:, k, j, blk * P:(blk + 1) * P], w2[:, wk, j, :],
                                              start=(j == 0), stop=(j == HB - 1))
                mm.then_inc(s_down, 1)

            over_tiles(pe, tile)

        @block.scalar
        def _(act):
            def tile(t, k, uses, first, last):
                if experts:
                    e = expert(act, t)
                for j in range(HB):
                    bias = flat(b1[:, bass.ds(e, 1), j:j + 1]) if experts else b1[:, j:j + 1]
                    act.wait_ge(s_up, HB * t + j + 1)
                    nc.scalar.activation(hT[:, k, j, :], ps_h[j % 4][:, 0:FT], func, bias=bias).then_inc(s_act, 1)

            over_tiles(act, tile)

        @block.vector
        def _(dve):
            def evacuate(t):
                if experts:
                    e = expert(dve, t)
                dve.wait_ge(s_flip, t + 1)
                for kb in range(KB):
                    if experts:
                        ins = v.tensor_scalar(xT[:, kb, :], ps_x[:, kb, :], p.ln_g[:, kb, bass.ds(e, 1)],
                                              p.ln_b[:, kb, bass.ds(e, 1)], ALU.mult, ALU.add)
                    else:
                        ins = v.tensor_copy(xT[:, kb, :], ps_x[:, kb, :])
                    ins.then_inc(s_xT, 1)

            evacuate(0)

            def tile(t, k, uses, first, last):
                if not last:
                    evacuate(t + 1)
                if experts:
                    e = expert(dve, t)
                dve.wait_ge(s_down, t + 1)
                if not (isinstance(uses, int) and uses == 0):
                    dve.wait_ge(s_out[k], 16 * uses)
                for blk in range(2):
                    bias = flat(b2[:, bass.ds(e, 1), :]) if experts else b2[:]
                    v.tensor_tensor(y[:, k, blk, :], ps_y[blk][:, 0:D], bias, ALU.add).then_inc(s_y, 1)

            over_tiles(dve, tile)

        if scatters is not None:
            @block.gpsimd
            def _(pool):
                scatter.run(pool, [(*scatters, None)])



def choose_larger_half(p):
    nc, v = p.nc, p.nc.vector
    with ExitStack() as outer:
        weight = p.share[:, 0, :]
        with ExitStack() as ctx:
            def put(t, slots):
                return [v.tensor_copy(slots[0], flat(p.xb[:, bass.ds(t, 1), :]))]

            def take(t, psum):
                return v.tensor_tensor(p.share[:, 0, bass.ds(t, 1)], psum[:, 0:1], p.mod_br[:], ALU.add)

            pr = Project(p, ctx, [[p.mod_wr[:, kb, :] for kb in range(KB)]], 1, put, take, None)
            s_dve = p.sem("h_s_dve", ctx)
            block = ctx.enter_context(nc.Block())

            @block.vector
            def _(dve):
                pr.dve(dve, Chain(dve, s_dve))

            @block.tensor
            def _(pe):
                pr.pe(pe)

            @block.scalar
            def _(act):
                pr.act(act)

        with ExitStack() as ctx:
            bits, sign, part = (p.sb("h_" + n, [P, NT], I32, ctx) for n in ("bits", "sign", "part"))
            high, low, hit, above, tie, ties, sel, ones, past, scan, carry = (
                p.sb("h_" + n, [P, NT], F32, ctx)
                for n in ("high", "low", "hit", "above", "tie", "ties", "sel", "ones", "past", "scan", "carry"))
            cell = p.sb("h_cell", [P, 12], F32, ctx)
            many = p.sb("h_many", [P, WAYS, NT], F32, ctx)
            nums, enough, steps_up = (p.sb("h_" + n, [P, WAYS], F32, ctx)
                                              for n in ("nums", "enough", "steps_up"))
            ps_n = p.ps("h_ps_n", [P, 512], ctx)
            s_dve, s_n, s_sum = (p.sem("h2_" + n, ctx) for n in ("s_dve", "s_n", "s_sum"))
            block = ctx.enter_context(nc.Block())
            at, num, goal, over, start = (cell[:, k:k + 1] for k in range(5))

            @block.tensor
            def _(pe):
                for r in range(2):
                    for n in range(ROUNDS):
                        pe.wait_ge(s_n, (ROUNDS + 1) * r + n + 1)
                        nc.tensor.matmul(ps_n[:, 0:WAYS], p.ones[:], nums[:], start=True, stop=True).then_inc(s_sum, 1)
                    pe.wait_ge(s_n, (ROUNDS + 1) * (r + 1))
                    nc.tensor.matmul(ps_n[:, 0:1], p.ones[:], num, start=True, stop=True).then_inc(s_sum, 1)
                pe.wait_ge(s_n, 2 * ROUNDS + 3)
                nc.tensor.matmul(ps_n[:, 64:64 + NT], p.before[:], tie[:], start=True, stop=True)
                nc.tensor.matmul(ps_n[:, 128:128 + NT], p.ones[:], tie[:], start=True, stop=True).then_inc(s_sum, 1)
                pe.wait_ge(s_n, 2 * ROUNDS + 4)
                nc.tensor.matmul(ps_n[:, 0:1], p.before[:], num, start=True, stop=True).then_inc(s_sum, 1)

            @block.vector
            def _(dve):
                c = Chain(dve, s_dve)
                wi = weight.bitcast(I32)
                c.link(v.tensor_single_scalar(sign[:], wi, 31, ALU.arith_shift_right))
                c.link(v.tensor_single_scalar(sign[:], sign[:], 0x7FFFFFFF, ALU.bitwise_and))
                c.link(v.tensor_tensor(bits[:], wi, sign[:], ALU.bitwise_xor))
                c.link(v.tensor_single_scalar(part[:], bits[:], 16, ALU.arith_shift_right))
                c.link(v.tensor_copy(high[:], part[:]))
                c.link(v.tensor_single_scalar(part[:], bits[:], 0xFFFF, ALU.bitwise_and))
                c.link(v.tensor_copy(low[:], part[:]))
                c.link(v.tensor_scalar(past[:], p.node_no[:], float(N), None, ALU.is_ge))
                c.link(v.tensor_scalar(scan[:], past[:], -200000.0, None, ALU.mult))
                c.link(v.tensor_tensor(high[:], high[:], scan[:], ALU.add))
                c.done(v.memset(goal, float(KEEP)))
                c.done(v.memset(ones[:], 1.0))
                c.done(v.memset(p.place_i[:], 0))
                c.settle()

                def search(r, values, first):
                    c.link(v.memset(at, first))
                    for n in range(ROUNDS):
                        step = float((WAYS + 1) ** (ROUNDS - 1 - n))
                        c.link(v.tensor_scalar(steps_up[:], p.iota[:, 1:WAYS + 1], step, at, ALU.mult, ALU.add))
                        c.link(v.tensor_tensor(many[:], values.unsqueeze(1).to_broadcast([P, WAYS, NT]),
                                               steps_up[:].unsqueeze(2).to_broadcast([P, WAYS, NT]), ALU.is_ge))
                        v.tensor_reduce(nums[:], many[:], AX, ALU.add).then_inc(s_n, 1)
                        dve.wait_ge(s_sum, (ROUNDS + 1) * r + n + 1)
                        c.link(v.tensor_scalar(enough[:], ps_n[:, 0:WAYS], goal, None, ALU.is_ge, ALU.add,
                                               accum_out=over))
                        c.link(v.scalar_tensor_tensor(out=at, in0=over, scalar=step, in1=at, op0=ALU.mult,
                                                      op1=ALU.add))
                    v.tensor_scalar(hit[:], values, at, None, ALU.is_gt, ALU.add, accum_out=num).then_inc(s_n, 1)
                    dve.wait_ge(s_sum, (ROUNDS + 1) * (r + 1))
                    c.link(v.tensor_tensor(goal, goal, ps_n[:, 0:1], ALU.subtract))

                search(0, high[:], -32768.0)
                c.done(v.tensor_scalar(above[:], high[:], at, None, ALU.is_gt))
                c.done(v.tensor_scalar(tie[:], high[:], at, None, ALU.is_equal))
                c.settle()
                c.link(v.tensor_scalar(low[:], low[:], 1.0, None, ALU.add))
                c.link(v.tensor_tensor(low[:], low[:], tie[:], ALU.mult))
                c.link(v.tensor_scalar(low[:], low[:], -1.0, None, ALU.add))
                search(1, low[:], 0.0)
                c.done(v.tensor_scalar(scan[:], low[:], at, None, ALU.is_gt))
                c.settle()
                c.link(v.tensor_tensor(above[:], above[:], scan[:], ALU.add))
                v.tensor_scalar(tie[:], low[:], at, None, ALU.is_equal).then_inc(s_n, 1)
                dve.wait_ge(s_sum, 2 * ROUNDS + 3)
                c.link(v.tensor_copy(carry[:], ps_n[:, 128:128 + NT]))
                c.link(v.tensor_tensor_scan(ties[:], ones[:], carry[:], 0.0, ALU.mult, ALU.add))
                c.link(v.tensor_tensor(ties[:], ties[:], carry[:], ALU.subtract))
                c.link(v.tensor_tensor(ties[:], ties[:], ps_n[:, 64:64 + NT], ALU.add))
                c.link(v.tensor_scalar(ties[:], ties[:], goal, None, ALU.is_lt))
                c.link(v.tensor_tensor(ties[:], ties[:], tie[:], ALU.mult))
                c.link(v.tensor_tensor(sel[:], above[:], ties[:], ALU.add))
                v.tensor_scalar(hit[:], sel[:], 0.0, None, ALU.add, ALU.add, accum_out=num).then_inc(s_n, 1)
                dve.wait_ge(s_sum, 2 * ROUNDS + 4)
                c.link(v.tensor_scalar(start, ps_n[:, 0:1], -1.0, None, ALU.add))
                c.link(v.tensor_tensor_scan(scan[:], ones[:], sel[:], start, ALU.mult, ALU.add))
                c.link(v.tensor_tensor(scan[:], scan[:], sel[:], ALU.mult))
                c.link(v.tensor_scalar(over, p.part_no[:], float(MOD_TILES * FT), None, ALU.add))
                c.link(v.tensor_scalar(hit[:], sel[:], -1.0, 1.0, ALU.mult, ALU.add))
                c.link(v.tensor_scalar(hit[:], hit[:], over, None, ALU.mult))
                c.link(v.tensor_tensor(scan[:], scan[:], hit[:], ALU.add))
                c.link(v.tensor_copy(p.place_i[:, 0, 0:NT], scan[:]))



INS = ["x", "src", "dst", "edge_weight", "L0_gnn_W0", "L0_gnn_b0", "L0_gnn_g0", "L0_gnn_beta0", "L0_gnn_W1",
       "L0_gnn_b1", "L0_gnn_g1", "L0_gnn_beta1", "L0_ffn_Wr", "L0_ffn_br", "L0_ffn_ln_g", "L0_ffn_ln_b",
       "L0_ffn_W1", "L0_ffn_b1", "L0_ffn_W2", "L0_ffn_b2", "L1_gnn_W_self", "L1_gnn_b_self", "L1_gnn_W_msg",
       "L1_gnn_b_msg", "L1_gnn_ln_gamma", "L1_gnn_ln_beta", "L1_ffn_wr", "L1_ffn_br", "L1_ffn_w1", "L1_ffn_b1",
       "L1_ffn_w2", "L1_ffn_b2"]


def columns(ap):
    return ap.rearrange("(b p) -> p b", p=P)


def build(nc, io, out):
    dram = {name: nc.dram_tensor(name, shape, dt).ap() for name, shape, dt in (
        ("table0", (P * QW, 1), I32), ("table1", (P * QW, 2), I32), ("xn", (NT * P, D), F32),
        ("h1", (NT * P, D), F32), ("x2", (NT * P, D), F32),
        ("moe_in", (MOE_TILES * FT, D), F32), ("moe_out", (MOE_TILES * FT + P, D), F32),
        ("mod_in", (MOD_TILES * FT, D), F32), ("mod_out", (MOD_TILES * FT + P, D), F32))}
    with ExitStack() as ctx:
        p = Program(nc, ctx)
        p.ident, p.before, p.upto, p.ones, p.iota = (p.sb(n, [P, P]) for n in ("ident", "before", "upto", "ones", "iota"))
        p.chunk_no, p.part_no, p.node_no = p.sb("chunk_no", [P, NCH]), p.sb("part_no", [P, 1]), p.sb("node_no", [P, NT])
        p.eps, p.idle = p.sb("eps", [P, 1]), p.sb("idle", [1, 2])
        p.acc, p.xb = p.sb("acc", [P, NT, D + 1]), p.sb("xb", [P, NT, D])
        p.edge_row, p.edge_local, p.edge_weight = p.sb("edge_row", [P, QW], I32), p.sb("edge_local", [P, QW]), p.sb("edge_weight", [P, QW])
        p.addr1, p.rec1, p.weight1 = p.sb("addr1", [P, EC], I32), p.sb("rec1", [P, EC], I32), p.sb("weight1", [P, EC])
        p.place_i, p.share, p.expert_of = p.sb("place_i", [P, TOP, NT + U], I32), p.sb("share", [P, TOP, NT]), p.sb("expert_of", [1, MOE_TILES], I32)
        p.wT, p.Wr, p.mod_wr = p.sb("wT", [P, 4, KB, D]), p.sb("Wr", [P, KB, EX]), p.sb("mod_wr", [P, KB, 1])
        p.br, p.mod_br = p.sb("br", [P, EX]), p.sb("mod_br", [P, 1])
        p.ln_g, p.ln_b = p.sb("ln_g", [P, KB, EX]), p.sb("ln_b", [P, KB, EX])
        p.moe_b1, p.moe_b2, p.mod_b1 = p.sb("moe_b1", [P, EX, HB]), p.sb("moe_b2", [P, EX, D]), p.sb("mod_b1", [P, HB])
        row_params = {name: p.sb("row_" + name, [P, D]) for name in
                      ("L0_gnn_b0", "L0_gnn_b1", "L1_gnn_b_self", "L1_gnn_b_msg", "L0_gnn_g0", "L0_gnn_g1",
                       "L1_gnn_ln_gamma", "L0_gnn_beta0", "L0_gnn_beta1", "L1_gnn_ln_beta", "L1_ffn_b2")}
        p.tile_of = [p.sb(f"tile_of{k}", [1, NCH], I32) for k in range(2)]
        p.norm_in, p.norm_out = RowNorm(p, ctx), RowNorm(p, ctx)
        p.table1 = dram["table1"]
        p.small = [(p.Wr[:], io["L0_ffn_Wr"].rearrange("(b p) e -> p b e", p=P)),
                   (p.br[:], io["L0_ffn_br"].partition_broadcast(P)),
                   (p.mod_br[:], io["L1_ffn_br"].partition_broadcast(P)),
                   (p.mod_wr[:], io["L1_ffn_wr"].rearrange("(b p) e -> p b e", p=P)),
                   (p.mod_b1[:], columns(io["L1_ffn_b1"]))]
        for e in range(EX):
            p.small += [(p.ln_g[:, :, e], columns(io["L0_ffn_ln_g"][e, :])),
                        (p.ln_b[:, :, e], columns(io["L0_ffn_ln_b"][e, :])),
                        (p.moe_b1[:, e, :], columns(io["L0_ffn_b1"][e, :])),
                        (p.moe_b2[:, e, :], io["L0_ffn_b2"][e, :].partition_broadcast(P))]
        for name, row in row_params.items():
            p.small.append((row[:], io[name].partition_broadcast(P)))

        def stage(name, make, *args):
            p.stage = name + "_"
            with nc.cleanup_on_exit():
                make(p, *args)

        stage("sort", sort_edges_and_normalize, io, dram)
        stage("unpack0", unpack_table, dram["table0"], 1)
        stage("sum0", sum_over_edges, dram["xn"], 0, False)
        stage("gnn0", gnn_dense, 0, True, row_params["L0_gnn_b0"], row_params["L0_gnn_g0"],
              row_params["L0_gnn_beta0"], ACT.Silu, None, dram["h1"], (0, 2))
        stage("sum1", sum_over_edges, dram["h1"], 0, False)
        stage("gnn1", gnn_dense, 1, True, row_params["L0_gnn_b1"], row_params["L0_gnn_g1"],
              row_params["L0_gnn_beta1"], ACT.Silu, io["x"], None, (2, 4))
        stage("route", route_to_experts)
        stage("moe_in", dispatch, dram["moe_in"], MOE_TILES * FT, TOP, True)
        stage("moe", ffn, dram["moe_in"], dram["moe_out"], MOE_TILES,
              (io["L0_ffn_W1"], io["L0_ffn_W2"], p.moe_b1, p.moe_b2), True, ACT.Gelu, (4, EC // SSTEP))
        stage("moe_out", combine, dram["moe_out"], TOP, False, p.share, p.norm_out, dram["x2"], dram["xn"], P)
        stage("unpack1", unpack_table, dram["table1"], 2)
        stage("sum2", sum_over_edges, dram["xn"], 1, True,
              ([p.wT[:, 2, kb, :] for kb in range(KB)], [row_params["L1_gnn_b_self"], row_params["L1_gnn_b_msg"]]))
        stage("gnn2", gnn_dense, 3, False, None,
              row_params["L1_gnn_ln_gamma"], row_params["L1_gnn_ln_beta"], ACT.Gelu, dram["x2"], None, None)
        stage("half", choose_larger_half)
        stage("half_in", dispatch, dram["mod_in"], MOD_TILES * FT, 1, False)
        stage("ffn", ffn, dram["mod_in"], dram["mod_out"], MOD_TILES,
              (io["L1_ffn_w1"], io["L1_ffn_w2"], p.mod_b1, row_params["L1_ffn_b2"]), False, ACT.Gelu_apprx_tanh, None)
        stage("half_out", combine, dram["mod_out"], 1, True, p.share, None, out, None, LAST)


def kernel(**inputs):
    import concourse.bacc as bacc
    from concourse.bass_utils import run_bass_kernel_spmd

    nc = bacc.Bacc("TRN2", target_bir_lowering=False, num_devices=1)
    arrays, io = {}, {}
    for name in INS:
        a = np.ascontiguousarray(inputs[name])
        arrays[f"in_{name}"] = a
        io[name] = nc.dram_tensor(f"in_{name}", a.shape, mybir.dt.from_np(a.dtype), kind="ExternalInput").ap()
    out = nc.dram_tensor("out", (N, D), F32, kind="ExternalOutput").ap()
    build(nc, io, out)
    r = run_bass_kernel_spmd(nc, [arrays], core_ids=[0])
    return r.results[0]["out"]
```
